# Optimizing a Trainium2 kernel written in Bass

```python
import numpy as np
import jax
import jax.numpy as jnp

def _softmax(x, axis=-1):
    return jax.nn.softmax(x, axis=axis)

def _gelu(x):
    return jax.nn.gelu(x, approximate=True)

def _silu(x):
    return jax.nn.silu(x)

def _sigmoid(x):
    return jax.nn.sigmoid(x)

def _layernorm(x, axis=-1, eps=1e-05):
    m = jnp.mean(x, axis=axis, keepdims=True)
    v = jnp.var(x, axis=axis, keepdims=True)
    return (x - m) / jnp.sqrt(v + eps)

def _scatter_add(tgt, idx, src, axis=0):
    return tgt.at[idx].add(src)

def _segment_sum(src, seg, n):
    return jax.ops.segment_sum(src, seg, n)
kernel_name = 'mk_gnn_resnorm_d4_gnn_r32_a49d97'

def setup_inputs(seed: int=0):
    np.random.seed(seed)
    _w = jnp.asarray

    def _rec_inputs():
        import jax
        import jax.numpy as jnp
        _gk = jax.random.key(seed)
        x = -0.000202 + 1 * jax.random.normal(jax.random.fold_in(_gk, 1), (50000, 128), jnp.float32)
        src = jax.random.randint(jax.random.fold_in(_gk, 2), (50000,), 0, 50000, jnp.int32)
        dst = jnp.minimum((50000 * jax.random.uniform(jax.random.fold_in(_gk, 3), (50000,)) ** 2.0).astype(jnp.int32), 49999)
        _o = jnp.argsort(dst, stable=True)
        src = src[_o]
        dst = dst[_o]
        edge_attr_64 = 0.000102155 + 1.00015 * jax.random.normal(jax.random.fold_in(_gk, 12), (50000, 64), jnp.float32)
        edge_attr_7 = -0.000187819 + 0.999723 * jax.random.normal(jax.random.fold_in(_gk, 13), (50000, 7), jnp.float32)
        edge_type_8 = jax.random.randint(jax.random.fold_in(_gk, 15), (50000,), 0, 8, jnp.int32)
        edge_weight = jax.random.uniform(jax.random.fold_in(_gk, 16), (50000,), jnp.float32, 0.0, 0.999999)
        edge_weight1 = jax.random.uniform(jax.random.fold_in(_gk, 17), (50000, 1), jnp.float32, 0.0, 0.999999)
        node_vec1 = jax.random.uniform(jax.random.fold_in(_gk, 18), (50000, 1), jnp.float32, 0.0, 15.9994)
        node_vec1_n2 = jax.random.uniform(jax.random.fold_in(_gk, 19), (50000, 1), jnp.float32, 0.0, 15.9994)
        return (x, src, dst, edge_attr_64, edge_attr_7, edge_type_8, edge_weight, edge_weight1, node_vec1, node_vec1_n2)
    x, src, dst, edge_attr_64, edge_attr_7, edge_type_8, edge_weight, edge_weight1, node_vec1, node_vec1_n2 = _rec_inputs()

    def _L0_gnn_setup():
        import jax, jax.numpy as jnp
        import numpy as np
        N = 50000
        E = 25000
        D = 128
        EDGE_RAW = 7
        key = jax.random.key(seed)
        ks = jax.random.split(key, 10)
        nfeat = jax.random.normal(ks[0], (N, D), dtype=jnp.float32)
        efeat = jax.random.normal(ks[1], (E, EDGE_RAW), dtype=jnp.float32)
        degs = jax.random.uniform(ks[2], (N, 1), dtype=jnp.float32) * 15.0 + 1.0
        norm = jax.random.uniform(ks[3], (E, 1), dtype=jnp.float32)
        src = jax.random.randint(ks[4], (E,), 0, N, dtype=jnp.int32)
        dst = jax.random.randint(ks[5], (E,), 0, N, dtype=jnp.int32)
        lim = 1.0 / np.sqrt(D)
        W = jax.random.uniform(ks[6], (D, D), dtype=jnp.float32, minval=-lim, maxval=lim)
        b = jnp.zeros((D,), dtype=jnp.float32)
        lim_e = 1.0 / np.sqrt(EDGE_RAW)
        We = jax.random.uniform(ks[7], (EDGE_RAW, D), dtype=jnp.float32, minval=-lim_e, maxval=lim_e)
        be = jnp.zeros((D,), dtype=jnp.float32)
        root_emb = jax.random.normal(ks[8], (1, D), dtype=jnp.float32)
        return {'nfeat': nfeat, 'efeat': efeat, 'degs': degs, 'norm': norm, 'src': src, 'dst': dst, 'W': W, 'b': b, 'We': We, 'be': be, 'root_emb': root_emb}
    _L0_gnn_all = _L0_gnn_setup()
    _L0_gnn_in = {k: v for k, v in _L0_gnn_all.items() if k in ('W', 'b', 'We', 'be', 'root_emb')}
    del _L0_gnn_all

    def _L1_gnn_setup():
        import jax, jax.numpy as jnp
        import numpy as np
        N_NODES = 50000
        N_EDGES = 18750
        IN_C = 128
        OUT_C = 128
        N_REL = 8
        key = jax.random.key(seed)
        k1, k2, k3, k4 = jax.random.split(key, 4)
        x = jax.random.normal(k1, (N_NODES, IN_C), dtype=jnp.float32)
        edge_index = jax.random.randint(k2, (2, N_EDGES), 0, N_NODES, dtype=jnp.int64)
        edge_type = jax.random.randint(k3, (N_EDGES,), 0, N_REL, dtype=jnp.int64)
        weight = jax.random.normal(k4, (N_REL, IN_C, OUT_C), dtype=jnp.float32)
        bias = jnp.zeros((OUT_C,), dtype=jnp.float32)
        return {'x': x, 'edge_index': edge_index, 'edge_type': edge_type, 'weight': weight, 'bias': bias}
    _L1_gnn_all = _L1_gnn_setup()
    _L1_gnn_in = {k: v for k, v in _L1_gnn_all.items() if k in ('weight', 'bias')}
    del _L1_gnn_all

    def _L2_gnn_setup():
        import jax, jax.numpy as jnp
        import numpy as np
        N_NODES = 3125
        FEAT = 128
        N_EDGES = 50000
        key = jax.random.key(seed)
        k1, k2, k3, k4, k5 = jax.random.split(key, 5)
        weight = jax.random.normal(k1, (N_NODES, FEAT), dtype=jnp.float32)
        cj = jax.random.uniform(k2, (N_NODES, 1), dtype=jnp.float32)
        ci = jax.random.uniform(k3, (N_NODES, 1), dtype=jnp.float32)
        src = jax.random.randint(k4, (N_EDGES,), 0, N_NODES, dtype=jnp.int32)
        dst = jax.random.randint(k5, (N_EDGES,), 0, N_NODES, dtype=jnp.int32)
        return {'weight': weight, 'cj': cj, 'ci': ci, 'src': src, 'dst': dst}
    _L2_gnn_all = _L2_gnn_setup()
    _L2_gnn_in = {k: v for k, v in _L2_gnn_all.items() if k in ()}
    del _L2_gnn_all

    def _L3_gnn_setup():
        import jax, jax.numpy as jnp
        import numpy as np
        N_NODES = 3125
        N_EDGES = 15625
        IN_CH = 128
        EDGE_CH = 64

        def _glorot(key, shape):
            fan_in, fan_out = (shape[0], shape[1])
            lim = (6.0 / (fan_in + fan_out)) ** 0.5
            return jax.random.uniform(key, shape, jnp.float32, -lim, lim)
        key = jax.random.key(seed)
        ks = jax.random.split(key, 14)
        x = jax.random.normal(ks[0], (N_NODES, IN_CH), jnp.float32)
        edge_index = jax.random.randint(ks[1], (2, N_EDGES), 0, N_NODES, jnp.int64)
        edge_attr = jax.random.normal(ks[2], (N_EDGES, EDGE_CH), jnp.float32)
        timestamps = jax.random.uniform(ks[3], (N_EDGES,), jnp.float32)
        We1 = _glorot(ks[4], (EDGE_CH, 2 * EDGE_CH))
        be1 = jnp.zeros((2 * EDGE_CH,), jnp.float32)
        We2 = _glorot(ks[5], (2 * EDGE_CH, IN_CH))
        be2 = jnp.zeros((IN_CH,), jnp.float32)
        Wt = _glorot(ks[6], (1, IN_CH))
        bt = jnp.zeros((IN_CH,), jnp.float32)
        Wn1 = _glorot(ks[7], (2 * IN_CH, IN_CH))
        bn1 = jnp.zeros((IN_CH,), jnp.float32)
        Wn2 = _glorot(ks[8], (IN_CH, IN_CH))
        bn2 = jnp.zeros((IN_CH,), jnp.float32)
        return {'x': x, 'edge_index': edge_index, 'edge_attr': edge_attr, 'timestamps': timestamps, 'We1': We1, 'be1': be1, 'We2': We2, 'be2': be2, 'Wt': Wt, 'bt': bt, 'Wn1': Wn1, 'bn1': bn1, 'Wn2': Wn2, 'bn2': bn2}
    _L3_gnn_all = _L3_gnn_setup()
    _L3_gnn_in = {k: v for k, v in _L3_gnn_all.items() if k in ('We1', 'be1', 'We2', 'be2', 'Wt', 'bt', 'Wn1', 'bn1', 'Wn2', 'bn2')}
    del _L3_gnn_all
    return {'x': x, 'src': src, 'dst': dst, 'edge_attr_64': edge_attr_64, 'edge_attr_7': edge_attr_7, 'edge_type_8': edge_type_8, 'edge_weight': edge_weight, 'edge_weight1': edge_weight1, 'node_vec1': node_vec1, 'node_vec1_n2': node_vec1_n2, 'L0_gnn_W': _L0_gnn_in['W'], 'L0_gnn_b': _L0_gnn_in['b'], 'L0_gnn_We': _L0_gnn_in['We'], 'L0_gnn_be': _L0_gnn_in['be'], 'L0_gnn_root_emb': _L0_gnn_in['root_emb'], 'L1_gnn_weight': _L1_gnn_in['weight'], 'L1_gnn_bias': _L1_gnn_in['bias'], 'L3_gnn_We1': _L3_gnn_in['We1'], 'L3_gnn_be1': _L3_gnn_in['be1'], 'L3_gnn_We2': _L3_gnn_in['We2'], 'L3_gnn_be2': _L3_gnn_in['be2'], 'L3_gnn_Wt': _L3_gnn_in['Wt'], 'L3_gnn_bt': _L3_gnn_in['bt'], 'L3_gnn_Wn1': _L3_gnn_in['Wn1'], 'L3_gnn_bn1': _L3_gnn_in['bn1'], 'L3_gnn_Wn2': _L3_gnn_in['Wn2'], 'L3_gnn_bn2': _L3_gnn_in['bn2']}

def reference(x, src, dst, edge_attr_64, edge_attr_7, edge_type_8, edge_weight, edge_weight1, node_vec1, node_vec1_n2, L0_gnn_W, L0_gnn_b, L0_gnn_We, L0_gnn_be, L0_gnn_root_emb, L1_gnn_weight, L1_gnn_bias, L3_gnn_We1, L3_gnn_be1, L3_gnn_We2, L3_gnn_be2, L3_gnn_Wt, L3_gnn_bt, L3_gnn_Wn1, L3_gnn_bn1, L3_gnn_Wn2, L3_gnn_bn2):
    import jax
    import jax.numpy as jnp

    def _L0_gnn_ref(nfeat, efeat, degs, norm, src, dst, W, b, We, be, root_emb):
        import jax, jax.numpy as jnp
        import numpy as np
        N = 50000
        E = 25000
        D = 128
        EDGE_RAW = 7
        h = nfeat @ W + b
        edge_emb = efeat @ We + be
        msg = norm * jax.nn.relu(h[src] + edge_emb)
        agg = jax.ops.segment_sum(msg, dst, num_segments=h.shape[0])
        rst = agg + jax.nn.relu(h + root_emb) / degs
        return rst

    def _L1_gnn_ref(x, edge_index, edge_type, weight, bias):
        import jax, jax.numpy as jnp
        import numpy as np
        N_NODES = 50000
        N_EDGES = 18750
        IN_C = 128
        OUT_C = 128
        N_REL = 8
        N = x.shape[0]
        src = edge_index[0]
        dst = edge_index[1]
        out = jnp.zeros((N, weight.shape[2]), dtype=x.dtype)
        for r in range(weight.shape[0]):
            rel_mask = (edge_type == r).astype(x.dtype)
            transformed = x @ weight[r]
            msgs = transformed[src] * rel_mask[:, None]
            sums = jax.ops.segment_sum(msgs, dst, num_segments=N)
            counts = jax.ops.segment_sum(rel_mask, dst, num_segments=N)
            mean = jnp.where(counts[:, None] > 0, sums / jnp.maximum(counts, 1.0)[:, None], 0.0)
            out = out + mean
        return out + bias

    def _L2_gnn_ref(weight, cj, ci, src, dst):
        import jax, jax.numpy as jnp
        import numpy as np
        N_NODES = 3125
        FEAT = 128
        N_EDGES = 50000
        feat = weight * cj
        msgs = feat[src]
        h = jax.ops.segment_sum(msgs, dst, num_segments=weight.shape[0])
        return h * ci

    def _L3_gnn_ref(x, edge_index, edge_attr, timestamps, We1, be1, We2, be2, Wt, bt, Wn1, bn1, Wn2, bn2):
        import jax, jax.numpy as jnp
        import numpy as np
        N_NODES = 3125
        N_EDGES = 15625
        IN_CH = 128
        EDGE_CH = 64

        def _glorot(key, shape):
            fan_in, fan_out = (shape[0], shape[1])
            lim = (6.0 / (fan_in + fan_out)) ** 0.5
            return jax.random.uniform(key, shape, jnp.float32, -lim, lim)
        ts = timestamps[:, None]
        ef = jax.nn.relu(edge_attr @ We1 + be1) @ We2 + be2
        tw = jax.nn.sigmoid(ts @ Wt + bt)
        ef = ef * tw
        row, col = (edge_index[0], edge_index[1])
        combined = jnp.concatenate([x[row], ef], axis=1)
        msg = jax.nn.relu(combined @ Wn1 + bn1) @ Wn2 + bn2
        out = jax.ops.segment_sum(msg, col, num_segments=x.shape[0])
        return out + x
    edge_index = jnp.stack([src, dst])
    x = _layernorm(x + _L0_gnn_ref(x, edge_attr_7, node_vec1, edge_weight1, src, dst, L0_gnn_W, L0_gnn_b, L0_gnn_We, L0_gnn_be, L0_gnn_root_emb), axis=-1)
    x = _layernorm(x + _L1_gnn_ref(x, edge_index, edge_type_8, L1_gnn_weight, L1_gnn_bias), axis=-1)
    x = _layernorm(x + _L2_gnn_ref(x, node_vec1, node_vec1_n2, src, dst), axis=-1)
    x = _layernorm(x + _L3_gnn_ref(x, edge_index, edge_attr_64, edge_weight, L3_gnn_We1, L3_gnn_be1, L3_gnn_We2, L3_gnn_be2, L3_gnn_Wt, L3_gnn_bt, L3_gnn_Wn1, L3_gnn_bn1, L3_gnn_Wn2, L3_gnn_bn2), axis=-1)
    return x

_drawn_inputs = setup_inputs


def setup_inputs(seed=0):
    import zlib

    import numpy as np

    out = dict(_drawn_inputs(seed))
    spreads = {'L0_gnn_b': (0.0, 0.1),
     'L0_gnn_be': (0.0, 0.348),
     'L1_gnn_bias': (0.0, 0.1),
     'L3_gnn_be1': (0.0, 0.789),
     'L3_gnn_be2': (0.0, 0.54),
     'L3_gnn_bt': (0.0, 0.8),
     'L3_gnn_bn1': (0.0, 0.1),
     'L3_gnn_bn2': (0.0, 0.1)}
    factors = {'edge_weight': 8.0, 'L3_gnn_Wt': 8.0}
    for name, (base, spread) in spreads.items():
        noise = np.random.default_rng([zlib.crc32(name.encode()), seed]).standard_normal(out[name].shape)
        drawn = base * np.exp(spread * noise) if base else spread * noise
        out[name] = jnp.asarray(drawn.astype(out[name].dtype))
    for name, factor in factors.items():
        out[name] = (out[name] * factor).astype(out[name].dtype)
    return out
```

```python
from contextlib import ExitStack

import concourse.bass as bass
from concourse import mybir

FP32 = mybir.dt.float32
BF16 = mybir.dt.bfloat16
I32 = mybir.dt.int32
ALU = mybir.AluOpType
ACT = mybir.ActivationFunctionType
AXX = mybir.AxisListType.X

P = 128
N = 50000
D = 128
UN = 8
T = -(-N // (P * UN)) * UN
TURNS = T // UN
R = T * P
HALF = UN // 2
REL = 8
RAW = 7
K9 = RAW + 2
ER = 64
AUG = 132
DUMP = R + 3 * P
EPS = 1e-5
BLK = T // 4
HI = -(-T // 16)
LO = 16


def wait(e, sem, n):
    if not isinstance(n, int) or n > 0:
        e.wait_ge(sem, n)


def walk(e, step, drain=0):
    for i in (0, 1):
        for k in range(UN):
            step(Tile(i, k))
    with e.Fori(2, TURNS - 1) as i:
        for k in range(UN):
            step(Tile(i, k))
    for k in range(UN):
        step(Tile(TURNS - 1, k))
    for k in range(drain):
        step(Tile(TURNS, k))


class Tile:

    def __init__(self, i, k):
        self.i, self.k = i, k
        self.n = i * UN + k
        self.slot = k % UN
        self.round = i + k // UN
        self.real = not isinstance(i, int) or 0 <= self.n < T

    def back(self, d):
        return Tile(self.i, self.k - d)

    def col(self, width=1):
        return bass.ds(self.n, width)


def cleared(nc, handles):
    nc.clear_and_free_semaphores(handles)
    nc.all_engine_barrier()


def sems(nc, ctx, stage, *names):
    handles = [nc.alloc_semaphore(f"{stage}_{n}") for n in names]
    ctx.callback(cleared, nc, handles)
    return handles


class Ring:

    def __init__(self, nc, name, n=UN):
        self.sems = [nc.alloc_semaphore(f"{name}{k}") for k in range(n)]
        self.base = 0

    def __getitem__(self, k):
        return self.sems[k]

    def next_layer(self):
        self.base += 16 * TURNS



LISTS = ("dst", "src", "etype", "norm", "weight")
CHUNK = R // 8
FIELDS = 3 + 2 + RAW + ER


def order_stage(nc, c, A, S):
    with ExitStack() as ctx:
        def sb(name, shape, dt=FP32):
            return ctx.enter_context(nc.sbuf_tensor(name, shape, dt))

        pair = sb("pair", [P, 2, T], I32)
        pairf = sb("pairf", [P, 2, T])
        falls = sb("falls", [P, T])
        worst = sb("worst", [P, 1])
        flag = sb("flag", [1, 1], I32)
        p_flag = ctx.enter_context(nc.psum_tensor("p_flag", [P, 512], FP32))
        loaded, v, voted, ready = sems(nc, ctx, "order", "loaded", "dve", "voted", "ready")
        with nc.Block() as block:
            @block.sync
            def _(sp):
                for j in (0, 1):
                    sp.dma_start(pair[:, j, :], A["dst"][j:j + R].rearrange("(p t) -> p t", p=P)).then_inc(loaded, 16)

            @block.vector
            def _(dve):
                dve.wait_ge(loaded, 32)
                dve.tensor_copy(pairf[:, :, :], pair[:, :, :]).then_inc(v, 1)
                dve.wait_ge(v, 1)
                dve.tensor_tensor(falls[:, :], pairf[:, 0, :], pairf[:, 1, :], ALU.is_gt).then_inc(v, 1)
                dve.wait_ge(v, 2)
                dve.reduce_max(worst[:, :], falls[:, :], AXX).then_inc(v, 1)
                dve.wait_ge(voted, 1)
                dve.tensor_copy(flag[:, :], p_flag[0:1, 0:1]).then_inc(ready, 1)

            @block.tensor
            def _(pe):
                pe.wait_ge(v, 3)
                pe.matmul(p_flag[0:1, 0:1], worst[:, :], c.ones[:, 0:1], start=True, stop=True).then_inc(voted, 1)

        keys_i = sb("keys_i", [P, CHUNK], I32)
        keys = sb("keys", [P, CHUNK])
        number = sb("number", [P, CHUNK])
        less = sb("less", [P, CHUNK])
        key_i = sb("key_i", [P, T], I32)
        key = sb("key", [P, T])
        own = sb("own", [P, T])
        part = sb("part", [P, 1])
        place = sb("place", [P, T])
        place_i = sb("place_i", [P, T], I32)
        record = sb("record", [P, 1, FIELDS], I32)
        target = sb("target", [P, 1], I32)
        (chunk_in, chunk_used, col_in, made, w, rank_done, record_in, pointed, sent, listed, small_in, sent_for) = sems(
            nc, ctx, "sort", "chunk_in", "chunk_used", "col_in", "made", "dve", "rank_done", "record_in", "pointed",
            "sent", "listed", "small_in", "sent_for")
        recs = nc.dram_tensor("recs", [R, FIELDS], I32).ap()
        parts = [("ints", 0, 3), ("floats", 3, 2 + RAW), ("raw64_rows", 5 + RAW, ER)]
        with nc.Block() as block:
            @block.sync
            def _(sp):
                unsorted = sp.value_load(flag[0:1, 0:1], min_val=0, max_val=P)
                with sp.If(unsorted > 0):
                    with nc.allow_non_contiguous_dma(reason="the general path for edges in any order"):
                        sp.dma_start(key_i[:, :], A["dst"][1:R + 1].rearrange("(t p) -> p t", p=P))\
                            .then_inc(col_in, 16)
                    for n in range(R // CHUNK):
                        if n:
                            sp.wait_ge(chunk_used, n)
                        sp.dma_start(keys_i[:, :], A["dst"][1 + n * CHUNK:1 + (n + 1) * CHUNK].partition_broadcast(P))\
                            .then_inc(chunk_in, 16)
                    sp.wait_ge(rank_done, 1)
                    with sp.Fori(0, T) as t:
                        sp.wait_ge(made, t + 1)
                        for name, at, n in parts:
                            sp.dma_start(record[:, 0, at:at + n], A[name][bass.ds(t * P, P), :].bitcast(I32))\
                                .then_inc(record_in, 16)
                    sp.wait_ge(made, T + 1)
                    columns = [(S["dst"][1:R + 1], 0), (S["src"], 1), (S["etype"], 2),
                               (S["norm"].bitcast(I32), 3), (S["weight"].bitcast(I32), 4)]
                    columns += [(S["raw7"][j, :].bitcast(I32), 5 + j) for j in range(RAW)]
                    columns += [(S["raw64"][j, :].bitcast(I32), 5 + RAW + j) for j in range(ER)]
                    with nc.allow_non_contiguous_dma(reason="the general path for edges in any order"):
                        for dst, j in columns:
                            sp.dma_start(dst.rearrange("(a b) -> a b", a=P),
                                         recs[:, j].rearrange("(a b) -> a b", a=P)).then_inc(listed, 16)
                    sp.dma_start(S["raw7"][RAW:K9, :], A["raw7"][RAW:K9, :]).then_inc(listed, 16)
                    for at in (0, R + 1):
                        sp.dma_start(S["dst"][at:at + 1], A["dst"][at:at + 1]).then_inc(listed, 16)
                    sp.wait_ge(listed, 16 * (FIELDS + 3))
                    sp.sem_inc(c.raw64_ready, 16)
                with sp.Else():
                    for name in LISTS:
                        sp.dma_start(S[name], A[name]).then_inc(small_in, 16)
                    sp.dma_start(S["raw7"], A["raw7"]).then_inc(small_in, 16)
                    sp.dma_start(S["raw64"], A["raw64"]).then_inc(c.raw64_ready, 16)
                    sp.wait_ge(small_in, 16 * (len(LISTS) + 1))

            @block.vector
            def _(dve):
                unsorted = dve.value_load(flag[0:1, 0:1], min_val=0, max_val=P)
                with dve.If(unsorted > 0):
                    count = [0]

                    def link(ins):
                        count[0] += 1
                        ins.then_inc(w, 1)
                        dve.wait_ge(w, count[0])

                    dve.wait_ge(col_in, 16)
                    dve.wait_ge(pointed, 1)
                    dve.tensor_copy(key[:, :], key_i[:, :])
                    link(dve.memset(place[:, :], 0.0))
                    for n in range(R // CHUNK):
                        dve.wait_ge(chunk_in, 16 * n + 16)
                        link(dve.tensor_copy(keys[:, :], keys_i[:, :]))
                        if n:
                            link(dve.tensor_scalar(own[:, :], own[:, :], -float(CHUNK), None, ALU.add))
                        base = count[0]
                        with dve.Fori(0, T) as t:
                            at = bass.ds(t, 1)
                            dve.tensor_scalar(less[:, :], number[:, :], own[:, at], None, ALU.is_lt).then_inc(w, 1)
                            dve.wait_ge(w, t * 5 + base + 1)
                            dve.scalar_tensor_tensor(less[:, :], keys[:, :], key[:, at], less[:, :],
                                                     ALU.is_equal, ALU.mult).then_inc(w, 1)
                            dve.wait_ge(w, t * 5 + base + 2)
                            dve.scalar_tensor_tensor(less[:, :], keys[:, :], key[:, at], less[:, :],
                                                     ALU.is_lt, ALU.add).then_inc(w, 1)
                            dve.wait_ge(w, t * 5 + base + 3)
                            dve.reduce_sum(part[:, :], less[:, :], AXX).then_inc(w, 1)
                            dve.wait_ge(w, t * 5 + base + 4)
                            dve.tensor_tensor(place[:, at], place[:, at], part[:, :], ALU.add).then_inc(w, 1)
                            dve.wait_ge(w, t * 5 + base + 5)
                        count[0] += 5 * T
                        dve.nop().then_inc(chunk_used, 1)
                    link(dve.tensor_copy(place_i[:, :], place[:, :]))
                    dve.nop().then_inc(rank_done, 1)
                with dve.Else():
                    dve.nop()

            @block.gpsimd
            def _(pool):
                unsorted = pool.value_load(flag[0:1, 0:1], min_val=0, max_val=P)
                with pool.If(unsorted > 0):
                    pool.iota(number[:, :], [[1, CHUNK]], base=0, channel_multiplier=0,
                              allow_small_or_imprecise_dtypes=True)
                    pool.iota(own[:, :], [[P, T]], base=0, channel_multiplier=1,
                              allow_small_or_imprecise_dtypes=True).then_inc(pointed, 1)
                    pool.wait_ge(rank_done, 1)
                    pool.nop().then_inc(made, 1)
                    with pool.Fori(0, T) as t:
                        pool.tensor_copy(target[:, :], place_i[:, bass.ds(t, 1)]).then_inc(pointed, 1)
                        pool.wait_ge(pointed, t + 2)
                        pool.wait_ge(record_in, t * (16 * len(parts)) + 16 * len(parts))
                        pool.sem_inc(sent_for, 1)
                        pool.indirect_dma_start(recs, bass.IndirectOffsetOnAxis(ap=target[:, 0:1], axis=0),
                                                record[:, 0, :], None).then_inc(sent, 16)
                        pool.wait_ge(sent, t * 16 + 16)
                        pool.sem_inc(made, 1)
                with pool.Else():
                    pool.nop()



def constants_stage(nc, c, A):
    with ExitStack() as ctx:
        loaded, zeroed, made = sems(nc, ctx, "const", "loaded", "zeroed", "made")
        loads = [
            (c.w0[:, :], A["L0_gnn_W"][:, :]),
            (c.we9[0:RAW, :], A["L0_gnn_We"][:, :]),
            (c.we9[RAW:RAW + 1, :], A["L0_gnn_b"]),
            (c.we9[RAW + 1:K9, :], A["L0_gnn_be"]),
            (c.root2[0:1, :], A["L0_gnn_b"]),
            (c.root2[1:2, :], A["L0_gnn_root_emb"][:, :]),
            (c.w1[:, :, :], A["L1_gnn_weight"].rearrange("r f g -> f r g")),
            (c.bias1[:, :], A["L1_gnn_bias"]),
            (c.we1[:, :], A["L3_gnn_We1"][:, :]),
            (c.we2[:, :], A["L3_gnn_We2"][:, :]),
            (c.wn1a[:, :], A["L3_gnn_Wn1"][0:D, :]),
            (c.wn1b[:, :], A["L3_gnn_Wn1"][D:2 * D, :]),
            (c.wn2[:, :], A["L3_gnn_Wn2"][:, :]),
            (c.bn1[:, :], A["L3_gnn_bn1"]),
            (c.bn2[:, :], A["L3_gnn_bn2"]),
            (c.cols[:, 0:1], A["L3_gnn_be1"]),
            (c.cols[:, 1:2], A["L3_gnn_be2"]),
            (c.cols[:, 2:3], A["L3_gnn_Wt"]),
            (c.cols[:, 3:4], A["L3_gnn_bt"]),
            (c.inv_deg[:, :], A["degree_cols"][:, :]),
            (c.scale2[:, :], A["scale2_cols"][:, :]),
        ]
        with nc.Block() as block:
            @block.sync
            def _(sp):
                for dst, src in loads:
                    sp.dma_start(dst, src).then_inc(loaded, 16)
                sp.wait_ge(loaded, 16 * len(loads))

            @block.gpsimd
            def _(pool):
                pool.memset(c.ident[:, :], 0.0).then_inc(zeroed, 1)
                pool.memset(c.upper[:, :], 1.0).then_inc(zeroed, 1)
                pool.iota(c.ramp[:, :], [[1, 2 * P]], base=0, channel_multiplier=0,
                          allow_small_or_imprecise_dtypes=True).then_inc(made, 1)
                pool.iota(c.tile_base[:, :], [[P, T]], base=0, channel_multiplier=0,
                          allow_small_or_imprecise_dtypes=True).then_inc(made, 1)
                pool.wait_ge(zeroed, 2)
                pool.affine_select(out=c.ident[:, :], in_=c.ident[:, :], compare_op=ALU.not_equal, fill=1.0,
                                   base=0, pattern=[[-1, P]], channel_multiplier=1).then_inc(made, 1)
                pool.affine_select(out=c.upper[:, :], in_=c.upper[:, :], compare_op=ALU.is_gt, fill=0.0,
                                   base=0, pattern=[[1, P]], channel_multiplier=-1).then_inc(made, 1)
                pool.wait_ge(made, 4)

            @block.vector
            def _(dve):
                dve.memset(c.ones[:, :], 1.0)
                dve.memset(c.zeros[:, :], 0.0)
                dve.memset(c.eps[:, :], EPS)
                dve.wait_ge(loaded, 16 * len(loads))
                dve.reciprocal(c.inv_deg[:, :], c.inv_deg[:, :])


def index_stage(nc, c, A):
    with ExitStack() as ctx:
        def sb(name, shape, dt=FP32):
            return ctx.enter_context(nc.sbuf_tensor(name, shape, dt))

        def ps(name, shape):
            return ctx.enter_context(nc.psum_tensor(name, shape, FP32))

        dsti = sb("dsti", [P, 3, T], I32)
        typi = sb("typi", [P, T], I32)
        dstf = sb("dstf", [P, 3, T])
        typf = sb("typf", [P, T])
        same = sb("same", [P, 2, T])
        first = sb("first", [P, T])
        onesT = sb("onesT", [P, T])
        rank = sb("rank", [P, T])
        fdst = sb("fdst", [P, T])
        masks = sb("masks", [P, REL, T])
        run = sb("run", [P, REL, T])
        tmp = sb("tmp", [P, REL, T])
        through = sb("through", [P, T])
        total = sb("total", [P, 2, T])
        ends = sb("ends", [P, 2, REL])
        endsT = sb("endsT", [REL, 2, P])
        carry = sb("carry", [REL, P + 1])
        carryC = sb("carryC", [P, REL])
        before = sb("before", [P, 1])
        digits_i = sb("digits_i", [P, 3, T], I32)
        digits = sb("digits", [P, 2, T])
        one_hi = sb("one_hi", [P, 2, UN, HI], BF16)
        one_lo = sb("one_lo", [P, 2, UN, LO], BF16)
        hist = sb("hist", [HI, LO])
        hrow = sb("hrow", [1, HI * LO])
        urow = sb("urow", [1, HI * LO + 1])
        lists_i = sb("lists_i", [BLK, 2, 4, P], I32)
        lists = sb("lists", [BLK, 6, 4, P])
        row = sb("row", [1, 6, T])
        row_i = sb("row_i", [1, T + 1], I32)
        p_small = ps("p_small", [P, 512])
        p_ends = ps("p_ends", [P, 512])
        p_carry = ps("p_carry", [P, 512])
        p_hist = ps("p_hist", [P, 512])
        p_cols = [ps(f"p_cols{j}", [P, T]) for j in range(2)]
        p_row = [ps(f"p_row{j}", [P, T]) for j in range(2)]
        (ld_edges, ld_lists, v, pe_s, st_lin, ld_lin, ld_hist, st_hist, digit_ready, digit_used, counted,
         turned, taken, zero_sem, act_s) = sems(
            nc, ctx, "index", "edges", "lists", "dve", "pe", "stored", "relisted", "hist_in", "hist_out",
            "digit_ready", "digit_used", "counted", "turned", "taken", "zeroed", "act")
        lin = [nc.dram_tensor(f"lin{j}", [R], FP32).ap() for j in range(3)]
        hist_d = nc.dram_tensor("hist_d", [HI * LO], FP32).ap()

        def pmajor(a, off=0):
            return a[off:off + R].rearrange("(p t) -> p t", p=P)

        def blocks(a, off=0):
            return a[off:off + R].rearrange("(b t p) -> t b p", b=4, p=P)

        marks = {}
        with nc.Block() as block:
            @block.vector
            def _(dve):
                count = [0]

                def link(ins, name=None):
                    count[0] += 1
                    ins.then_inc(v, 1)
                    dve.wait_ge(v, count[0])
                    if name:
                        marks[name] = count[0]

                dve.memset(onesT[:, :], 1.0)
                dve.memset(urow[:, 0:1], 0.0)
                link(dve.memset(carry[:, :], 0.0))
                dve.wait_ge(ld_edges, 64)
                dve.tensor_copy(typf[:, :], typi[:, :])
                link(dve.tensor_copy(dstf[:, :, :], dsti[:, :, :]))
                for side in (0, 1):
                    last = dve.tensor_tensor(same[:, side, :], dstf[:, 1, :], dstf[:, 2 * side, :], ALU.is_equal)
                link(last)
                link(dve.tensor_scalar(first[:, :], same[:, 0, :], -1.0, 1.0, ALU.mult, ALU.add))
                dve.tensor_tensor(fdst[:, :], first[:, :], dstf[:, 1, :], ALU.mult)
                link(dve.tensor_tensor_scan(rank[:, :], onesT[:, :], first[:, :], 0.0, ALU.mult, ALU.add), "run")
                dve.wait_ge(pe_s, 1)
                link(dve.tensor_copy(before[:, :], p_small[:, 0:1]))
                link(dve.tensor_scalar(rank[:, :], rank[:, :], before[:, 0:1], -1.0, ALU.add, ALU.add), "rank")
                link(dve.tensor_scalar(digits_i[:, 0, :], dsti[:, 1, :], 7, None, ALU.arith_shift_right))
                dve.tensor_scalar(digits_i[:, 1, :], digits_i[:, 0, :], 4, None, ALU.arith_shift_right)
                link(dve.tensor_scalar(digits_i[:, 2, :], digits_i[:, 0, :], 15, None, ALU.bitwise_and))
                link(dve.tensor_copy(digits[:, :, :], digits_i[:, 1:3, :]))
                link(dve.scalar_tensor_tensor(digits[:, 0, :], digits[:, 0, :], 1.0, first[:, :], ALU.add, ALU.mult))
                link(dve.tensor_scalar(digits[:, 0, :], digits[:, 0, :], -1.0, None, ALU.add))

                def digit_turn(i, h):
                    if not isinstance(i, int):
                        dve.wait_ge(digit_used, i * 2 + h - 1)
                    for oh, d, n in ((one_hi, 0, HI), (one_lo, 1, LO)):
                        ins = dve.tensor_tensor(
                            oh[:, h, :, :],
                            c.ramp[:, None, 0:n].to_broadcast([P, UN, n]),
                            digits[:, d, bass.ds(i * 2 * UN + h * UN, UN)][:, :, None].to_broadcast([P, UN, n]),
                            ALU.is_equal)
                    ins.then_inc(digit_ready, 1)
                for h in (0, 1):
                    digit_turn(0, h)
                with dve.Fori(1, TURNS // 2) as i:
                    for h in (0, 1):
                        digit_turn(i, h)
                dve.wait_ge(digit_used, TURNS // 2 * 2 - 1)
                for oh, d, n in ((one_hi, 0, HI), (one_lo, 1, LO)):
                    ins = dve.tensor_tensor(
                        oh[:, 0, :, :], c.ramp[:, None, 0:n].to_broadcast([P, UN, n]),
                        digits[:, d, T - UN:T][:, :, None].to_broadcast([P, UN, n]), ALU.is_equal)
                ins.then_inc(digit_ready, 1)
                dve.wait_ge(counted, 1)
                link(dve.tensor_copy(hist[:, :], p_hist[0:HI, 0:LO]), "hist")
                for r in range(REL):
                    last = dve.tensor_scalar(masks[:, r, :], typf[:, :], float(r), None, ALU.is_equal)
                link(last)
                for side in (0, 1):
                    seg = same[:, side, :] if side == 0 else same[:, side, ::-1]
                    way = slice(None) if side == 0 else slice(None, None, -1)
                    end = slice(T - 1, T) if side == 0 else slice(0, 1)
                    for r in range(REL):
                        dve.tensor_tensor_scan(run[:, r, way], seg, masks[:, r, way], 0.0, ALU.mult, ALU.add)
                    link(dve.tensor_tensor_scan(through[:, way], seg, seg, 1.0, ALU.mult, ALU.mult))
                    dve.tensor_copy(ends[:, 0, :, None], run[:, :, end])
                    link(dve.tensor_copy(ends[:, 1, :, None], through[:, None, end].to_broadcast([P, REL, 1])),
                         f"ends{side}")
                    dve.wait_ge(pe_s, 2 + 2 * side)
                    link(dve.tensor_copy(endsT[:, :, :], p_ends[0:REL, 0:2 * P].rearrange("r (a p) -> r a p", a=2)))
                    if side == 0:
                        link(dve.tensor_tensor_scan(carry[:, 1:P + 1], endsT[:, 1, :], endsT[:, 0, :], 0.0,
                                                    ALU.mult, ALU.add), "carry0")
                    else:
                        link(dve.memset(carry[:, P:P + 1], 0.0))
                        link(dve.tensor_tensor_scan(carry[:, 0:P][:, ::-1], endsT[:, 1, ::-1], endsT[:, 0, ::-1],
                                                    0.0, ALU.mult, ALU.add), "carry1")
                    dve.wait_ge(pe_s, 3 + 2 * side)
                    link(dve.tensor_copy(carryC[:, :], p_carry[:, 0:REL]))
                    link(dve.tensor_tensor(tmp[:, :, :], through[:, None, :].to_broadcast([P, REL, T]),
                                           carryC[:, :, None].to_broadcast([P, REL, T]), ALU.mult))
                    link(dve.tensor_tensor(tmp[:, :, :], tmp[:, :, :], run[:, :, :], ALU.add))
                    link(dve.tensor_tensor(tmp[:, :, :], tmp[:, :, :], masks[:, :, :], ALU.mult))
                    link(dve.tensor_reduce(total[:, side, :], tmp[:, :, :].rearrange("p r t -> p t r"), AXX, ALU.add))
                link(dve.scalar_tensor_tensor(total[:, 0, :], total[:, 0, :], -1.0, total[:, 1, :], ALU.add, ALU.add))
                link(dve.reciprocal(total[:, 1, :], total[:, 0, :]), "inv")
                dve.wait_ge(ld_hist, 16)
                link(dve.tensor_tensor_scan(urow[:, 1:HI * LO + 1], onesT[0:1, 0:1].to_broadcast([1, HI * LO]),
                                            hrow[:, :], 0.0, ALU.mult, ALU.add))
                link(dve.tensor_copy(c.sum_start[:, :], urow[:, 0:T]))
                dve.wait_ge(ld_lists, 48)
                dve.tensor_copy(lists[:, 2, :, :], lists_i[:, 1, :, :])
                link(dve.tensor_copy(lists[:, 1, :, :], lists_i[:, 0, :, :]), "lists")
                dve.wait_ge(turned, 1)
                dve.tensor_copy(c.norm[:, :], p_cols[0][:, :]).then_inc(taken, 1)
                dve.wait_ge(turned, 2)
                dve.tensor_copy(c.src[:, :], p_cols[1][:, :]).then_inc(taken, 1)
                dve.wait_ge(turned, 3)
                for r in range(REL):
                    ins = dve.tensor_scalar(c.is_rel[:, :, r], p_cols[0][:, :], float(r), None, ALU.is_equal)
                ins.then_inc(taken, 1)
                dve.wait_ge(turned, 4)
                link(dve.tensor_copy(c.rank[:, :], p_cols[1][:, :]))
                dve.nop().then_inc(taken, 1)
                dve.wait_ge(turned, 5)
                dve.tensor_copy(c.inv[:, :], p_cols[0][:, :]).then_inc(taken, 1)
                dve.wait_ge(turned, 6)
                dve.tensor_copy(c.first_dst[:, :], p_cols[1][:, :]).then_inc(taken, 1)
                link(dve.tensor_copy(row_i[:, 0:T], c.rank[0:1, :]))
                link(dve.tensor_scalar(row_i[:, 0:T], row_i[:, 0:T], 7, 7, ALU.arith_shift_right,
                                       ALU.logical_shift_left))
                link(dve.tensor_copy(row[:, 0, :], row_i[:, 0:T]))
                dve.memset(row[:, 1, :], 1.0)
                link(dve.memset(row[:, 2, :], 0.0))
                link(dve.tensor_tensor(row[:, 1, 0:T - 1], row[:, 0, 1:T], row[:, 0, 0:T - 1], ALU.is_gt))
                link(dve.tensor_scalar(row[:, 2, :], row[:, 1, :], -1.0, 1.0, ALU.mult, ALU.add), "rows")
                link(dve.tensor_scalar(row[:, 3, :], c.tile_base[0:1, :], float(DUMP), None, ALU.add))
                link(dve.tensor_tensor(row[:, 4, :], row[:, 0, :], row[:, 3, :], ALU.subtract))
                link(dve.tensor_tensor(row[:, 4, :], row[:, 4, :], row[:, 1, :], ALU.mult))
                link(dve.tensor_tensor(row[:, 4, :], row[:, 4, :], row[:, 3, :], ALU.add))
                dve.tensor_copy(c.sum_row[:, 0:T], row[:, 4, :])
                dve.tensor_scalar(c.sum_row[:, T:T + 1], row[:, 0, T - 1:T], float(P), None, ALU.add)
                link(dve.tensor_scalar(c.sum_row[:, T + 1:T + 2], row[:, 0, T - 1:T], float(2 * P), None, ALU.add))
                dve.wait_ge(pe_s, 6)
                dve.tensor_tensor(c.rank[:, :], c.rank[:, :], p_row[0][:, :], ALU.subtract)
                link(dve.tensor_copy(c.goes_on[:, :], p_row[1][:, :]))

            @block.sync
            def _(sp):
                for j in range(3):
                    sp.dma_start(dsti[:, j, :], pmajor(A["dst"], j)).then_inc(ld_edges, 16)
                sp.dma_start(typi[:, :], pmajor(A["etype"])).then_inc(ld_edges, 16)
                sp.dma_start(lists[:, 0, :, :], blocks(A["norm"])).then_inc(ld_lists, 16)
                sp.dma_start(lists_i[:, 0, :, :], blocks(A["src"])).then_inc(ld_lists, 16)
                sp.dma_start(lists_i[:, 1, :, :], blocks(A["etype"])).then_inc(ld_lists, 16)
                sp.wait_ge(v, marks["rank"])
                sp.dma_start(pmajor(lin[0]), rank[:, :]).then_inc(st_lin, 16)
                sp.dma_start(pmajor(lin[2]), fdst[:, :]).then_inc(st_lin, 16)
                sp.wait_ge(v, marks["hist"])
                sp.dma_start(hist_d.rearrange("(h l) -> h l", l=LO), hist[:, :]).then_inc(st_hist, 16)
                sp.wait_ge(st_hist, 16)
                sp.dma_start(hrow[:, :], hist_d.rearrange("(a h) -> a h", a=1)).then_inc(ld_hist, 16)
                sp.wait_ge(v, marks["inv"])
                sp.dma_start(pmajor(lin[1]), total[:, 1, :]).then_inc(st_lin, 16)
                sp.wait_ge(st_lin, 48)
                for j in range(3):
                    sp.dma_start(lists[:, 3 + j, :, :], blocks(lin[j])).then_inc(ld_lin, 16)
                sp.wait_ge(ld_lin, 48)

            @block.tensor
            def _(pe):
                pe.wait_ge(v, marks["run"])
                pe.matmul(p_small[:, 0:1], c.upper[:, :], rank[:, T - 1:T], start=True, stop=True).then_inc(pe_s, 1)

                def count_turn(i, h, start=False, stop=False):
                    pe.wait_ge(digit_ready, i * 2 + h + 1)
                    for u in range(UN):
                        ins = pe.matmul(p_hist[0:HI, 0:LO], one_hi[:, h, u, :], one_lo[:, h, u, :],
                                        start=start and u == 0, stop=stop and u == UN - 1)
                    ins.then_inc(digit_used, 1)
                count_turn(0, 0, start=True)
                count_turn(0, 1)
                with pe.Fori(1, TURNS // 2) as i:
                    for h in (0, 1):
                        count_turn(i, h)
                count_turn(TURNS // 2, 0, stop=True)
                pe.wait_ge(digit_used, TURNS)
                pe.nop().then_inc(counted, 1)
                for side in (0, 1):
                    pe.wait_ge(v, marks[f"ends{side}"])
                    for a in (0, 1):
                        ins = pe.transpose(p_ends[0:REL, a * P:a * P + P], ends[:, a, :], c.ident[:, :])
                    ins.then_inc(pe_s, 1)
                    pe.wait_ge(v, marks[f"carry{side}"])
                    pe.transpose(p_carry[:, 0:REL], carry[:, side:side + P], c.ident[0:REL, 0:REL]).then_inc(pe_s, 1)
                pe.wait_ge(v, marks["lists"])
                for j in range(6):
                    if j == 3:
                        pe.wait_ge(ld_lin, 48)
                    if j >= 2:
                        pe.wait_ge(taken, j - 1)
                    for b in range(4):
                        ins = pe.transpose(p_cols[j % 2][:, b * BLK:b * BLK + BLK], lists[:, j, b, :],
                                           c.ident[0:BLK, 0:BLK])
                    ins.then_inc(turned, 1)
                pe.wait_ge(v, marks["rows"])
                pe.matmul(p_row[0][:, :], c.ones[0:1, :], row[:, 0, :], start=True, stop=True)
                pe.matmul(p_row[1][:, :], c.ones[0:1, :], row[:, 2, :], start=True, stop=True).then_inc(pe_s, 1)



def edge_stage(nc, c, layer, A, rows_in, width, sums):
    L = f"edge{layer}"
    with ExitStack() as ctx:
        def sb(name, shape, dt=FP32):
            return ctx.enter_context(nc.sbuf_tensor(f"{L}_{name}", shape, dt))

        def ps(name, shape):
            return ctx.enter_context(nc.psum_tensor(f"{L}_{name}", shape, FP32))

        wide = AUG if layer in (0, 3) else D
        idx = sb("idx", [P, UN], I32)
        gathered = sb("gathered", [P, UN, width])
        one_hot = sb("one_hot", [P, 2, 2 * P])
        acc = sb("acc", [P, AUG])
        out = sb("out", [P, UN, AUG])
        xT = sb("xT", [P, 2, P])
        msg = sb("msg", [P, 2, AUG])
        p_sum = [ps(f"p_sum{j}", [P, 2, 256]) for j in range(2)]
        if layer in (0, 1, 3):
            p_T = [ps(f"p_T{j}", [P, 512]) for j in range(2)]
        if layer in (0, 3):
            p_z = [ps(f"p_z{j}", [P, 512]) for j in range(2)]
        if layer == 0:
            raw = sb("raw", [K9, 2, HALF * P])
        if layer == 1:
            p_z = [ps(f"p_z{j}", [P, REL, P]) for j in range(2)]
            pick = sb("pick", [P, 2, P])
        if layer == 3:
            raw = sb("raw", [ER, 2, HALF * P])
            weight = sb("weight", [P, 2, HALF * P])
            h1 = sb("h1", [P, 2, HALF * P])
            tw = sb("tw", [P, 2, HALF * P])
            ef = sb("ef", [P, 2, HALF * P])
            p_e = [ps(f"p_e{j}", [P, HALF * P]) for j in range(2)]
        (prepared, indexed, turned, copied, product, message, hot, summed, closed, added,
         v, ended, drained, passed) = sems(
            nc, ctx, L, "prepared", "indexed", "turned", "copied", "product", "message", "hot", "summed",
            "closed", "added", "dve", "ended", "drained", "passed")
        got, stored = c.got, c.closed_out
        if layer in (0, 3):
            raw_in = Ring(nc, f"{L}_raw_in", 2)
        if layer == 3:
            e_h1, e_relu, e_tw, e_ef, e_done = sems(nc, ctx, L, "e_h1", "e_relu", "e_tw", "e_ef", "e_done")

        PREPARED = 3

        with nc.Block() as block:
            @block.gpsimd
            def _(pool):
                pool.wait_ge(prepared, PREPARED)

                def step(t):
                    if t.k % HALF == 0:
                        h = t.k // HALF
                        if not isinstance(t.i, int) or t.i > 0:
                            for j in range(HALF):
                                pool.wait_ge(got[t.slot + j], got.base + 16 * t.i)
                        pool.tensor_copy(idx[:, t.slot:t.slot + HALF], c.src[:, bass.ds(t.n, HALF)])\
                            .then_inc(indexed, 1)
                        pool.wait_ge(indexed, 2 * t.i + h + 1)
                    wait(pool, summed if layer == 2 else turned, t.n + 1 - UN)
                    if layer == 0:
                        wait(pool, hot, t.n + 1 - UN)
                    pool.sem_inc(passed, 1)
                    pool.indirect_dma_start(gathered[:, t.slot, :], None, rows_in,
                                            bass.IndirectOffsetOnAxis(ap=idx[:, t.slot:t.slot + 1], axis=0))\
                        .then_inc(got[t.slot], 16)
                walk(pool, step)

            @block.sync
            def _(sp):
                def load_raw(i, h):
                    cols = bass.ds(i * UN * P + h * HALF * P, HALF * P)
                    if layer == 0:
                        sp.dma_start(raw[:, h, :], A["raw7"][:, cols]).then_inc(raw_in[h], 16)
                    if layer == 3:
                        sp.dma_start(raw[:, h, :], A["raw64"][:, cols]).then_inc(raw_in[h], 16)
                        sp.dma_start(weight[:, h, :], A["weight"][cols].partition_broadcast(P))\
                            .then_inc(raw_in[h], 16)

                if layer == 3:
                    sp.wait_ge(c.raw64_ready, 16)
                load_raw(0, 0)
                load_raw(0, 1)

                def step(t):
                    if t.real:
                        row = sp.value_load(c.sum_row[0:1, t.col()], min_val=0, max_val=DUMP + R)
                        sp.wait_ge(closed, t.n + 1)
                        sp.dma_start(sums[bass.ds(row, P), 0:wide], out[:, t.slot, 0:wide])\
                            .then_inc(stored[t.slot], 16)
                    if t.k % HALF == HALF - 1 and not (isinstance(t.i, int) and t.i == TURNS - 1):
                        load_raw(t.i + 1, t.k // HALF)
                walk(sp, step)
                sp.wait_ge(ended, 1)
                row = sp.value_load(c.sum_row[0:1, T:T + 1], min_val=0, max_val=DUMP)
                sp.dma_start(sums[bass.ds(row, P), 0:wide], acc[:, 0:wide]).then_inc(drained, 16)
                if layer == 0:
                    row = sp.value_load(c.sum_row[0:1, T + 1:T + 2], min_val=0, max_val=DUMP)
                    sp.dma_start(sums[bass.ds(row, P), :], c.zeros[:, :]).then_inc(drained, 16)
                sp.wait_ge(drained, 32 if layer == 0 else 16)
                for k in range(UN):
                    sp.wait_ge(stored[k], stored.base + 16 * TURNS)

            @block.scalar
            def _(act):
                def copy_turned(t):
                    if not t.real:
                        return
                    act.wait_ge(turned, t.n + 1)
                    wait(act, product, t.n - 1)
                    act.copy(xT[:, t.slot % 2, :], p_T[t.slot % 2][:, 0:P]).then_inc(copied, 1)

                def relu_message(t):
                    if not t.real:
                        return
                    act.wait_ge(product, t.n + 1)
                    wait(act, summed, t.n - 1)
                    act.activation(msg[:, t.slot % 2, 0:P], p_z[t.slot % 2][:, 0:P], ACT.Relu).then_inc(message, 1)

                def edge_half(g, h):
                    act.wait_ge(e_h1, g + 1)
                    wait(act, e_done, g - 1)
                    wait(act, e_ef, g - 1)
                    act.activation(h1[:, h, :], p_e[0][:, :], ACT.Relu, bias=c.cols[:, 0:1]).then_inc(e_relu, 1)
                    act.activation(tw[:, h, :], weight[:, h, :], ACT.Sigmoid, scale=c.cols[:, 2:3],
                                   bias=c.cols[:, 3:4]).then_inc(e_tw, 1)

                if layer in (0, 1):
                    walk(act, copy_turned)
                if layer == 3:
                    def step(t):
                        if t.real and t.k % HALF == 0:
                            h = t.k // HALF
                            edge_half(2 * t.i + h, h)
                        copy_turned(t)
                        relu_message(t.back(1))
                    walk(act, step, 1)

            @block.tensor
            def _(pe):
                pe.wait_ge(prepared, PREPARED)

                def turn(t):
                    if not t.real:
                        return
                    pe.wait_ge(got[t.slot], got.base + 16 * t.round + 16)
                    wait(pe, copied, t.n - 1)
                    pe.transpose(p_T[t.slot % 2][:, 0:P], gathered[:, t.slot, 0:D], c.ident[:, :]).then_inc(turned, 1)

                def multiply(t):
                    if not t.real:
                        return
                    x, z = xT[:, t.slot % 2, :], p_z[t.slot % 2]
                    if layer == 0:
                        pe.wait_ge(raw_in[t.slot // HALF], 16 * t.round + 16)
                    if layer == 3:
                        pe.wait_ge(e_ef, 2 * t.round + t.slot // HALF + 1)
                    pe.wait_ge(copied, t.n + 1)
                    wait(pe, message, t.n - 1)
                    if layer == 0:
                        pe.matmul(z[:, 0:P], x, c.w0[:, :], start=True, stop=False)
                        pe.matmul(z[:, 0:P], raw[:, t.slot // HALF, bass.ts(t.slot % HALF, P)], c.we9[:, :],
                                  start=False, stop=True).then_inc(product, 1)
                    if layer == 1:
                        for half in (0, 1):
                            ins = pe.matmul(z[:, half * 4:half * 4 + 4, :], x, c.w1[:, half * 4:half * 4 + 4, :],
                                            start=True, stop=True)
                        ins.then_inc(product, 1)
                    if layer == 3:
                        k = t.slot % HALF
                        pe.matmul(z[:, 0:P], x, c.wn1a[:, :], start=True, stop=False)
                        pe.matmul(z[:, 0:P], ef[:, t.slot // HALF, k * P:k * P + P], c.wn1b[:, :],
                                  start=False, stop=False)
                        pe.matmul(z[:, 0:P], c.ones[0:1, :], c.bn1[0:1, :], start=False, stop=True).then_inc(product, 1)

                def add_up(t):
                    if not t.real:
                        return
                    if layer == 2:
                        pe.wait_ge(got[t.slot], got.base + 16 * t.round + 16)
                        rows = gathered[:, t.slot, 0:D]
                    else:
                        pe.wait_ge(message, t.n + 1)
                        rows = pick[:, t.slot % 2, :] if layer == 1 else msg[:, t.slot % 2, 0:wide]
                    pe.wait_ge(hot, t.n + 1)
                    wait(pe, added, t.n - 1)
                    for half in (0, 1):
                        ins = pe.matmul(p_sum[t.slot % 2][:, half, 0:wide],
                                        one_hot[:, t.slot % 2, half * P:half * P + P], rows, start=True, stop=True)
                    ins.then_inc(summed, 1)

                def features(t):
                    h = t.slot // HALF
                    g = 2 * t.round + h
                    pe.wait_ge(raw_in[h], 32 * t.round + 32)
                    wait(pe, e_relu, g)
                    pe.matmul(p_e[0][:, :], c.we1[:, :], raw[:, h, :], start=True, stop=True).then_inc(e_h1, 1)

                def features2(t):
                    h = t.slot // HALF
                    g = 2 * t.round + h
                    pe.wait_ge(e_relu, g + 1)
                    wait(pe, e_ef, g)
                    pe.matmul(p_e[1][:, :], c.we2[:, :], h1[:, h, :], start=True, stop=True).then_inc(e_done, 1)

                if layer == 2:
                    walk(pe, add_up)
                else:
                    def step(t):
                        turn(t)
                        if layer == 3 and t.real and t.k % HALF == 0:
                            features(t)
                        if layer == 3 and t.real and t.k % HALF == 1:
                            features2(t.back(1))
                        lag = 2 if layer == 3 else 1
                        multiply(t.back(lag))
                        add_up(t.back(lag + 1))
                    walk(pe, step, 3 if layer == 3 else 2)

            @block.vector
            def _(dve):
                dve.memset(acc[:, :], 0.0).then_inc(prepared, 1)
                dve.memset(msg[:, :, P:P + 1], 1.0).then_inc(prepared, 1)
                dve.memset(msg[:, :, P + 1:AUG], 0.0).then_inc(prepared, 1)
                dve.wait_ge(prepared, PREPARED)

                def make_hot(t):
                    if not t.real:
                        return
                    wait(dve, summed, t.n - 1)
                    j = t.slot % 2
                    rank = c.rank[:, t.col()]
                    if layer == 0:
                        dve.wait_ge(got[t.slot], got.base + 16 * t.round + 16)
                        dve.wait_ge(prepared, PREPARED)
                        dve.tensor_copy(msg[:, j, P:P + 1], c.first_dst[:, t.col()])
                        dve.tensor_copy(c.src_scale[:, t.col()], gathered[:, t.slot, D:D + 1])
                    if layer in (0, 3):
                        dve.tensor_scalar(one_hot[:, j, :], c.ramp[:, :], rank, None, ALU.is_equal).then_inc(hot, 1)
                    else:
                        factor = c.inv if layer == 1 else c.src_scale
                        dve.tensor_scalar(one_hot[:, j, :], c.ramp[:, :], rank, factor[:, t.col()],
                                          ALU.is_equal, ALU.mult).then_inc(hot, 1)

                def make_message(t):
                    if not t.real:
                        return
                    j = t.slot % 2
                    dve.wait_ge(product, t.n + 1)
                    wait(dve, summed, t.n - 1)
                    if layer == 0:
                        dve.tensor_scalar(msg[:, j, 0:P], p_z[j][:, 0:P], 0.0, c.norm[:, t.col()],
                                          ALU.max, ALU.mult).then_inc(message, 1)
                    if layer == 1:
                        dve.tensor_scalar(pick[:, j, :], p_z[j][:, 0, :], c.is_rel[:, bass.ds(t.n, 1), 0], None,
                                          ALU.mult).then_inc(v, 1)
                        for r in range(1, REL):
                            dve.wait_ge(v, t.n * (REL - 1) + r)
                            dve.scalar_tensor_tensor(pick[:, j, :], p_z[j][:, r, :], c.is_rel[:, bass.ds(t.n, 1), r],
                                                     pick[:, j, :], ALU.mult, ALU.add)\
                                .then_inc(v if r < REL - 1 else message, 1)

                def close(t):
                    if not t.real:
                        return
                    j = t.slot % 2
                    dve.wait_ge(summed, t.n + 1)
                    wait(dve, stored[t.slot], stored.base + 16 * t.round)
                    wait(dve, added, t.n)
                    dve.tensor_tensor(out[:, t.slot, 0:wide], acc[:, 0:wide], p_sum[j][:, 0, 0:wide], ALU.add)\
                        .then_inc(closed, 1)
                    dve.wait_ge(closed, t.n + 1)
                    dve.scalar_tensor_tensor(acc[:, 0:wide], out[:, t.slot, 0:wide], c.goes_on[:, t.col()],
                                             p_sum[j][:, 1, 0:wide], ALU.mult, ALU.add).then_inc(added, 1)

                def weigh(t):
                    h = t.slot // HALF
                    g = 2 * t.round + h
                    dve.wait_ge(e_tw, g + 1)
                    dve.wait_ge(e_done, g + 1)
                    wait(dve, product, t.n - HALF)
                    dve.scalar_tensor_tensor(ef[:, h, :], p_e[1][:, :], c.cols[:, 1:2], tw[:, h, :],
                                             ALU.add, ALU.mult).then_inc(e_ef, 1)

                def step(t):
                    make_hot(t)
                    if layer == 3 and t.real and t.k % HALF == 0:
                        weigh(t)
                    if layer in (0, 1):
                        make_message(t)
                    close(t.back(1))
                walk(dve, step, 1)
                dve.wait_ge(added, T)
                dve.nop().then_inc(ended, 1)



def node_stage(nc, c, layer, rows_in, rows_out, sums):
    L = f"node{layer}"
    with ExitStack() as ctx:
        def sb(name, shape, dt=FP32):
            return ctx.enter_context(nc.sbuf_tensor(f"{L}_{name}", shape, dt))

        def ps(name, shape):
            return ctx.enter_context(nc.psum_tensor(f"{L}_{name}", shape, FP32))

        wide = AUG if layer in (0, 3) else D
        x = sb("x", [P, UN, D])
        sumrows = sb("sumrows", [P, UN, AUG])
        place = sb("place", [P, 2, P])
        y = sb("y", [P, UN, D])
        out = sb("out", [P, UN, D])
        stats = sb("stats", [P, UN, 6])
        moments = sb("moments", [P, UN, 2])
        std = sb("std", [P, UN])
        rstd = sb("rstd", [P, UN])
        p_y = [ps(f"p_y{j}", [P, 512]) for j in range(2)]
        if layer == 0:
            xT = sb("xT", [P, 2, P])
            own = sb("own", [P, 2, P])
            p_T = [ps(f"p_T{j}", [P, 512]) for j in range(2)]
            p_h = [ps(f"p_h{j}", [P, 512]) for j in range(2)]
        if layer == 3:
            sT = sb("sT", [P, 2, P])
            deg = sb("deg", [1, 2, P])
            p_s = [ps(f"p_s{j}", [P, 512]) for j in range(2)]
            p_d = [ps(f"p_d{j}", [P, 512]) for j in range(2)]
        (placed, turned, copied, product, owned, summed, made, halves, measured, rooted, inverted,
         normed, marked, passed) = sems(
            nc, ctx, L, "placed", "turned", "copied", "product", "owned", "summed", "made", "halves", "measured",
            "rooted", "inverted", "normed", "marked", "passed")
        x_in, sums_in, stored = c.x_in, c.sums_in, c.rows_out

        with nc.Block() as block:
            @block.sync
            def _(sp):
                def step(t):
                    h = t.slot // HALF
                    if t.k % HALF == 0:
                        wait(sp, made, t.n - HALF)
                        if not isinstance(t.i, int) or t.i > 0:
                            sp.wait_ge(made, 1)
                        sp.dma_start(x[:, t.slot:t.slot + HALF, :],
                                     rows_in[bass.ds(t.n * P, HALF * P), 0:D].rearrange("(k p) d -> p k d", p=P))\
                            .then_inc(x_in[h], 16)
                    row = sp.value_load(c.sum_start[0:1, t.col()], min_val=0, max_val=R)
                    wait(sp, summed, t.n + 1 - UN)
                    sp.dma_start(sumrows[:, t.slot, 0:wide], sums[bass.ds(row, P), 0:wide])\
                        .then_inc(sums_in[t.slot], 16)
                walk(sp, step)

            @block.gpsimd
            def _(pool):
                def step(t):
                    if t.k % HALF == HALF - 1:
                        h = t.slot // HALF
                        b = t.back(HALF - 1)
                        pool.wait_ge(normed, t.n + 1)
                        pool.sem_inc(passed, 1)
                        pool.dma_start(rows_out[bass.ds(b.n * P, HALF * P), :].rearrange("(k p) d -> p k d", p=P),
                                       out[:, b.slot:b.slot + HALF, :]).then_inc(stored[h], 16)
                walk(pool, step)
                for h in (0, 1):
                    pool.wait_ge(stored[h], stored.base + 16 * TURNS)

            @block.scalar
            def _(act):
                def copy_turned(t):
                    if not t.real:
                        return
                    j = t.slot % 2
                    act.wait_ge(turned, t.n + 1)
                    wait(act, product if layer == 0 else summed, t.n - 1)
                    if layer == 0:
                        act.copy(xT[:, j, :], p_T[j][:, 0:P]).then_inc(copied, 1)
                    else:
                        act.copy(deg[:, j, :], p_d[j][0:1, 0:P])
                        act.copy(sT[:, j, :], p_s[j][:, 0:P]).then_inc(copied, 1)

                def relu_own(t):
                    if not t.real:
                        return
                    j = t.slot % 2
                    act.wait_ge(product, t.n + 1)
                    wait(act, made, t.n - 1)
                    act.activation(own[:, j, :], p_h[j][:, 0:P], ACT.Relu).then_inc(owned, 1)

                def root(t):
                    if not t.real:
                        return
                    act.wait_ge(measured, t.n + HALF)
                    g = slice(t.slot, t.slot + HALF)
                    act.activation(std[:, g, None], moments[:, g, 1:2], ACT.Sqrt, bias=c.eps[:, 0:1]).then_inc(rooted, 1)

                def step(t):
                    if layer in (0, 3):
                        copy_turned(t)
                    if layer == 0:
                        relu_own(t.back(1))
                    if t.k % HALF == HALF - 1:
                        root(t.back(UN - 1))
                walk(act, step, HALF)

            @block.tensor
            def _(pe):
                def turn(t):
                    if not t.real:
                        return
                    j = t.slot % 2
                    pe.wait_ge(x_in[t.slot // HALF], x_in.base + 16 * t.round + 16)
                    wait(pe, copied, t.n - 1)
                    pe.transpose(p_T[j][:, 0:P], x[:, t.slot, :], c.ident[:, :]).then_inc(turned, 1)

                def own_product(t):
                    if not t.real:
                        return
                    j = t.slot % 2
                    pe.wait_ge(copied, t.n + 1)
                    wait(pe, owned, t.n - 1)
                    pe.matmul(p_h[j][:, 0:P], xT[:, j, :], c.w0[:, :], start=True, stop=False)
                    pe.matmul(p_h[j][:, 0:P], c.ones[0:2, :], c.root2[:, :], start=False, stop=True)\
                        .then_inc(product, 1)

                def place_sums(t):
                    if not t.real:
                        return
                    j = t.slot % 2
                    pe.wait_ge(placed, t.n + 1)
                    wait(pe, made, t.n - 1)
                    if layer in (0, 1):
                        pe.wait_ge(x_in[t.slot // HALF], x_in.base + 16 * t.round + 16)
                        pe.matmul(p_y[j][:, 0:P], place[:, j, :], sumrows[:, t.slot, 0:D], start=True, stop=False)
                        if layer == 1:
                            pe.matmul(p_y[j][:, 0:P], c.ones[0:1, :], c.bias1[:, :], start=False, stop=False)
                        pe.matmul(p_y[j][:, 0:P], c.ident[:, :], x[:, t.slot, :], start=False, stop=True)\
                            .then_inc(summed, 1)
                    if layer == 2:
                        pe.matmul(p_y[j][:, 0:P], place[:, j, :], sumrows[:, t.slot, 0:D], start=True, stop=True)\
                            .then_inc(summed, 1)

                def place_turned(t):
                    if not t.real:
                        return
                    j = t.slot % 2
                    pe.wait_ge(placed, t.n + 1)
                    wait(pe, copied, t.n - 1)
                    pe.matmul(p_d[j][0:1, 0:P], sumrows[:, t.slot, D:D + 1], place[:, j, :], start=True, stop=True)
                    pe.matmul(p_s[j][:, 0:P], sumrows[:, t.slot, 0:D], place[:, j, :], start=True, stop=True)\
                        .then_inc(turned, 1)

                def last_product(t):
                    if not t.real:
                        return
                    j = t.slot % 2
                    pe.wait_ge(copied, t.n + 1)
                    wait(pe, made, t.n - 1)
                    pe.matmul(p_y[j][:, 0:P], sT[:, j, :], c.wn2[:, :], start=True, stop=False)
                    pe.matmul(p_y[j][:, 0:P], deg[0:1, j, :], c.bn2[:, :], start=False, stop=True).then_inc(summed, 1)

                def step(t):
                    if layer == 0:
                        turn(t)
                        own_product(t.back(1))
                        place_sums(t.back(1))
                    elif layer == 3:
                        place_turned(t)
                        last_product(t.back(1))
                    else:
                        place_sums(t)
                walk(pe, step, 0 if layer in (1, 2) else 1)

            @block.vector
            def _(dve):
                def mark(t):
                    if not t.real:
                        return
                    j = t.slot % 2
                    wait(dve, turned if layer == 3 else summed, t.n - 1)
                    if layer == 0:
                        dve.wait_ge(sums_in[t.slot], sums_in.base + 16 * t.round + 16)
                        dve.tensor_tensor(c.node_of[:, t.col()], sumrows[:, t.slot, D:D + 1],
                                          c.tile_base[:, t.col()], ALU.subtract).then_inc(marked, 1)
                        dve.wait_ge(marked, t.n + 1)
                    else:
                        dve.wait_ge(sums_in[t.slot], sums_in.base + 16 * t.round + 16)
                    dve.tensor_scalar(place[:, j, :], c.ramp[:, 0:P], c.node_of[:, t.col()], None, ALU.is_equal)\
                        .then_inc(placed, 1)

                def make(t):
                    if not t.real:
                        return
                    j, s = t.slot % 2, t.slot
                    wait(dve, normed, t.n + 1 - UN)
                    dve.wait_ge(summed, t.n + 1)
                    if layer == 0:
                        dve.wait_ge(owned, t.n + 1)
                        ins = dve.scalar_tensor_tensor(y[:, s, :], own[:, j, :], c.inv_deg[:, t.col()],
                                                       p_y[j][:, 0:P], ALU.mult, ALU.add)
                    if layer == 1:
                        ins = dve.tensor_copy(y[:, s, :], p_y[j][:, 0:P])
                    if layer in (2, 3):
                        dve.wait_ge(x_in[s // HALF], x_in.base + 16 * t.round + 16)
                    if layer == 2:
                        ins = dve.scalar_tensor_tensor(y[:, s, :], p_y[j][:, 0:P], c.scale2[:, t.col()],
                                                       x[:, s, :], ALU.mult, ALU.add)
                    if layer == 3:
                        ins = dve.scalar_tensor_tensor(y[:, s, :], x[:, s, :], 2.0, p_y[j][:, 0:P],
                                                       ALU.mult, ALU.add)
                    ins.then_inc(made, 1)

                def measure(t):
                    if not t.real:
                        return
                    dve.wait_ge(made, t.n + 1)
                    dve.bn_stats(stats[:, t.slot, :], y[:, t.slot, :]).then_inc(halves, 1)

                def spread_of(t):
                    if not t.real:
                        return
                    dve.wait_ge(halves, t.n + 1)
                    dve.sem_inc(passed, 1)
                    dve.bn_aggr(moments[:, t.slot, :], stats[:, t.slot, :]).then_inc(measured, 1)

                def invert(t):
                    if not t.real:
                        return
                    g = slice(t.slot, t.slot + HALF)
                    dve.wait_ge(rooted, t.round * 2 + t.slot // HALF + 1)
                    dve.reciprocal(rstd[:, g], std[:, g]).then_inc(inverted, 1)
                    dve.wait_ge(inverted, t.round * 2 + t.slot // HALF + 1)

                def norm(t):
                    if not t.real:
                        return
                    s = t.slot
                    wait(dve, stored[s // HALF], stored.base + 16 * t.round)
                    dve.tensor_scalar(out[:, s, :], y[:, s, :], moments[:, s, 0:1], rstd[:, s:s + 1],
                                      ALU.subtract, ALU.mult).then_inc(normed, 1)

                def step(t):
                    mark(t)
                    make(t.back(1))
                    measure(t.back(2))
                    spread_of(t.back(3))
                    if t.k % HALF == 0:
                        invert(t.back(UN))
                    norm(t.back(UN))
                walk(dve, step, UN)



INPUTS = ["x_aug", "ints", "floats", "raw64_rows", "src", "dst", "etype", "norm", "weight", "raw7", "raw64", "degree_cols", "scale2_cols",
          "L0_gnn_W", "L0_gnn_b", "L0_gnn_We", "L0_gnn_be", "L0_gnn_root_emb", "L1_gnn_weight", "L1_gnn_bias",
          "L3_gnn_We1", "L3_gnn_be1", "L3_gnn_We2", "L3_gnn_be2", "L3_gnn_Wt", "L3_gnn_bt", "L3_gnn_Wn1",
          "L3_gnn_bn1", "L3_gnn_Wn2", "L3_gnn_bn2"]


class Constants:

    def __init__(self, nc, ctx):
        def sb(name, shape, dt=FP32):
            return ctx.enter_context(nc.sbuf_tensor(name, shape, dt))

        self.ident = sb("ident", [P, P])
        self.upper = sb("upper", [P, P])
        self.ramp = sb("ramp", [P, 2 * P])
        self.tile_base = sb("tile_base", [P, T])
        self.ones = sb("ones", [P, P])
        self.zeros = sb("zeros", [P, AUG])
        self.eps = sb("eps", [P, 1])
        self.w0 = sb("w0", [D, D])
        self.we9 = sb("we9", [K9, D])
        self.root2 = sb("root2", [2, D])
        self.w1 = sb("w1", [D, REL, D])
        self.bias1 = sb("bias1", [1, D])
        self.we1 = sb("we1", [ER, D])
        self.we2 = sb("we2", [D, D])
        self.wn1a = sb("wn1a", [D, D])
        self.wn1b = sb("wn1b", [D, D])
        self.wn2 = sb("wn2", [D, D])
        self.bn1 = sb("bn1", [1, D])
        self.bn2 = sb("bn2", [1, D])
        self.cols = sb("cols", [P, 4])
        self.inv_deg = sb("inv_deg", [P, T])
        self.scale2 = sb("scale2", [P, T])
        self.src = sb("src_cols", [P, T], I32)
        self.norm = sb("norm_cols", [P, T])
        self.is_rel = sb("is_rel", [P, T, REL])
        self.rank = sb("rank_cols", [P, T])
        self.inv = sb("inv_cols", [P, T])
        self.first_dst = sb("first_dst", [P, T])
        self.src_scale = sb("src_scale", [P, T])
        self.goes_on = sb("goes_on", [P, T])
        self.node_of = sb("node_of", [P, T])
        self.got = Ring(nc, "got")
        self.closed_out = Ring(nc, "closed_out")
        self.x_in = Ring(nc, "x_in", 2)
        self.sums_in = Ring(nc, "sums_in")
        self.rows_out = Ring(nc, "rows_out", 2)
        self.sum_row = sb("sum_row", [1, T + 2], I32)
        self.sum_start = sb("sum_start", [1, T], I32)


def program(nc, A, out):
    with ExitStack() as ctx:
        c = Constants(nc, ctx)
        sums = nc.dram_tensor("sums", [DUMP + R + P, AUG], FP32).ap()
        rows = [nc.dram_tensor(f"rows{j}", [R, D], FP32).ap() for j in range(3)]
        S = {name: nc.dram_tensor(f"by_dst_{name}", A[name].shape, A[name].dtype).ap()
             for name in LISTS + ("raw7", "raw64")}
        c.raw64_ready = nc.alloc_semaphore("raw64_ready")
        constants_stage(nc, c, A)
        order_stage(nc, c, A, S)
        index_stage(nc, c, S)
        x = A["x_aug"]
        for layer in range(4):
            y = rows[layer] if layer < 3 else out
            edge_stage(nc, c, layer, S, x, AUG if layer == 0 else D, sums)
            node_stage(nc, c, layer, x, y, sums)
            for ring in (c.got, c.closed_out, c.x_in, c.sums_in, c.rows_out):
                ring.next_layer()
            x = y


def laid_out(inputs):
    import numpy as np

    def pad(a, rows, value=0):
        a = np.asarray(a)
        return np.concatenate([a, np.full((rows - a.shape[0],) + a.shape[1:], value, a.dtype)])

    def cols(a):
        return np.ascontiguousarray(a.reshape(T, P).T)

    A = {k: np.ascontiguousarray(inputs[k]) for k in INPUTS if k in inputs}
    nv = pad(np.asarray(inputs["node_vec1"]).reshape(-1), R, 1)
    x = pad(inputs["x"], R)
    A["x_aug"] = np.concatenate([x, nv[:, None], np.zeros((R, AUG - D - 1), x.dtype)], axis=1)
    A["src"] = pad(inputs["src"], R)
    dst = pad(inputs["dst"], R, R - 1)
    A["dst"] = np.concatenate([np.full(1, -1, dst.dtype), dst, np.full(1, R, dst.dtype)])
    A["etype"] = pad(inputs["edge_type_8"], R)
    A["norm"] = pad(np.asarray(inputs["edge_weight1"]).reshape(-1), R)
    A["weight"] = pad(inputs["edge_weight"], R)
    e7 = pad(inputs["edge_attr_7"], R)
    A["raw7"] = np.concatenate([e7.T, np.ones((2, R), e7.dtype)])
    A["raw64"] = np.ascontiguousarray(pad(inputs["edge_attr_64"], R).T)
    A["ints"] = np.stack([dst, A["src"], A["etype"]], axis=1)
    A["floats"] = np.concatenate([A["norm"][:, None], A["weight"][:, None], e7], axis=1)
    A["raw64_rows"] = pad(inputs["edge_attr_64"], R)
    A["degree_cols"] = cols(nv)
    A["scale2_cols"] = cols(pad(np.asarray(inputs["node_vec1_n2"]).reshape(-1), R, 1))
    return {k: A[k] for k in INPUTS}


def kernel(**inputs):
    import numpy as np
    import concourse.bacc as bacc
    from concourse.bass_utils import run_bass_kernel_spmd

    nc = bacc.Bacc("TRN2", target_bir_lowering=False, num_devices=1)
    arrays = {f"in_{k}": v for k, v in laid_out(inputs).items()}
    A = {k[3:]: nc.dram_tensor(k, v.shape, mybir.dt.from_np(v.dtype), kind="ExternalInput").ap()
         for k, v in arrays.items()}
    out = nc.dram_tensor("out_rows", (R, D), FP32, kind="ExternalOutput").ap()
    program(nc, A, out)
    r = run_bass_kernel_spmd(nc, [arrays], core_ids=[0])
    return r.results[0]["out_rows"][:N]
```

```python
from contextlib import ExitStack

import concourse.bass as bass
from concourse import mybir

FP32 = mybir.dt.float32
BF16 = mybir.dt.bfloat16
I32 = mybir.dt.int32
ALU = mybir.AluOpType
ACT = mybir.ActivationFunctionType
AXX = mybir.AxisListType.X

P = 128
N = 50000
D = 128
UN = 8
T = -(-N // (P * UN)) * UN
TURNS = T // UN
R = T * P
HALF = UN // 2
WIDE = 2 * UN
DEEP = 4
REL = 8
RAW = 7
K9 = RAW + 2
ER = 64
AUG = 132
DUMP = R + 3 * P
EPS = 1e-5
BLK = T // 4
HI = -(-T // 16)
LO = 16


def wait(e, sem, n):
    if not isinstance(n, int) or n > 0:
        e.wait_ge(sem, n)


def walk(e, step, drain=0, unroll=UN, last=1):
    turns = -(-T // unroll)
    left = T - (turns - 1) * unroll
    for i in (0, 1):
        for k in range(unroll):
            step(Tile(i, k, unroll))
    with e.Fori(2, turns - last) as i:
        for k in range(unroll):
            step(Tile(i, k, unroll))
    for i in range(turns - last, turns - 1):
        for k in range(unroll):
            step(Tile(i, k, unroll))
    for k in range(left + drain):
        step(Tile(turns - 1, k, unroll))


class Tile:

    def __init__(self, i, k, unroll=UN):
        self.i, self.k, self.unroll = i, k, unroll
        self.n = i * unroll + k
        self.slot = k % unroll
        self.round = i + k // unroll
        self.s8 = k % UN
        self.round8 = i * (unroll // UN) + k // UN
        self.group = i * (unroll // HALF) + k // HALF
        self.j = k % DEEP
        self.b = k % 2
        self.real = not isinstance(i, int) or 0 <= self.n < T

    def back(self, d):
        return Tile(self.i, self.k - d, self.unroll)

    def col(self, width=1):
        return bass.ds(self.n, width)


def cleared(nc, handles):
    nc.clear_and_free_semaphores(handles)
    nc.all_engine_barrier()


def sems(nc, ctx, stage, *names):
    handles = [nc.alloc_semaphore(f"{stage}_{n}") for n in names]
    ctx.callback(cleared, nc, handles)
    return handles


class Ring:

    def __init__(self, nc, name, n, dmas=0):
        self.sems = [nc.alloc_semaphore(f"{name}{k}") for k in range(n)]
        self.uses = [len(range(k, dmas, n)) for k in range(n)]
        self.base = [0] * n

    def __getitem__(self, k):
        return self.sems[k]

    def next_layer(self):
        self.base = [b + 16 * u for b, u in zip(self.base, self.uses)]



LISTS = ("dst", "src", "etype", "norm", "weight")
CHUNK = R // 8
FIELDS = 3 + 2 + RAW + ER


def order_stage(nc, c, A, S):
    with ExitStack() as ctx:
        def sb(name, shape, dt=FP32):
            return ctx.enter_context(nc.sbuf_tensor(name, shape, dt))

        pair = sb("pair", [P, 2, T], I32)
        pairf = sb("pairf", [P, 2, T])
        falls = sb("falls", [P, T])
        worst = sb("worst", [P, 1])
        flag = sb("flag", [1, 1], I32)
        p_flag = ctx.enter_context(nc.psum_tensor("p_flag", [P, 512], FP32))
        loaded, v, voted, ready = sems(nc, ctx, "order", "loaded", "dve", "voted", "ready")
        with nc.Block() as block:
            @block.sync
            def _(sp):
                for j in (0, 1):
                    sp.dma_start(pair[:, j, :], A["dst"][j:j + R].rearrange("(p t) -> p t", p=P)).then_inc(loaded, 16)

            @block.vector
            def _(dve):
                dve.wait_ge(loaded, 32)
                dve.tensor_copy(pairf[:, :, :], pair[:, :, :]).then_inc(v, 1)
                dve.wait_ge(v, 1)
                dve.tensor_tensor(falls[:, :], pairf[:, 0, :], pairf[:, 1, :], ALU.is_gt).then_inc(v, 1)
                dve.wait_ge(v, 2)
                dve.reduce_max(worst[:, :], falls[:, :], AXX).then_inc(v, 1)
                dve.wait_ge(voted, 1)
                dve.tensor_copy(flag[:, :], p_flag[0:1, 0:1]).then_inc(ready, 1)

            @block.tensor
            def _(pe):
                pe.wait_ge(v, 3)
                pe.matmul(p_flag[0:1, 0:1], worst[:, :], c.ones[:, 0:1], start=True, stop=True).then_inc(voted, 1)

        keys_i = sb("keys_i", [P, CHUNK], I32)
        keys = sb("keys", [P, CHUNK])
        number = sb("number", [P, CHUNK])
        less = sb("less", [P, CHUNK])
        key_i = sb("key_i", [P, T], I32)
        key = sb("key", [P, T])
        own = sb("own", [P, T])
        part = sb("part", [P, 1])
        place = sb("place", [P, T])
        place_i = sb("place_i", [P, T], I32)
        record = sb("record", [P, 1, FIELDS], I32)
        target = sb("target", [P, 1], I32)
        (chunk_in, chunk_used, col_in, made, w, rank_done, record_in, pointed, sent, listed, small_in, sent_for) = sems(
            nc, ctx, "sort", "chunk_in", "chunk_used", "col_in", "made", "dve", "rank_done", "record_in", "pointed",
            "sent", "listed", "small_in", "sent_for")
        recs = nc.dram_tensor("recs", [R, FIELDS], I32).ap()
        parts = [("ints", 0, 3), ("floats", 3, 2 + RAW), ("raw64_rows", 5 + RAW, ER)]
        with nc.Block() as block:
            @block.sync
            def _(sp):
                unsorted = sp.value_load(flag[0:1, 0:1], min_val=0, max_val=P)
                with sp.If(unsorted > 0):
                    with nc.allow_non_contiguous_dma(reason="the general path for edges in any order"):
                        sp.dma_start(key_i[:, :], A["dst"][1:R + 1].rearrange("(t p) -> p t", p=P))\
                            .then_inc(col_in, 16)
                    for n in range(R // CHUNK):
                        if n:
                            sp.wait_ge(chunk_used, n)
                        sp.dma_start(keys_i[:, :], A["dst"][1 + n * CHUNK:1 + (n + 1) * CHUNK].partition_broadcast(P))\
                            .then_inc(chunk_in, 16)
                    sp.wait_ge(rank_done, 1)
                    with sp.Fori(0, T) as t:
                        sp.wait_ge(made, t + 1)
                        for name, at, n in parts:
                            sp.dma_start(record[:, 0, at:at + n], A[name][bass.ds(t * P, P), :].bitcast(I32))\
                                .then_inc(record_in, 16)
                    sp.wait_ge(made, T + 1)
                    columns = [(S["dst"][1:R + 1], 0), (S["src"], 1), (S["etype"], 2),
                               (S["norm"].bitcast(I32), 3), (S["weight"].bitcast(I32), 4)]
                    columns += [(S["raw7"][j, :].bitcast(I32), 5 + j) for j in range(RAW)]
                    columns += [(S["raw64"][j, :].bitcast(I32), 5 + RAW + j) for j in range(ER)]
                    with nc.allow_non_contiguous_dma(reason="the general path for edges in any order"):
                        for dst, j in columns:
                            sp.dma_start(dst.rearrange("(a b) -> a b", a=P),
                                         recs[:, j].rearrange("(a b) -> a b", a=P)).then_inc(listed, 16)
                    sp.dma_start(S["raw7"][RAW:K9, :], A["raw7"][RAW:K9, :]).then_inc(listed, 16)
                    for at in (0, R + 1):
                        sp.dma_start(S["dst"][at:at + 1], A["dst"][at:at + 1]).then_inc(listed, 16)
                    sp.wait_ge(listed, 16 * (FIELDS + 3))
                    sp.sem_inc(c.raw64_ready, 16)
                with sp.Else():
                    for name in LISTS:
                        sp.dma_start(S[name], A[name]).then_inc(small_in, 16)
                    sp.dma_start(S["raw7"], A["raw7"]).then_inc(small_in, 16)
                    sp.dma_start(S["raw64"], A["raw64"]).then_inc(c.raw64_ready, 16)
                    sp.wait_ge(small_in, 16 * (len(LISTS) + 1))

            @block.vector
            def _(dve):
                unsorted = dve.value_load(flag[0:1, 0:1], min_val=0, max_val=P)
                with dve.If(unsorted > 0):
                    count = [0]

                    def link(ins):
                        count[0] += 1
                        ins.then_inc(w, 1)
                        dve.wait_ge(w, count[0])

                    dve.wait_ge(col_in, 16)
                    dve.wait_ge(pointed, 1)
                    dve.tensor_copy(key[:, :], key_i[:, :])
                    link(dve.memset(place[:, :], 0.0))
                    for n in range(R // CHUNK):
                        dve.wait_ge(chunk_in, 16 * n + 16)
                        link(dve.tensor_copy(keys[:, :], keys_i[:, :]))
                        if n:
                            link(dve.tensor_scalar(own[:, :], own[:, :], -float(CHUNK), None, ALU.add))
                        base = count[0]
                        with dve.Fori(0, T) as t:
                            at = bass.ds(t, 1)
                            dve.tensor_scalar(less[:, :], number[:, :], own[:, at], None, ALU.is_lt).then_inc(w, 1)
                            dve.wait_ge(w, t * 5 + base + 1)
                            dve.scalar_tensor_tensor(less[:, :], keys[:, :], key[:, at], less[:, :],
                                                     ALU.is_equal, ALU.mult).then_inc(w, 1)
                            dve.wait_ge(w, t * 5 + base + 2)
                            dve.scalar_tensor_tensor(less[:, :], keys[:, :], key[:, at], less[:, :],
                                                     ALU.is_lt, ALU.add).then_inc(w, 1)
                            dve.wait_ge(w, t * 5 + base + 3)
                            dve.reduce_sum(part[:, :], less[:, :], AXX).then_inc(w, 1)
                            dve.wait_ge(w, t * 5 + base + 4)
                            dve.tensor_tensor(place[:, at], place[:, at], part[:, :], ALU.add).then_inc(w, 1)
                            dve.wait_ge(w, t * 5 + base + 5)
                        count[0] += 5 * T
                        dve.nop().then_inc(chunk_used, 1)
                    link(dve.tensor_copy(place_i[:, :], place[:, :]))
                    dve.nop().then_inc(rank_done, 1)
                with dve.Else():
                    dve.nop()

            @block.gpsimd
            def _(pool):
                unsorted = pool.value_load(flag[0:1, 0:1], min_val=0, max_val=P)
                with pool.If(unsorted > 0):
                    pool.iota(number[:, :], [[1, CHUNK]], base=0, channel_multiplier=0,
                              allow_small_or_imprecise_dtypes=True)
                    pool.iota(own[:, :], [[P, T]], base=0, channel_multiplier=1,
                              allow_small_or_imprecise_dtypes=True).then_inc(pointed, 1)
                    pool.wait_ge(rank_done, 1)
                    pool.nop().then_inc(made, 1)
                    with pool.Fori(0, T) as t:
                        pool.tensor_copy(target[:, :], place_i[:, bass.ds(t, 1)]).then_inc(pointed, 1)
                        pool.wait_ge(pointed, t + 2)
                        pool.wait_ge(record_in, t * (16 * len(parts)) + 16 * len(parts))
                        pool.sem_inc(sent_for, 1)
                        pool.indirect_dma_start(recs, bass.IndirectOffsetOnAxis(ap=target[:, 0:1], axis=0),
                                                record[:, 0, :], None).then_inc(sent, 16)
                        pool.wait_ge(sent, t * 16 + 16)
                        pool.sem_inc(made, 1)
                with pool.Else():
                    pool.nop()



def constants_stage(nc, c, A):
    with ExitStack() as ctx:
        loaded, zeroed, made = sems(nc, ctx, "const", "loaded", "zeroed", "made")
        loads = [
            (c.w0[:, :], A["L0_gnn_W"][:, :]),
            (c.we9[0:RAW, :], A["L0_gnn_We"][:, :]),
            (c.we9[RAW:RAW + 1, :], A["L0_gnn_b"]),
            (c.we9[RAW + 1:K9, :], A["L0_gnn_be"]),
            (c.root2[0:1, :], A["L0_gnn_b"]),
            (c.root2[1:2, :], A["L0_gnn_root_emb"][:, :]),
            (c.w1[:, :, :], A["L1_gnn_weight"].rearrange("r f g -> f r g")),
            (c.bias1[:, :], A["L1_gnn_bias"]),
            (c.we1[:, :], A["L3_gnn_We1"][:, :]),
            (c.we2[:, :], A["L3_gnn_We2"][:, :]),
            (c.wn1a[:, :], A["L3_gnn_Wn1"][0:D, :]),
            (c.wn1b[:, :], A["L3_gnn_Wn1"][D:2 * D, :]),
            (c.wn2[:, :], A["L3_gnn_Wn2"][:, :]),
            (c.bn1[:, :], A["L3_gnn_bn1"]),
            (c.bn2[:, :], A["L3_gnn_bn2"]),
            (c.cols[:, 0:1], A["L3_gnn_be1"]),
            (c.cols[:, 1:2], A["L3_gnn_be2"]),
            (c.cols[:, 2:3], A["L3_gnn_Wt"]),
            (c.cols[:, 3:4], A["L3_gnn_bt"]),
            (c.inv_deg[:, :], A["degree_cols"][:, :]),
            (c.scale2[:, :], A["scale2_cols"][:, :]),
        ]
        with nc.Block() as block:
            @block.sync
            def _(sp):
                for dst, src in loads:
                    sp.dma_start(dst, src).then_inc(loaded, 16)
                sp.wait_ge(loaded, 16 * len(loads))

            @block.gpsimd
            def _(pool):
                pool.memset(c.ident[:, :], 0.0).then_inc(zeroed, 1)
                pool.memset(c.upper[:, :], 1.0).then_inc(zeroed, 1)
                pool.iota(c.ramp[:, :], [[1, 2 * P]], base=0, channel_multiplier=0,
                          allow_small_or_imprecise_dtypes=True).then_inc(made, 1)
                pool.iota(c.tile_base[:, :], [[P, T]], base=0, channel_multiplier=0,
                          allow_small_or_imprecise_dtypes=True).then_inc(made, 1)
                pool.wait_ge(zeroed, 2)
                pool.affine_select(out=c.ident[:, :], in_=c.ident[:, :], compare_op=ALU.not_equal, fill=1.0,
                                   base=0, pattern=[[-1, P]], channel_multiplier=1).then_inc(made, 1)
                pool.affine_select(out=c.upper[:, :], in_=c.upper[:, :], compare_op=ALU.is_gt, fill=0.0,
                                   base=0, pattern=[[1, P]], channel_multiplier=-1).then_inc(made, 1)
                pool.wait_ge(made, 4)

            @block.vector
            def _(dve):
                dve.memset(c.ones[:, :], 1.0)
                dve.memset(c.zeros[:, :], 0.0)
                dve.memset(c.eps[:, :], EPS)
                dve.wait_ge(loaded, 16 * len(loads))
                dve.reciprocal(c.inv_deg[:, :], c.inv_deg[:, :])


def index_stage(nc, c, A):
    with ExitStack() as ctx:
        def sb(name, shape, dt=FP32):
            return ctx.enter_context(nc.sbuf_tensor(name, shape, dt))

        def ps(name, shape):
            return ctx.enter_context(nc.psum_tensor(name, shape, FP32))

        dsti = sb("dsti", [P, 3, T], I32)
        typi = sb("typi", [P, T], I32)
        dstf = sb("dstf", [P, 3, T])
        typf = sb("typf", [P, T])
        same = sb("same", [P, 2, T])
        first = sb("first", [P, T])
        onesT = sb("onesT", [P, T])
        rank = sb("rank", [P, T])
        fdst = sb("fdst", [P, T])
        masks = sb("masks", [P, REL, T])
        run = sb("run", [P, REL, T])
        tmp = sb("tmp", [P, REL, T])
        through = sb("through", [P, T])
        total = sb("total", [P, 2, T])
        ends = sb("ends", [P, 2, REL])
        endsT = sb("endsT", [REL, 2, P])
        carry = sb("carry", [REL, P + 1])
        carryC = sb("carryC", [P, REL])
        before = sb("before", [P, 1])
        digits_i = sb("digits_i", [P, 3, T], I32)
        digits = sb("digits", [P, 2, T])
        one_hi = sb("one_hi", [P, 2, UN, HI], BF16)
        one_lo = sb("one_lo", [P, 2, UN, LO], BF16)
        hist = sb("hist", [HI, LO])
        hrow = sb("hrow", [1, HI * LO])
        urow = sb("urow", [1, HI * LO + 1])
        lists_i = sb("lists_i", [BLK, 2, 4, P], I32)
        lists = sb("lists", [BLK, 6, 4, P])
        row = sb("row", [1, 6, T])
        row_i = sb("row_i", [1, T + 1], I32)
        p_small = ps("p_small", [P, 512])
        p_ends = ps("p_ends", [P, 512])
        p_carry = ps("p_carry", [P, 512])
        p_hist = ps("p_hist", [P, 512])
        p_cols = [ps(f"p_cols{j}", [P, T]) for j in range(2)]
        p_row = [ps(f"p_row{j}", [P, T]) for j in range(2)]
        (ld_edges, ld_lists, v, pe_s, st_lin, ld_lin, ld_hist, st_hist, digit_ready, digit_used, counted,
         turned, taken, zero_sem, act_s) = sems(
            nc, ctx, "index", "edges", "lists", "dve", "pe", "stored", "relisted", "hist_in", "hist_out",
            "digit_ready", "digit_used", "counted", "turned", "taken", "zeroed", "act")
        lin = [nc.dram_tensor(f"lin{j}", [R], FP32).ap() for j in range(3)]
        hist_d = nc.dram_tensor("hist_d", [HI * LO], FP32).ap()

        def pmajor(a, off=0):
            return a[off:off + R].rearrange("(p t) -> p t", p=P)

        def blocks(a, off=0):
            return a[off:off + R].rearrange("(b t p) -> t b p", b=4, p=P)

        marks = {}
        with nc.Block() as block:
            @block.vector
            def _(dve):
                count = [0]

                def link(ins, name=None):
                    count[0] += 1
                    ins.then_inc(v, 1)
                    dve.wait_ge(v, count[0])
                    if name:
                        marks[name] = count[0]

                dve.memset(onesT[:, :], 1.0)
                dve.memset(urow[:, 0:1], 0.0)
                link(dve.memset(carry[:, :], 0.0))
                dve.wait_ge(ld_edges, 64)
                dve.tensor_copy(typf[:, :], typi[:, :])
                link(dve.tensor_copy(dstf[:, :, :], dsti[:, :, :]))
                for side in (0, 1):
                    last = dve.tensor_tensor(same[:, side, :], dstf[:, 1, :], dstf[:, 2 * side, :], ALU.is_equal)
                link(last)
                link(dve.tensor_scalar(first[:, :], same[:, 0, :], -1.0, 1.0, ALU.mult, ALU.add))
                dve.tensor_tensor(fdst[:, :], first[:, :], dstf[:, 1, :], ALU.mult)
                link(dve.tensor_tensor_scan(rank[:, :], onesT[:, :], first[:, :], 0.0, ALU.mult, ALU.add), "run")
                dve.wait_ge(pe_s, 1)
                link(dve.tensor_copy(before[:, :], p_small[:, 0:1]))
                link(dve.tensor_scalar(rank[:, :], rank[:, :], before[:, 0:1], -1.0, ALU.add, ALU.add), "rank")
                link(dve.tensor_scalar(digits_i[:, 0, :], dsti[:, 1, :], 7, None, ALU.arith_shift_right))
                dve.tensor_scalar(digits_i[:, 1, :], digits_i[:, 0, :], 4, None, ALU.arith_shift_right)
                link(dve.tensor_scalar(digits_i[:, 2, :], digits_i[:, 0, :], 15, None, ALU.bitwise_and))
                link(dve.tensor_copy(digits[:, :, :], digits_i[:, 1:3, :]))
                link(dve.scalar_tensor_tensor(digits[:, 0, :], digits[:, 0, :], 1.0, first[:, :], ALU.add, ALU.mult))
                link(dve.tensor_scalar(digits[:, 0, :], digits[:, 0, :], -1.0, None, ALU.add))

                def digit_turn(i, h):
                    if not isinstance(i, int):
                        dve.wait_ge(digit_used, i * 2 + h - 1)
                    for oh, d, n in ((one_hi, 0, HI), (one_lo, 1, LO)):
                        ins = dve.tensor_tensor(
                            oh[:, h, :, :],
                            c.ramp[:, None, 0:n].to_broadcast([P, UN, n]),
                            digits[:, d, bass.ds(i * 2 * UN + h * UN, UN)][:, :, None].to_broadcast([P, UN, n]),
                            ALU.is_equal)
                    ins.then_inc(digit_ready, 1)
                for h in (0, 1):
                    digit_turn(0, h)
                with dve.Fori(1, TURNS // 2) as i:
                    for h in (0, 1):
                        digit_turn(i, h)
                dve.wait_ge(digit_used, TURNS // 2 * 2 - 1)
                for oh, d, n in ((one_hi, 0, HI), (one_lo, 1, LO)):
                    ins = dve.tensor_tensor(
                        oh[:, 0, :, :], c.ramp[:, None, 0:n].to_broadcast([P, UN, n]),
                        digits[:, d, T - UN:T][:, :, None].to_broadcast([P, UN, n]), ALU.is_equal)
                ins.then_inc(digit_ready, 1)
                dve.wait_ge(counted, 1)
                link(dve.tensor_copy(hist[:, :], p_hist[0:HI, 0:LO]), "hist")
                for r in range(REL):
                    last = dve.tensor_scalar(masks[:, r, :], typf[:, :], float(r), None, ALU.is_equal)
                link(last)
                for side in (0, 1):
                    seg = same[:, side, :] if side == 0 else same[:, side, ::-1]
                    way = slice(None) if side == 0 else slice(None, None, -1)
                    end = slice(T - 1, T) if side == 0 else slice(0, 1)
                    for r in range(REL):
                        dve.tensor_tensor_scan(run[:, r, way], seg, masks[:, r, way], 0.0, ALU.mult, ALU.add)
                    link(dve.tensor_tensor_scan(through[:, way], seg, seg, 1.0, ALU.mult, ALU.mult))
                    dve.tensor_copy(ends[:, 0, :, None], run[:, :, end])
                    link(dve.tensor_copy(ends[:, 1, :, None], through[:, None, end].to_broadcast([P, REL, 1])),
                         f"ends{side}")
                    dve.wait_ge(pe_s, 2 + 2 * side)
                    link(dve.tensor_copy(endsT[:, :, :], p_ends[0:REL, 0:2 * P].rearrange("r (a p) -> r a p", a=2)))
                    if side == 0:
                        link(dve.tensor_tensor_scan(carry[:, 1:P + 1], endsT[:, 1, :], endsT[:, 0, :], 0.0,
                                                    ALU.mult, ALU.add), "carry0")
                    else:
                        link(dve.memset(carry[:, P:P + 1], 0.0))
                        link(dve.tensor_tensor_scan(carry[:, 0:P][:, ::-1], endsT[:, 1, ::-1], endsT[:, 0, ::-1],
                                                    0.0, ALU.mult, ALU.add), "carry1")
                    dve.wait_ge(pe_s, 3 + 2 * side)
                    link(dve.tensor_copy(carryC[:, :], p_carry[:, 0:REL]))
                    link(dve.tensor_tensor(tmp[:, :, :], through[:, None, :].to_broadcast([P, REL, T]),
                                           carryC[:, :, None].to_broadcast([P, REL, T]), ALU.mult))
                    link(dve.tensor_tensor(tmp[:, :, :], tmp[:, :, :], run[:, :, :], ALU.add))
                    link(dve.tensor_tensor(tmp[:, :, :], tmp[:, :, :], masks[:, :, :], ALU.mult))
                    link(dve.tensor_reduce(total[:, side, :], tmp[:, :, :].rearrange("p r t -> p t r"), AXX, ALU.add))
                link(dve.scalar_tensor_tensor(total[:, 0, :], total[:, 0, :], -1.0, total[:, 1, :], ALU.add, ALU.add))
                link(dve.reciprocal(total[:, 1, :], total[:, 0, :]), "inv")
                dve.wait_ge(ld_hist, 16)
                link(dve.tensor_tensor_scan(urow[:, 1:HI * LO + 1], onesT[0:1, 0:1].to_broadcast([1, HI * LO]),
                                            hrow[:, :], 0.0, ALU.mult, ALU.add))
                link(dve.tensor_copy(c.sum_start[:, :], urow[:, 0:T]))
                dve.wait_ge(ld_lists, 48)
                dve.tensor_copy(lists[:, 2, :, :], lists_i[:, 1, :, :])
                link(dve.tensor_copy(lists[:, 1, :, :], lists_i[:, 0, :, :]), "lists")
                dve.wait_ge(turned, 1)
                dve.tensor_copy(c.norm[:, :], p_cols[0][:, :]).then_inc(taken, 1)
                dve.wait_ge(turned, 2)
                dve.tensor_copy(c.src[:, :], p_cols[1][:, :]).then_inc(taken, 1)
                dve.wait_ge(turned, 3)
                for r in range(REL):
                    ins = dve.tensor_scalar(c.is_rel[:, :, r], p_cols[0][:, :], float(r), None, ALU.is_equal)
                ins.then_inc(taken, 1)
                dve.wait_ge(turned, 4)
                link(dve.tensor_copy(c.rank[:, :], p_cols[1][:, :]))
                dve.nop().then_inc(taken, 1)
                dve.wait_ge(turned, 5)
                dve.tensor_copy(c.inv[:, :], p_cols[0][:, :]).then_inc(taken, 1)
                dve.wait_ge(turned, 6)
                dve.tensor_copy(c.first_dst[:, :], p_cols[1][:, :]).then_inc(taken, 1)
                link(dve.tensor_copy(row_i[:, 0:T], c.rank[0:1, :]))
                link(dve.tensor_scalar(row_i[:, 0:T], row_i[:, 0:T], 7, 7, ALU.arith_shift_right,
                                       ALU.logical_shift_left))
                link(dve.tensor_copy(row[:, 0, :], row_i[:, 0:T]))
                dve.memset(row[:, 1, :], 1.0)
                link(dve.memset(row[:, 2, :], 0.0))
                link(dve.tensor_tensor(row[:, 1, 0:T - 1], row[:, 0, 1:T], row[:, 0, 0:T - 1], ALU.is_gt))
                link(dve.tensor_scalar(row[:, 2, :], row[:, 1, :], -1.0, 1.0, ALU.mult, ALU.add), "rows")
                link(dve.tensor_scalar(row[:, 3, :], c.tile_base[0:1, :], float(DUMP), None, ALU.add))
                link(dve.tensor_tensor(row[:, 4, :], row[:, 0, :], row[:, 3, :], ALU.subtract))
                link(dve.tensor_tensor(row[:, 4, :], row[:, 4, :], row[:, 1, :], ALU.mult))
                link(dve.tensor_tensor(row[:, 4, :], row[:, 4, :], row[:, 3, :], ALU.add))
                dve.tensor_copy(c.sum_row[:, 0:T], row[:, 4, :])
                dve.tensor_scalar(c.sum_row[:, T:T + 1], row[:, 0, T - 1:T], float(P), None, ALU.add)
                link(dve.tensor_scalar(c.sum_row[:, T + 1:T + 2], row[:, 0, T - 1:T], float(2 * P), None, ALU.add))
                dve.wait_ge(pe_s, 6)
                dve.tensor_tensor(c.rank[:, :], c.rank[:, :], p_row[0][:, :], ALU.subtract)
                link(dve.tensor_copy(c.goes_on[:, :], p_row[1][:, :]))
                dve.tensor_scalar(c.minus_rank[:, :], c.rank[:, :], -1.0, None, ALU.mult)
                link(dve.tensor_scalar(c.minus_inv[:, :], c.inv[:, :], -1.0, None, ALU.mult))

            @block.sync
            def _(sp):
                for j in range(3):
                    sp.dma_start(dsti[:, j, :], pmajor(A["dst"], j)).then_inc(ld_edges, 16)
                sp.dma_start(typi[:, :], pmajor(A["etype"])).then_inc(ld_edges, 16)
                sp.dma_start(lists[:, 0, :, :], blocks(A["norm"])).then_inc(ld_lists, 16)
                sp.dma_start(lists_i[:, 0, :, :], blocks(A["src"])).then_inc(ld_lists, 16)
                sp.dma_start(lists_i[:, 1, :, :], blocks(A["etype"])).then_inc(ld_lists, 16)
                sp.wait_ge(v, marks["rank"])
                sp.dma_start(pmajor(lin[0]), rank[:, :]).then_inc(st_lin, 16)
                sp.dma_start(pmajor(lin[2]), fdst[:, :]).then_inc(st_lin, 16)
                sp.wait_ge(v, marks["hist"])
                sp.dma_start(hist_d.rearrange("(h l) -> h l", l=LO), hist[:, :]).then_inc(st_hist, 16)
                sp.wait_ge(st_hist, 16)
                sp.dma_start(hrow[:, :], hist_d.rearrange("(a h) -> a h", a=1)).then_inc(ld_hist, 16)
                sp.wait_ge(v, marks["inv"])
                sp.dma_start(pmajor(lin[1]), total[:, 1, :]).then_inc(st_lin, 16)
                sp.wait_ge(st_lin, 48)
                for j in range(3):
                    sp.dma_start(lists[:, 3 + j, :, :], blocks(lin[j])).then_inc(ld_lin, 16)
                sp.wait_ge(ld_lin, 48)

            @block.tensor
            def _(pe):
                pe.wait_ge(v, marks["run"])
                pe.matmul(p_small[:, 0:1], c.upper[:, :], rank[:, T - 1:T], start=True, stop=True).then_inc(pe_s, 1)

                def count_turn(i, h, start=False, stop=False):
                    pe.wait_ge(digit_ready, i * 2 + h + 1)
                    for u in range(UN):
                        ins = pe.matmul(p_hist[0:HI, 0:LO], one_hi[:, h, u, :], one_lo[:, h, u, :],
                                        start=start and u == 0, stop=stop and u == UN - 1)
                    ins.then_inc(digit_used, 1)
                count_turn(0, 0, start=True)
                count_turn(0, 1)
                with pe.Fori(1, TURNS // 2) as i:
                    for h in (0, 1):
                        count_turn(i, h)
                count_turn(TURNS // 2, 0, stop=True)
                pe.wait_ge(digit_used, TURNS)
                pe.nop().then_inc(counted, 1)
                for side in (0, 1):
                    pe.wait_ge(v, marks[f"ends{side}"])
                    for a in (0, 1):
                        ins = pe.transpose(p_ends[0:REL, a * P:a * P + P], ends[:, a, :], c.ident[:, :])
                    ins.then_inc(pe_s, 1)
                    pe.wait_ge(v, marks[f"carry{side}"])
                    pe.transpose(p_carry[:, 0:REL], carry[:, side:side + P], c.ident[0:REL, 0:REL]).then_inc(pe_s, 1)
                pe.wait_ge(v, marks["lists"])
                for j in range(6):
                    if j == 3:
                        pe.wait_ge(ld_lin, 48)
                    if j >= 2:
                        pe.wait_ge(taken, j - 1)
                    for b in range(4):
                        ins = pe.transpose(p_cols[j % 2][:, b * BLK:b * BLK + BLK], lists[:, j, b, :],
                                           c.ident[0:BLK, 0:BLK])
                    ins.then_inc(turned, 1)
                pe.wait_ge(v, marks["rows"])
                pe.matmul(p_row[0][:, :], c.ones[0:1, :], row[:, 0, :], start=True, stop=True)
                pe.matmul(p_row[1][:, :], c.ones[0:1, :], row[:, 2, :], start=True, stop=True).then_inc(pe_s, 1)



def edge_stage(nc, c, layer, A, rows_in, width, sums):
    L = f"edge{layer}"
    with ExitStack() as ctx:
        def sb(name, shape, dt=FP32):
            return ctx.enter_context(nc.sbuf_tensor(f"{L}_{name}", shape, dt))

        def ps(name, shape):
            return ctx.enter_context(nc.psum_tensor(f"{L}_{name}", shape, FP32))

        wide = AUG if layer in (0, 3) else D
        idx = sb("idx", [P, UN], I32)
        gathered = sb("gathered", [P, UN, width])
        one_hot = sb("one_hot", [P, DEEP, 2 * P])
        acc = sb("acc", [P, AUG])
        out = sb("out", [P, UN, AUG])
        xT = sb("xT", [P, DEEP, P])
        msg = sb("msg", [P, DEEP, AUG])
        n_sum = 2 if layer in (1, 3) else DEEP
        p_sum = [ps(f"p_sum{j}", [P, 2, 256])[:, :, 0:wide] for j in range(n_sum)]
        if layer in (0, 1, 3):
            p_T = [ps(f"p_T{j}", [P, 512])[:, 0:P] for j in range(2)]
        if layer in (0, 3):
            p_z = [ps(f"p_z{j}", [P, 512])[:, 0:P] for j in range(2)]
        if layer == 0:
            raw = sb("raw", [K9, 2, HALF * P])
        if layer == 1:
            p_z = [ps(f"p_z{j}", [P, REL, P]) for j in range(2)]
            pick = sb("pick", [P, 3, 2, P])
            away = sb("away", [P, 2, 2 * P])
            pick_ring = 2
        if layer == 3:
            raw = sb("raw", [ER, 2, HALF * P])
            weight = sb("weight", [P, 2, HALF * P])
            h1 = sb("h1", [P, 2, HALF * P])
            tw = sb("tw", [P, 2, HALF * P])
            ef = sb("ef", [P, 2, HALF * P])
            p_e = [ps(f"p_e{j}", [P, HALF * P]) for j in range(2)]
        (prepared, indexed, turned, copied, product, message, hot, summed, closed, added,
         v, ended, drained, passed, passed_act, gone, picked) = sems(
            nc, ctx, L, "prepared", "indexed", "turned", "copied", "product", "message", "hot", "summed",
            "closed", "added", "dve", "ended", "drained", "passed", "passed_act", "gone", "picked")
        got, stored = c.got, c.closed_out
        if layer in (0, 3):
            raw_in = Ring(nc, f"{L}_raw_in", 2)
        if layer == 3:
            e_h1, e_relu, e_tw, e_ef, e_done = sems(nc, ctx, L, "e_h1", "e_relu", "e_tw", "e_ef", "e_done")

        PREPARED = 3

        with nc.Block() as block:
            @block.gpsimd
            def _(pool):
                pool.wait_ge(prepared, PREPARED)

                def copy_indices(slot, n):
                    pool.tensor_copy(idx[:, slot:slot + HALF], c.src[:, bass.ds(n, HALF)]).then_inc(indexed, 1)

                copy_indices(0, 0)

                def step(t):
                    if t.k % HALF == 0:
                        pool.wait_ge(indexed, t.group + 1)
                    read = {0: copied, 2: summed}.get(layer, turned)
                    wait(pool, read, t.n + 1 - UN)
                    pool.sem_inc(passed, 1)
                    pool.indirect_dma_start(gathered[:, t.slot, :], None, rows_in,
                                            bass.IndirectOffsetOnAxis(ap=idx[:, t.slot:t.slot + 1], axis=0))\
                        .then_inc(got[t.slot], 16)
                    if t.k % HALF == HALF - 1 and (t.k < HALF or not isinstance(t.i, int) or t.i < TURNS - 1):
                        nxt = Tile(t.i, t.k + 1)
                        for j in range(nxt.slot, nxt.slot + HALF):
                            wait(pool, got[j], got.base[j] + 16 * nxt.round)
                        copy_indices(nxt.slot, nxt.n)
                walk(pool, step)

            @block.sync
            def _(sp):
                def load_raw(t):
                    h = t.slot // HALF
                    cols = bass.ds(t.n * P, HALF * P)
                    sp.dma_start(raw[:, h, :], A["raw7" if layer == 0 else "raw64"][:, cols]).then_inc(raw_in[h], 16)
                    if layer == 3:
                        sp.dma_start(weight[:, h, :], A["weight"][cols].partition_broadcast(P))\
                            .then_inc(raw_in[h], 16)

                if layer == 3:
                    sp.wait_ge(c.raw64_ready, 16)
                if layer in (0, 3):
                    load_raw(Tile(0, 0))
                    load_raw(Tile(0, HALF))
                if layer == 3:
                    sp.wait_ge(e_h1, 1)
                    sp.wait_ge(e_tw, 1)
                    load_raw(Tile(0, UN))

                def step(t):
                    if layer == 0 and t.k % HALF == 1:
                        nxt = Tile(t.i, t.k - 1 + 2 * HALF)
                        if nxt.real:
                            sp.wait_ge(product, t.n + 3)
                            load_raw(nxt)
                    if layer == 3 and t.k % HALF == 2:
                        nxt = Tile(t.i, t.k - 2 + 3 * HALF)
                        if nxt.real:
                            sp.wait_ge(e_h1, t.group + 2)
                            sp.wait_ge(e_tw, t.group + 2)
                            load_raw(nxt)
                    row = sp.value_load(c.sum_row[0:1, t.col()], min_val=0, max_val=DUMP + R)
                    sp.wait_ge(closed, t.n + 1)
                    sp.dma_start(sums[bass.ds(row, P), 0:wide], out[:, t.slot, 0:wide])\
                        .then_inc(stored[t.slot], 16)
                walk(sp, step, last=2)
                sp.wait_ge(ended, 1)
                row = sp.value_load(c.sum_row[0:1, T:T + 1], min_val=0, max_val=DUMP)
                sp.dma_start(sums[bass.ds(row, P), 0:wide], acc[:, 0:wide]).then_inc(drained, 16)
                if layer == 0:
                    row = sp.value_load(c.sum_row[0:1, T + 1:T + 2], min_val=0, max_val=DUMP)
                    sp.dma_start(sums[bass.ds(row, P), :], c.zeros[:, :]).then_inc(drained, 16)
                sp.wait_ge(drained, 32 if layer == 0 else 16)
                for k in range(UN):
                    sp.wait_ge(stored[k], stored.base[k] + 16 * TURNS)

            @block.scalar
            def _(act):
                def copy_turned(t):
                    if not t.real:
                        return
                    act.wait_ge(turned, t.n + 1)
                    wait(act, product, t.n + 1 - DEEP)
                    if layer == 0:
                        wait(act, summed, t.n + 1 - DEEP)
                        act.copy(xT[:, t.j, :], p_T[t.b])
                        act.copy(msg[:, t.j, P:P + 1], c.first_dst[:, t.col()])
                        act.copy(c.src_scale[:, t.col()], gathered[:, t.slot, D:D + 1]).then_inc(copied, 1)
                    else:
                        act.copy(xT[:, t.j, :], p_T[t.b]).then_inc(copied, 1)

                def relu_message(t):
                    if not t.real:
                        return
                    act.wait_ge(product, t.n + 1)
                    wait(act, summed, t.n + 1 - DEEP)
                    act.activation(msg[:, t.j, 0:P], p_z[t.b], ACT.Relu).then_inc(message, 1)

                def edge_half(g, h):
                    act.wait_ge(e_h1, g + 1)
                    wait(act, e_done, g - 1)
                    wait(act, e_ef, g - 1)
                    act.activation(h1[:, h, :], p_e[0][:, :], ACT.Relu, bias=c.cols[:, 0:1]).then_inc(e_relu, 1)
                    act.activation(tw[:, h, :], weight[:, h, :], ACT.Sigmoid, scale=c.cols[:, 2:3],
                                   bias=c.cols[:, 3:4]).then_inc(e_tw, 1)

                def hot_scaled(t):
                    if not t.real:
                        return
                    wait(act, summed, t.n + 1 - DEEP)
                    act.sem_inc(passed_act, 1)
                    act.activation(away[:, t.slot % 2, :], c.ramp[:, :], ACT.Abs, bias=c.minus_rank[:, t.col()])\
                        .then_inc(gone, 1)
                    act.wait_ge(gone, t.n + 1)
                    act.sem_inc(passed_act, 1)
                    act.activation(one_hot[:, t.j, :], away[:, t.slot % 2, :], ACT.Relu,
                                   bias=c.inv[:, t.col()], scale=c.minus_inv[:, t.col()]).then_inc(hot, 1)

                def pick_first(t):
                    if not t.real:
                        return
                    act.wait_ge(product, t.n + 1)
                    wait(act, message, t.n - 1)
                    act.sem_inc(passed_act, 1)
                    for r in (0, 1):
                        ins = act.activation(pick[:, r, t.slot % 2, :], p_z[t.slot % 2][:, r, :], ACT.Copy,
                                             scale=c.is_rel[:, bass.ds(t.n, 1), r])
                    ins.then_inc(picked, 1)

                if layer == 0:
                    walk(act, copy_turned)
                if layer == 1:
                    def step(t):
                        copy_turned(t)
                        hot_scaled(t)
                        pick_first(t.back(2))
                    walk(act, step, 2)
                if layer == 3:
                    def step(t):
                        if t.real and t.k % HALF == 0:
                            h = t.k // HALF
                            edge_half(2 * t.i + h, h)
                        copy_turned(t)
                        relu_message(t.back(3))
                    walk(act, step, 3)

            @block.tensor
            def _(pe):
                pe.wait_ge(prepared, PREPARED)

                def turn(t):
                    if not t.real:
                        return
                    pe.wait_ge(got[t.slot], got.base[t.slot] + 16 * t.round + 16)
                    wait(pe, copied, t.n - 1)
                    pe.transpose(p_T[t.b], gathered[:, t.slot, 0:D], c.ident[:, :]).then_inc(turned, 1)

                def multiply(t):
                    if not t.real:
                        return
                    x = xT[:, t.j, :]
                    if layer == 0:
                        pe.wait_ge(raw_in[t.slot // HALF], 16 * t.round + 16)
                    if layer == 3:
                        pe.wait_ge(e_ef, 2 * t.round + t.slot // HALF + 1)
                    pe.wait_ge(copied, t.n + 1)
                    wait(pe, message, t.n - 1)
                    if layer == 0:
                        pe.matmul(p_z[t.b], x, c.w0[:, :], start=True, stop=False)
                        pe.matmul(p_z[t.b], raw[:, t.slot // HALF, bass.ts(t.slot % HALF, P)], c.we9[:, :],
                                  start=False, stop=True).then_inc(product, 1)
                    if layer == 1:
                        for half in (0, 1):
                            ins = pe.matmul(p_z[t.slot % 2][:, half * 4:half * 4 + 4, :], x, c.w1[:, half * 4:half * 4 + 4, :],
                                            start=True, stop=True)
                        ins.then_inc(product, 1)
                    if layer == 3:
                        k = t.slot % HALF
                        pe.matmul(p_z[t.b], x, c.wn1a[:, :], start=True, stop=False)
                        pe.matmul(p_z[t.b], ef[:, t.slot // HALF, k * P:k * P + P], c.wn1b[:, :],
                                  start=False, stop=False)
                        pe.matmul(p_z[t.b], c.ones[0:1, :], c.bn1[0:1, :], start=False, stop=True).then_inc(product, 1)

                def add_up(t):
                    if not t.real:
                        return
                    if layer == 2:
                        pe.wait_ge(got[t.slot], got.base[t.slot] + 16 * t.round + 16)
                        rows = gathered[:, t.slot, 0:D]
                    else:
                        pe.wait_ge(message, t.n + 1)
                        rows = pick[:, 2, t.slot % 2, :] if layer == 1 else msg[:, t.j, 0:wide]
                    pe.wait_ge(hot, t.n + 1)
                    wait(pe, added, t.n + 1 - n_sum)
                    for half in (0, 1):
                        ins = pe.matmul(p_sum[t.slot % n_sum][:, half, :], one_hot[:, t.j, half * P:half * P + P], rows,
                                        start=True, stop=True)
                    ins.then_inc(summed, 1)

                def features(t):
                    h = t.slot // HALF
                    g = 2 * t.round + h
                    pe.wait_ge(raw_in[h], 32 * t.round + 32)
                    wait(pe, e_relu, g)
                    pe.matmul(p_e[0][:, :], c.we1[:, :], raw[:, h, :], start=True, stop=True).then_inc(e_h1, 1)

                def features2(t):
                    h = t.slot // HALF
                    g = 2 * t.round + h
                    pe.wait_ge(e_relu, g + 1)
                    wait(pe, e_ef, g)
                    pe.matmul(p_e[1][:, :], c.we2[:, :], h1[:, h, :], start=True, stop=True).then_inc(e_done, 1)

                if layer == 2:
                    walk(pe, add_up)
                else:
                    def step(t):
                        turn(t)
                        if layer == 3 and t.real and t.k % HALF == 0:
                            features(t)
                        if layer == 3 and t.real and t.k % HALF == 1:
                            features2(t.back(1))
                        multiply(t.back(2))
                        add_up(t.back(4))
                    walk(pe, step, 4)

            @block.vector
            def _(dve):
                dve.memset(acc[:, :], 0.0).then_inc(prepared, 1)
                dve.memset(msg[:, :, P:P + 1], 1.0).then_inc(prepared, 1)
                dve.memset(msg[:, :, P + 1:AUG], 0.0).then_inc(prepared, 1)
                dve.wait_ge(prepared, PREPARED)

                def make_hot(t):
                    if not t.real:
                        return
                    wait(dve, summed, t.n + 1 - DEEP)
                    j = t.j
                    rank = c.rank[:, t.col()]
                    if layer in (0, 3):
                        dve.tensor_scalar(one_hot[:, j, :], c.ramp[:, :], rank, None, ALU.is_equal).then_inc(hot, 1)
                    else:
                        dve.tensor_scalar(one_hot[:, j, :], c.ramp[:, :], rank, c.src_scale[:, t.col()],
                                          ALU.is_equal, ALU.mult).then_inc(hot, 1)

                def make_message(t):
                    if not t.real:
                        return
                    if layer == 0:
                        dve.wait_ge(product, t.n + 1)
                        wait(dve, summed, t.n + 1 - DEEP)
                        dve.tensor_scalar(msg[:, t.j, 0:P], p_z[t.b], 0.0, c.norm[:, t.col()],
                                          ALU.max, ALU.mult).then_inc(message, 1)
                    if layer == 1:
                        j = t.slot % 2
                        dve.wait_ge(picked, t.n + 1)
                        for r in range(2, REL):
                            if r > 3:
                                dve.wait_ge(v, t.n * (REL - 2) + r - 3)
                            dve.scalar_tensor_tensor(pick[:, r % 2, j, :], p_z[j][:, r, :],
                                                     c.is_rel[:, bass.ds(t.n, 1), r], pick[:, r % 2, j, :],
                                                     ALU.mult, ALU.add).then_inc(v, 1)

                def join(t):
                    if not t.real:
                        return
                    j = t.slot % 2
                    dve.wait_ge(v, t.n * (REL - 2) + REL - 2)
                    wait(dve, summed, t.n - 1)
                    dve.tensor_tensor(pick[:, 2, j, :], pick[:, 0, j, :], pick[:, 1, j, :], ALU.add)\
                        .then_inc(message, 1)

                def close(t):
                    if not t.real:
                        return
                    j = t.j
                    dve.wait_ge(summed, t.n + 1)
                    wait(dve, stored[t.slot], stored.base[t.slot] + 16 * t.round)
                    wait(dve, added, t.n)
                    dve.tensor_tensor(out[:, t.slot, 0:wide], acc[:, 0:wide], p_sum[t.slot % n_sum][:, 0, :], ALU.add)\
                        .then_inc(closed, 1)
                    dve.wait_ge(closed, t.n + 1)
                    dve.scalar_tensor_tensor(acc[:, 0:wide], out[:, t.slot, 0:wide], c.goes_on[:, t.col()],
                                             p_sum[t.slot % n_sum][:, 1, :], ALU.mult, ALU.add).then_inc(added, 1)

                def weigh(t):
                    h = t.slot // HALF
                    g = 2 * t.round + h
                    dve.wait_ge(e_tw, g + 1)
                    dve.wait_ge(e_done, g + 1)
                    wait(dve, product, t.n - HALF)
                    dve.scalar_tensor_tensor(ef[:, h, :], p_e[1][:, :], c.cols[:, 1:2], tw[:, h, :],
                                             ALU.add, ALU.mult).then_inc(e_ef, 1)

                def step(t):
                    if layer == 1:
                        make_message(t.back(3))
                        close(t.back(5))
                        join(t.back(3))
                        return
                    make_hot(t.back(2) if layer != 2 else t)
                    if layer == 3 and t.real and t.k % HALF == 1:
                        weigh(t.back(1))
                    if layer == 0:
                        make_message(t.back(3))
                    close(t.back(2 if layer == 2 else 5))
                walk(dve, step, 2 if layer == 2 else 5)
                dve.wait_ge(added, T)
                dve.nop().then_inc(ended, 1)



def node_stage(nc, c, layer, rows_in, rows_out, sums):
    L = f"node{layer}"
    with ExitStack() as ctx:
        def sb(name, shape, dt=FP32):
            return ctx.enter_context(nc.sbuf_tensor(f"{L}_{name}", shape, dt))

        def ps(name, shape):
            return ctx.enter_context(nc.psum_tensor(f"{L}_{name}", shape, FP32))

        wide = AUG if layer in (0, 3) else D
        x = sb("x", [P, WIDE, D])
        sumrows = sb("sumrows", [P, WIDE, AUG])
        place = sb("place", [P, DEEP, P])
        y = sb("y", [P, UN, D])
        out = sb("out", [P, UN, D])
        stats = sb("stats", [P, UN, 6])
        moments = sb("moments", [P, UN, 2])
        std = sb("std", [P, UN])
        rstd = sb("rstd", [P, UN])
        shift = sb("shift", [P, UN])
        p_y = [ps(f"p_y{j}", [P, 512])[:, 0:P] for j in range(DEEP)]
        if layer == 0:
            xT = sb("xT", [P, DEEP, P])
            own = sb("own", [P, DEEP, P])
            p_T = [ps(f"p_T{j}", [P, 512])[:, 0:P] for j in range(2)]
            p_h = [ps(f"p_h{j}", [P, 512])[:, 0:P] for j in range(2)]
        if layer == 3:
            sT = sb("sT", [P, DEEP, P])
            deg = sb("deg", [1, DEEP, P])
            p_s = [ps(f"p_s{j}", [P, 2, 256]) for j in range(2)]
        (placed, turned, copied, product, owned, summed, made, halves, measured, rooted, inverted,
         shifted, normed, marked, passed, passed_pool, passed_dve) = sems(
            nc, ctx, L, "placed", "turned", "copied", "product", "owned", "summed", "made", "halves", "measured",
            "rooted", "inverted", "shifted", "normed", "marked", "passed", "passed_pool", "passed_dve")
        NORM_LAG = UN + 2
        x_in, sums_in, stored = c.x_in, c.sums_in, c.rows_out

        with nc.Block() as block:
            @block.sync
            def _(sp):
                def step(t):
                    if t.k % HALF == 0 and t.real:
                        wait(sp, made, t.n + HALF - WIDE)
                        sp.sem_inc(passed, 1)
                        sp.dma_start(x[:, t.slot:t.slot + HALF, :],
                                     rows_in[bass.ds(t.n * P, HALF * P), 0:D].rearrange("(k p) d -> p k d", p=P))\
                            .then_inc(x_in[t.slot // HALF], 16)
                    row = sp.value_load(c.sum_start[0:1, t.col()], min_val=0, max_val=R)
                    wait(sp, last_used, t.n + 1 - WIDE)
                    sp.dma_start(sumrows[:, t.slot, 0:wide], sums[bass.ds(row, P), 0:wide])\
                        .then_inc(sums_in[t.slot], 16)
                last_used = turned if layer == 3 else summed
                walk(sp, step, unroll=WIDE)

            @block.gpsimd
            def _(pool):
                def step(t):
                    if t.k % HALF == HALF - 1:
                        h = t.s8 // HALF
                        b = t.back(HALF - 1)
                        pool.wait_ge(normed, t.n + 1)
                        pool.sem_inc(passed_pool, 1)
                        pool.dma_start(rows_out[bass.ds(b.n * P, HALF * P), :].rearrange("(k p) d -> p k d", p=P),
                                       out[:, b.s8:b.s8 + HALF, :]).then_inc(stored[h], 16)
                walk(pool, step, unroll=WIDE)
                for h in (0, 1):
                    pool.wait_ge(stored[h], stored.base[h] + 16 * TURNS)

            @block.scalar
            def _(act):
                def copy_turned(t):
                    if not t.real:
                        return
                    j = t.j
                    act.wait_ge(turned, t.n + 1)
                    wait(act, product if layer == 0 else summed, t.n + 1 - DEEP)
                    if layer == 0:
                        act.copy(xT[:, j, :], p_T[t.b]).then_inc(copied, 1)
                    else:
                        act.copy(deg[:, j, :], p_s[t.b][0:1, 1, 0:P])
                        act.copy(sT[:, j, :], p_s[t.b][:, 0, 0:P]).then_inc(copied, 1)

                def relu_own(t):
                    if not t.real:
                        return
                    j = t.j
                    act.wait_ge(product, t.n + 1)
                    wait(act, made, t.n + 1 - DEEP)
                    act.activation(own[:, j, :], p_h[t.b], ACT.Relu).then_inc(owned, 1)

                def root(t):
                    if not t.real:
                        return
                    act.wait_ge(measured, t.n + HALF)
                    g = slice(t.s8, t.s8 + HALF)
                    act.activation(std[:, g, None], moments[:, g, 1:2], ACT.Sqrt, bias=c.eps[:, 0:1]).then_inc(rooted, 1)

                def norm(t):
                    if not t.real:
                        return
                    s = t.s8
                    if s % HALF == 0:
                        act.wait_ge(shifted, t.group + 1)
                        h = s // HALF
                        wait(act, stored[h], stored.base[h] + 16 * t.round8)
                    act.activation(out[:, s, :], y[:, s, :], ACT.Identity, bias=shift[:, s:s + 1],
                                   scale=rstd[:, s:s + 1]).then_inc(normed, 1)

                def step(t):
                    if layer in (0, 3):
                        copy_turned(t)
                    if layer == 0:
                        relu_own(t.back(2))
                    if t.k % HALF == 0:
                        root(t.back(UN))
                    norm(t.back(NORM_LAG))
                walk(act, step, UN + HALF + 1, WIDE)

            @block.tensor
            def _(pe):
                def turn(t):
                    if not t.real:
                        return
                    j = t.j
                    pe.wait_ge(x_in[t.slot // HALF], x_in.base[t.slot // HALF] + 16 * t.round + 16)
                    wait(pe, copied, t.n - 1)
                    pe.transpose(p_T[t.b], x[:, t.slot, :], c.ident[:, :]).then_inc(turned, 1)

                def own_product(t):
                    if not t.real:
                        return
                    j = t.j
                    pe.wait_ge(copied, t.n + 1)
                    wait(pe, owned, t.n - 1)
                    pe.matmul(p_h[t.b], xT[:, j, :], c.w0[:, :], start=True, stop=False)
                    pe.matmul(p_h[t.b], c.ones[0:2, :], c.root2[:, :], start=False, stop=True)\
                        .then_inc(product, 1)

                def place_sums(t):
                    if not t.real:
                        return
                    j = t.j
                    pe.wait_ge(placed, t.n + 1)
                    wait(pe, made, t.n + 1 - DEEP)
                    if layer == 0:
                        pe.wait_ge(x_in[t.slot // HALF], x_in.base[t.slot // HALF] + 16 * t.round + 16)
                        pe.matmul(p_y[j], place[:, j, :], sumrows[:, t.slot, 0:D], start=True, stop=False)
                        pe.matmul(p_y[j], c.ident[:, :], x[:, t.slot, :], start=False, stop=True)\
                            .then_inc(summed, 1)
                    if layer == 1:
                        pe.matmul(p_y[j], place[:, j, :], sumrows[:, t.slot, 0:D], start=True, stop=False)
                        pe.matmul(p_y[j], c.ones[0:1, :], c.bias1[:, :], start=False, stop=True)\
                            .then_inc(summed, 1)
                    if layer == 2:
                        pe.matmul(p_y[j], place[:, j, :], sumrows[:, t.slot, 0:D], start=True, stop=True)\
                            .then_inc(summed, 1)

                def place_turned(t):
                    if not t.real:
                        return
                    j = t.j
                    pe.wait_ge(placed, t.n + 1)
                    wait(pe, copied, t.n - 1)
                    pe.matmul(p_s[t.b][0:1, 1, 0:P], sumrows[:, t.slot, D:D + 1], place[:, j, :], start=True, stop=True)
                    pe.matmul(p_s[t.b][:, 0, 0:P], sumrows[:, t.slot, 0:D], place[:, j, :], start=True, stop=True)\
                        .then_inc(turned, 1)

                def last_product(t):
                    if not t.real:
                        return
                    j = t.j
                    pe.wait_ge(copied, t.n + 1)
                    wait(pe, made, t.n + 1 - DEEP)
                    pe.matmul(p_y[j], sT[:, j, :], c.wn2[:, :], start=True, stop=False)
                    pe.matmul(p_y[j], deg[0:1, j, :], c.bn2[:, :], start=False, stop=True).then_inc(summed, 1)

                def step(t):
                    if layer == 0:
                        turn(t)
                        own_product(t.back(1))
                        place_sums(t.back(1))
                    elif layer == 3:
                        place_turned(t.back(1))
                        last_product(t.back(2))
                    else:
                        place_sums(t.back(1))
                walk(pe, step, 2, WIDE)

            @block.vector
            def _(dve):
                def mark(t):
                    if not t.real:
                        return
                    j = t.j
                    wait(dve, turned if layer == 3 else summed, t.n + 1 - DEEP)
                    if layer == 0:
                        dve.wait_ge(sums_in[t.slot], sums_in.base[t.slot] + 16 * t.round + 16)
                        dve.tensor_tensor(c.node_of[:, t.col()], sumrows[:, t.slot, D:D + 1],
                                          c.tile_base[:, t.col()], ALU.subtract).then_inc(marked, 1)
                        dve.wait_ge(marked, t.n + 1)
                    else:
                        dve.wait_ge(sums_in[t.slot], sums_in.base[t.slot] + 16 * t.round + 16)
                    dve.tensor_scalar(place[:, j, :], c.ramp[:, 0:P], c.node_of[:, t.col()], None, ALU.is_equal)\
                        .then_inc(placed, 1)

                def make(t):
                    if not t.real:
                        return
                    j, s = t.j, t.slot
                    wait(dve, normed, t.n + 1 - UN)
                    dve.wait_ge(summed, t.n + 1)
                    if layer == 0:
                        dve.wait_ge(owned, t.n + 1)
                        ins = dve.scalar_tensor_tensor(y[:, t.s8, :], own[:, j, :], c.inv_deg[:, t.col()],
                                                       p_y[j], ALU.mult, ALU.add)
                    if layer != 0:
                        dve.wait_ge(x_in[s // HALF], x_in.base[s // HALF] + 16 * t.round + 16)
                    if layer == 1:
                        ins = dve.tensor_tensor(y[:, t.s8, :], p_y[j], x[:, s, :], ALU.add)
                    if layer == 2:
                        ins = dve.scalar_tensor_tensor(y[:, t.s8, :], p_y[j], c.scale2[:, t.col()],
                                                       x[:, s, :], ALU.mult, ALU.add)
                    if layer == 3:
                        ins = dve.scalar_tensor_tensor(y[:, t.s8, :], x[:, s, :], 2.0, p_y[j],
                                                       ALU.mult, ALU.add)
                    ins.then_inc(made, 1)

                def measure(t):
                    if not t.real:
                        return
                    dve.wait_ge(made, t.n + 1)
                    dve.bn_stats(stats[:, t.s8, :], y[:, t.s8, :]).then_inc(halves, 1)

                def spread_of(t):
                    if not t.real:
                        return
                    dve.wait_ge(halves, t.n + 1)
                    dve.sem_inc(passed_dve, 1)
                    dve.bn_aggr(moments[:, t.s8, :], stats[:, t.s8, :]).then_inc(measured, 1)

                def invert(t):
                    if not t.real:
                        return
                    g = slice(t.s8, t.s8 + HALF)
                    dve.wait_ge(rooted, t.group + 1)
                    wait(dve, normed, t.n + HALF - UN)
                    dve.reciprocal(rstd[:, g], std[:, g]).then_inc(inverted, 1)

                def shift_of(t):
                    if not t.real:
                        return
                    g = slice(t.s8, t.s8 + HALF)
                    dve.wait_ge(inverted, t.group + 1)
                    dve.scalar_tensor_tensor(shift[:, g, None], moments[:, g, 0:1], -1.0, rstd[:, g, None],
                                             ALU.mult, ALU.mult).then_inc(shifted, 1)

                def step(t):
                    mark(t)
                    make(t.back(3))
                    measure(t.back(4))
                    spread_of(t.back(5))
                    if t.k % HALF == 0:
                        invert(t.back(UN))
                    if t.k % HALF == 1:
                        shift_of(t.back(UN + 1))
                walk(dve, step, UN + 2, WIDE)



INPUTS = ["x_aug", "ints", "floats", "raw64_rows", "src", "dst", "etype", "norm", "weight", "raw7", "raw64", "degree_cols", "scale2_cols",
          "L0_gnn_W", "L0_gnn_b", "L0_gnn_We", "L0_gnn_be", "L0_gnn_root_emb", "L1_gnn_weight", "L1_gnn_bias",
          "L3_gnn_We1", "L3_gnn_be1", "L3_gnn_We2", "L3_gnn_be2", "L3_gnn_Wt", "L3_gnn_bt", "L3_gnn_Wn1",
          "L3_gnn_bn1", "L3_gnn_Wn2", "L3_gnn_bn2"]


class Constants:

    def __init__(self, nc, ctx):
        def sb(name, shape, dt=FP32):
            return ctx.enter_context(nc.sbuf_tensor(name, shape, dt))

        self.ident = sb("ident", [P, P])
        self.upper = sb("upper", [P, P])
        self.ramp = sb("ramp", [P, 2 * P])
        self.tile_base = sb("tile_base", [P, T])
        self.ones = sb("ones", [P, P])
        self.zeros = sb("zeros", [P, AUG])
        self.eps = sb("eps", [P, 1])
        self.w0 = sb("w0", [D, D])
        self.we9 = sb("we9", [K9, D])
        self.root2 = sb("root2", [2, D])
        self.w1 = sb("w1", [D, REL, D])
        self.bias1 = sb("bias1", [1, D])
        self.we1 = sb("we1", [ER, D])
        self.we2 = sb("we2", [D, D])
        self.wn1a = sb("wn1a", [D, D])
        self.wn1b = sb("wn1b", [D, D])
        self.wn2 = sb("wn2", [D, D])
        self.bn1 = sb("bn1", [1, D])
        self.bn2 = sb("bn2", [1, D])
        self.cols = sb("cols", [P, 4])
        self.inv_deg = sb("inv_deg", [P, T])
        self.scale2 = sb("scale2", [P, T])
        self.src = sb("src_cols", [P, T], I32)
        self.norm = sb("norm_cols", [P, T])
        self.is_rel = sb("is_rel", [P, T, REL])
        self.rank = sb("rank_cols", [P, T])
        self.minus_rank = sb("minus_rank", [P, T])
        self.inv = sb("inv_cols", [P, T])
        self.minus_inv = sb("minus_inv", [P, T])
        self.first_dst = sb("first_dst", [P, T])
        self.src_scale = sb("src_scale", [P, T])
        self.goes_on = sb("goes_on", [P, T])
        self.node_of = sb("node_of", [P, T])
        self.got = Ring(nc, "got", UN, T)
        self.closed_out = Ring(nc, "closed_out", UN, T)
        self.x_in = Ring(nc, "x_in", WIDE // HALF, T // HALF)
        self.sums_in = Ring(nc, "sums_in", WIDE, T)
        self.rows_out = Ring(nc, "rows_out", 2, T // HALF)
        self.sum_row = sb("sum_row", [1, T + 2], I32)
        self.sum_start = sb("sum_start", [1, T], I32)


def program(nc, A, out):
    with ExitStack() as ctx:
        c = Constants(nc, ctx)
        sums = nc.dram_tensor("sums", [DUMP + R + P, AUG], FP32).ap()
        rows = [nc.dram_tensor(f"rows{j}", [R, D], FP32).ap() for j in range(3)]
        S = {name: nc.dram_tensor(f"by_dst_{name}", A[name].shape, A[name].dtype).ap()
             for name in LISTS + ("raw7", "raw64")}
        c.raw64_ready = nc.alloc_semaphore("raw64_ready")
        constants_stage(nc, c, A)
        order_stage(nc, c, A, S)
        index_stage(nc, c, S)
        x = A["x_aug"]
        for layer in range(4):
            y = rows[layer] if layer < 3 else out
            edge_stage(nc, c, layer, S, x, AUG if layer == 0 else D, sums)
            node_stage(nc, c, layer, x, y, sums)
            for ring in (c.got, c.closed_out, c.x_in, c.sums_in, c.rows_out):
                ring.next_layer()
            x = y


def laid_out(inputs):
    import numpy as np

    def pad(a, rows, value=0):
        a = np.asarray(a)
        return np.concatenate([a, np.full((rows - a.shape[0],) + a.shape[1:], value, a.dtype)])

    def cols(a):
        return np.ascontiguousarray(a.reshape(T, P).T)

    A = {k: np.ascontiguousarray(inputs[k]) for k in INPUTS if k in inputs}
    nv = pad(np.asarray(inputs["node_vec1"]).reshape(-1), R, 1)
    x = pad(inputs["x"], R)
    A["x_aug"] = np.concatenate([x, nv[:, None], np.zeros((R, AUG - D - 1), x.dtype)], axis=1)
    A["src"] = pad(inputs["src"], R)
    dst = pad(inputs["dst"], R, R - 1)
    A["dst"] = np.concatenate([np.full(1, -1, dst.dtype), dst, np.full(1, R, dst.dtype)])
    A["etype"] = pad(inputs["edge_type_8"], R)
    A["norm"] = pad(np.asarray(inputs["edge_weight1"]).reshape(-1), R)
    A["weight"] = pad(inputs["edge_weight"], R)
    e7 = pad(inputs["edge_attr_7"], R)
    A["raw7"] = np.concatenate([e7.T, np.ones((2, R), e7.dtype)])
    A["raw64"] = np.ascontiguousarray(pad(inputs["edge_attr_64"], R).T)
    A["ints"] = np.stack([dst, A["src"], A["etype"]], axis=1)
    A["floats"] = np.concatenate([A["norm"][:, None], A["weight"][:, None], e7], axis=1)
    A["raw64_rows"] = pad(inputs["edge_attr_64"], R)
    A["degree_cols"] = cols(nv)
    A["scale2_cols"] = cols(pad(np.asarray(inputs["node_vec1_n2"]).reshape(-1), R, 1))
    return {k: A[k] for k in INPUTS}


def kernel(**inputs):
    import numpy as np
    import concourse.bacc as bacc
    from concourse.bass_utils import run_bass_kernel_spmd

    nc = bacc.Bacc("TRN2", target_bir_lowering=False, num_devices=1)
    arrays = {f"in_{k}": v for k, v in laid_out(inputs).items()}
    A = {k[3:]: nc.dram_tensor(k, v.shape, mybir.dt.from_np(v.dtype), kind="ExternalInput").ap()
         for k, v in arrays.items()}
    out = nc.dram_tensor("out_rows", (R, D), FP32, kind="ExternalOutput").ap()
    program(nc, A, out)
    r = run_bass_kernel_spmd(nc, [arrays], core_ids=[0])
    return r.results[0]["out_rows"][:N]
```

```python
from contextlib import ExitStack

import concourse.bass as bass
from concourse import mybir

FP32 = mybir.dt.float32
BF16 = mybir.dt.bfloat16
I32 = mybir.dt.int32
ALU = mybir.AluOpType
ACT = mybir.ActivationFunctionType
AXX = mybir.AxisListType.X

P = 128
N = 50000
D = 128
UN = 8
T = -(-N // (P * UN)) * UN
TURNS = T // UN
R = T * P
HALF = UN // 2
WIDE = 2 * UN
DEEP = 4
REL = 8
RAW = 7
K9 = RAW + 2
ER = 64
AUG = 132
DUMP = R + 3 * P
EPS = 1e-5
BLK = T // 4
HI = -(-T // 16)
LO = 16


def wait(e, sem, n):
    if not isinstance(n, int) or n > 0:
        e.wait_ge(sem, n)


def walk(e, step, drain=0, unroll=UN, last=1):
    turns = -(-T // unroll)
    left = T - (turns - 1) * unroll
    for i in (0, 1):
        for k in range(unroll):
            step(Tile(i, k, unroll))
    with e.Fori(2, turns - last) as i:
        for k in range(unroll):
            step(Tile(i, k, unroll))
    for i in range(turns - last, turns - 1):
        for k in range(unroll):
            step(Tile(i, k, unroll))
    for k in range(left + drain):
        step(Tile(turns - 1, k, unroll))


class Tile:

    def __init__(self, i, k, unroll=UN):
        self.i, self.k, self.unroll = i, k, unroll
        self.n = i * unroll + k
        self.slot = k % unroll
        self.round = i + k // unroll
        self.group = i * (unroll // HALF) + k // HALF
        self.j = k % DEEP
        self.b = k % 2
        self.real = not isinstance(i, int) or 0 <= self.n < T

    def back(self, d):
        return Tile(self.i, self.k - d, self.unroll)

    def col(self, width=1):
        return bass.ds(self.n, width)


def cleared(nc, handles):
    nc.clear_and_free_semaphores(handles)
    nc.all_engine_barrier()


def sems(nc, ctx, stage, *names):
    handles = [nc.alloc_semaphore(f"{stage}_{n}") for n in names]
    ctx.callback(cleared, nc, handles)
    return handles


def row_number(nc, e, place, most):
    return nc.values_load(place, engines=(e.engine,), min_val=0, max_val=most,
                          skip_runtime_bounds_check_because="the index stage writes no other rows")


class Ring:

    def __init__(self, nc, name, n, dmas=0):
        self.sems = [nc.alloc_semaphore(f"{name}{k}") for k in range(n)]
        self.uses = [len(range(k, dmas, n)) for k in range(n)]
        self.base = [0] * n

    def __getitem__(self, k):
        return self.sems[k]

    def next_layer(self):
        self.base = [b + 16 * u for b, u in zip(self.base, self.uses)]



LISTS = ("dst", "src", "etype", "norm", "weight")
CHUNK = R // 8
FIELDS = 3 + 2 + RAW + ER


def order_stage(nc, c, A, S):
    with ExitStack() as ctx:
        def sb(name, shape, dt=FP32):
            return ctx.enter_context(nc.sbuf_tensor(name, shape, dt))

        pair = sb("pair", [P, 2, T], I32)
        pairf = sb("pairf", [P, 2, T])
        falls = sb("falls", [P, T])
        worst = sb("worst", [P, 1])
        p_flag = ctx.enter_context(nc.psum_tensor("p_flag", [P, 512], FP32))
        loaded, v, voted, ready = sems(nc, ctx, "order", "loaded", "dve", "voted", "ready")
        with nc.Block() as block:
            @block.sync
            def _(sp):
                for j in (0, 1):
                    sp.dma_start(pair[:, j, :], A["dst"][j:j + R].rearrange("(p t) -> p t", p=P)).then_inc(loaded, 16)

            @block.vector
            def _(dve):
                dve.wait_ge(loaded, 32)
                dve.tensor_copy(pairf[:, :, :], pair[:, :, :]).then_inc(v, 1)
                dve.wait_ge(v, 1)
                dve.tensor_tensor(falls[:, :], pairf[:, 0, :], pairf[:, 1, :], ALU.is_gt).then_inc(v, 1)
                dve.wait_ge(v, 2)
                dve.reduce_max(worst[:, :], falls[:, :], AXX).then_inc(v, 1)
                dve.wait_ge(voted, 1)
                dve.tensor_copy(c.falls[:, :], p_flag[0:1, 0:1]).then_inc(ready, 1)

            @block.tensor
            def _(pe):
                pe.wait_ge(v, 3)
                pe.matmul(p_flag[0:1, 0:1], worst[:, :], c.ones[:, 0:1], start=True, stop=True).then_inc(voted, 1)

        keys_i = sb("keys_i", [P, CHUNK], I32)
        keys = sb("keys", [P, CHUNK])
        number = sb("number", [P, CHUNK])
        less = sb("less", [P, CHUNK])
        key_i = sb("key_i", [P, T], I32)
        key = sb("key", [P, T])
        own = sb("own", [P, T])
        part = sb("part", [P, 1])
        place = sb("place", [P, T])
        place_i = sb("place_i", [P, T], I32)
        record = sb("record", [P, 1, FIELDS], I32)
        target = sb("target", [P, 1], I32)
        (chunk_in, chunk_used, col_in, made, w, rank_done, record_in, pointed, sent, listed, small_in, sent_for) = sems(
            nc, ctx, "sort", "chunk_in", "chunk_used", "col_in", "made", "dve", "rank_done", "record_in", "pointed",
            "sent", "listed", "small_in", "sent_for")
        recs = nc.dram_tensor("recs", [R, FIELDS], I32).ap()
        parts = [("ints", 0, 3), ("floats", 3, 2 + RAW), ("raw64_rows", 5 + RAW, ER)]
        with nc.Block() as block:
            @block.sync
            def _(sp):
                unsorted = sp.value_load(c.falls[0:1, 0:1], min_val=0, max_val=P)
                with sp.If(unsorted > 0):
                    with nc.allow_non_contiguous_dma(reason="the general path for edges in any order"):
                        sp.dma_start(key_i[:, :], A["dst"][1:R + 1].rearrange("(t p) -> p t", p=P))\
                            .then_inc(col_in, 16)
                    for n in range(R // CHUNK):
                        if n:
                            sp.wait_ge(chunk_used, n)
                        sp.dma_start(keys_i[:, :], A["dst"][1 + n * CHUNK:1 + (n + 1) * CHUNK].partition_broadcast(P))\
                            .then_inc(chunk_in, 16)
                    sp.wait_ge(rank_done, 1)
                    with sp.Fori(0, T) as t:
                        sp.wait_ge(made, t + 1)
                        for name, at, n in parts:
                            sp.dma_start(record[:, 0, at:at + n], A[name][bass.ds(t * P, P), :].bitcast(I32))\
                                .then_inc(record_in, 16)
                    sp.wait_ge(made, T + 1)
                    columns = [(S["dst"][1:R + 1], 0), (S["src"], 1), (S["etype"], 2),
                               (S["norm"].bitcast(I32), 3), (S["weight"].bitcast(I32), 4)]
                    columns += [(S["raw7"][j, :].bitcast(I32), 5 + j) for j in range(RAW)]
                    columns += [(S["raw64"][j, :].bitcast(I32), 5 + RAW + j) for j in range(ER)]
                    with nc.allow_non_contiguous_dma(reason="the general path for edges in any order"):
                        for dst, j in columns:
                            sp.dma_start(dst.rearrange("(a b) -> a b", a=P),
                                         recs[:, j].rearrange("(a b) -> a b", a=P)).then_inc(listed, 16)
                    sp.dma_start(S["raw7"][RAW:K9, :], A["raw7"][RAW:K9, :]).then_inc(listed, 16)
                    for at in (0, R + 1):
                        sp.dma_start(S["dst"][at:at + 1], A["dst"][at:at + 1]).then_inc(listed, 16)
                    sp.wait_ge(listed, 16 * (FIELDS + 3))
                with sp.Else():
                    for name in LISTS:
                        sp.dma_start(S[name], A[name]).then_inc(small_in, 16)
                    sp.dma_start(S["raw7"], A["raw7"]).then_inc(small_in, 16)
                    sp.wait_ge(small_in, 16 * (len(LISTS) + 1))

            @block.vector
            def _(dve):
                unsorted = dve.value_load(c.falls[0:1, 0:1], min_val=0, max_val=P)
                with dve.If(unsorted > 0):
                    count = [0]

                    def link(ins):
                        count[0] += 1
                        ins.then_inc(w, 1)
                        dve.wait_ge(w, count[0])

                    dve.wait_ge(col_in, 16)
                    dve.wait_ge(pointed, 1)
                    dve.tensor_copy(key[:, :], key_i[:, :])
                    link(dve.memset(place[:, :], 0.0))
                    for n in range(R // CHUNK):
                        dve.wait_ge(chunk_in, 16 * n + 16)
                        link(dve.tensor_copy(keys[:, :], keys_i[:, :]))
                        if n:
                            link(dve.tensor_scalar(own[:, :], own[:, :], -float(CHUNK), None, ALU.add))
                        base = count[0]
                        with dve.Fori(0, T) as t:
                            at = bass.ds(t, 1)
                            dve.tensor_scalar(less[:, :], number[:, :], own[:, at], None, ALU.is_lt).then_inc(w, 1)
                            dve.wait_ge(w, t * 5 + base + 1)
                            dve.scalar_tensor_tensor(less[:, :], keys[:, :], key[:, at], less[:, :],
                                                     ALU.is_equal, ALU.mult).then_inc(w, 1)
                            dve.wait_ge(w, t * 5 + base + 2)
                            dve.scalar_tensor_tensor(less[:, :], keys[:, :], key[:, at], less[:, :],
                                                     ALU.is_lt, ALU.add).then_inc(w, 1)
                            dve.wait_ge(w, t * 5 + base + 3)
                            dve.reduce_sum(part[:, :], less[:, :], AXX).then_inc(w, 1)
                            dve.wait_ge(w, t * 5 + base + 4)
                            dve.tensor_tensor(place[:, at], place[:, at], part[:, :], ALU.add).then_inc(w, 1)
                            dve.wait_ge(w, t * 5 + base + 5)
                        count[0] += 5 * T
                        dve.nop().then_inc(chunk_used, 1)
                    link(dve.tensor_copy(place_i[:, :], place[:, :]))
                    dve.nop().then_inc(rank_done, 1)
                with dve.Else():
                    dve.nop()

            @block.gpsimd
            def _(pool):
                unsorted = pool.value_load(c.falls[0:1, 0:1], min_val=0, max_val=P)
                with pool.If(unsorted > 0):
                    pool.iota(number[:, :], [[1, CHUNK]], base=0, channel_multiplier=0,
                              allow_small_or_imprecise_dtypes=True)
                    pool.iota(own[:, :], [[P, T]], base=0, channel_multiplier=1,
                              allow_small_or_imprecise_dtypes=True).then_inc(pointed, 1)
                    pool.wait_ge(rank_done, 1)
                    pool.nop().then_inc(made, 1)
                    with pool.Fori(0, T) as t:
                        pool.tensor_copy(target[:, :], place_i[:, bass.ds(t, 1)]).then_inc(pointed, 1)
                        pool.wait_ge(pointed, t + 2)
                        pool.wait_ge(record_in, t * (16 * len(parts)) + 16 * len(parts))
                        pool.sem_inc(sent_for, 1)
                        pool.indirect_dma_start(recs, bass.IndirectOffsetOnAxis(ap=target[:, 0:1], axis=0),
                                                record[:, 0, :], None).then_inc(sent, 16)
                        pool.wait_ge(sent, t * 16 + 16)
                        pool.sem_inc(made, 1)
                with pool.Else():
                    pool.nop()



def constants_stage(nc, c, A):
    with ExitStack() as ctx:
        loaded, zeroed, made, split = sems(nc, ctx, "const", "loaded", "zeroed", "made", "split")

        def sb(name, shape, dt=FP32):
            return ctx.enter_context(nc.sbuf_tensor(f"const_{name}", shape, dt))

        root = sb("root", [3, 2, D])
        bias = sb("bias", [3, 3, D])
        low = sb("low", [3, 3, D], BF16)
        part = sb("part", [3, 3, 3, D])
        rows = sb("rows", [3, 3, D])
        loads = [
            (c.w0[:, :], A["L0_gnn_W"][:, :]),
            (c.we9[0:RAW, :], A["L0_gnn_We"][:, :]),
            (c.we9[RAW:RAW + 1, :], A["L0_gnn_b"]),
            (c.we9[RAW + 1:K9, :], A["L0_gnn_be"]),
            (c.w1[:, :, :], A["L1_gnn_weight"].rearrange("r f g -> f r g")),
            (c.we1[:, :], A["L3_gnn_We1"][:, :]),
            (c.we2[:, :], A["L3_gnn_We2"][:, :]),
            (c.wn1a[:, :], A["L3_gnn_Wn1"][0:D, :]),
            (c.wn1b[:, :], A["L3_gnn_Wn1"][D:2 * D, :]),
            (c.wn2[:, :], A["L3_gnn_Wn2"][:, :]),
            (root[:, 0, :], A["L0_gnn_b"][0:D].partition_broadcast(3)),
            (root[:, 1, :], A["L0_gnn_root_emb"][0, :].partition_broadcast(3)),
            (bias[:, 1, :], A["L1_gnn_bias"][0:D].partition_broadcast(3)),
            (bias[:, 2, :], A["L3_gnn_bn1"][0:D].partition_broadcast(3)),
            (c.bn2[:, :], A["L3_gnn_bn2"]),
            (c.cols[:, 0:1], A["L3_gnn_be1"]),
            (c.cols[:, 1:2], A["L3_gnn_be2"]),
            (c.cols[:, 2:3], A["L3_gnn_Wt"]),
            (c.cols[:, 3:4], A["L3_gnn_bt"]),
            (c.inv_deg[:, :], A["degree_cols"][:, :]),
            (c.scale2[:, :], A["scale2_cols"][:, :]),
        ]
        with nc.Block() as block:
            @block.sync
            def _(sp):
                for dst, src in loads:
                    sp.dma_start(dst, src).then_inc(loaded, 16)
                sp.wait_ge(loaded, 16 * len(loads))

            @block.gpsimd
            def _(pool):
                pool.memset(c.ident[:, :], 0.0).then_inc(zeroed, 1)
                pool.memset(c.upper[:, :], 1.0).then_inc(zeroed, 1)
                pool.iota(c.ramp[:, :], [[1, 2 * P]], base=0, channel_multiplier=0,
                          allow_small_or_imprecise_dtypes=True).then_inc(made, 1)
                pool.iota(c.tile_base[:, :], [[P, T]], base=0, channel_multiplier=0,
                          allow_small_or_imprecise_dtypes=True).then_inc(made, 1)
                pool.wait_ge(zeroed, 2)
                pool.affine_select(out=c.ident[:, :], in_=c.ident[:, :], compare_op=ALU.not_equal, fill=1.0,
                                   base=0, pattern=[[-1, P]], channel_multiplier=1).then_inc(made, 1)
                pool.affine_select(out=c.upper[:, :], in_=c.upper[:, :], compare_op=ALU.is_gt, fill=0.0,
                                   base=0, pattern=[[1, P]], channel_multiplier=-1).then_inc(made, 1)
                pool.wait_ge(made, 4)

            @block.vector
            def _(dve):
                dve.memset(c.ones[:, :], 1.0)
                dve.memset(c.zeros[:, :], 0.0)
                dve.memset(c.eps[:, :], EPS)
                dve.wait_ge(loaded, 16 * len(loads))
                dve.reciprocal(c.inv_deg[:, :], c.inv_deg[:, :])
                dve.tensor_tensor(bias[:, 0, :], root[:, 0, :], root[:, 1, :], ALU.add).then_inc(split, 1)
                steps = 1
                for k in range(3):
                    dve.wait_ge(split, steps)
                    dve.tensor_copy(low[:, :, :], bias[:, :, :]).then_inc(split, 1)
                    dve.wait_ge(split, steps + 1)
                    dve.tensor_copy(part[:, k, :, :], low[:, :, :]).then_inc(split, 1)
                    dve.wait_ge(split, steps + 2)
                    dve.tensor_tensor(bias[:, :, :], bias[:, :, :], part[:, k, :, :], ALU.subtract).then_inc(split, 1)
                    steps += 3
                dve.wait_ge(split, steps)
                dve.wait_ge(made, 4)
                dve.tensor_scalar(rows[:, :, :], part[:, 0, :, :], c.ident[0:3, 0:1], None, ALU.mult).then_inc(split, 1)
                for k in (1, 2):
                    dve.wait_ge(split, steps + k)
                    dve.scalar_tensor_tensor(rows[:, :, :], part[:, k, :, :], c.ident[0:3, k:k + 1], rows[:, :, :],
                                             ALU.mult, ALU.add).then_inc(split, 1)
                dve.wait_ge(split, steps + 3)
                dve.tensor_copy(c.bias3[:, :, :], rows[:, :, :])
                dve.memset(c.ones3[:, :], 1.0)


def index_stage(nc, c, A, raw64_in):
    with ExitStack() as ctx:
        def sb(name, shape, dt=FP32):
            return ctx.enter_context(nc.sbuf_tensor(name, shape, dt))

        def ps(name, shape):
            return ctx.enter_context(nc.psum_tensor(name, shape, FP32))

        dsti = sb("dsti", [P, 3, T], I32)
        typi = sb("typi", [P, T], I32)
        dstf = sb("dstf", [P, 3, T])
        typf = sb("typf", [P, T])
        same = sb("same", [P, 2, T])
        first = sb("first", [P, T])
        onesT = sb("onesT", [P, T])
        rank = sb("rank", [P, T])
        fdst = sb("fdst", [P, T])
        masks = sb("masks", [P, REL, T])
        run = sb("run", [P, REL, T])
        tmp = sb("tmp", [P, REL, T])
        through = sb("through", [P, T])
        total = sb("total", [P, 2, T])
        ends = sb("ends", [P, 2, REL])
        endsT = sb("endsT", [REL, 2, P])
        carry = sb("carry", [REL, P + 1])
        carryC = sb("carryC", [P, REL])
        before = sb("before", [P, 1])
        digits_i = sb("digits_i", [P, 3, T], I32)
        digits = sb("digits", [P, 2, T])
        one_hi = sb("one_hi", [P, 2, UN, HI], BF16)
        one_lo = sb("one_lo", [P, 2, UN, LO], BF16)
        hist = sb("hist", [HI, LO])
        hrow = sb("hrow", [1, HI * LO])
        urow = sb("urow", [1, HI * LO + 1])
        lists_i = sb("lists_i", [BLK, 2, 4, P], I32)
        lists = sb("lists", [BLK, 6, 4, P])
        row = sb("row", [1, 6, T])
        row_i = sb("row_i", [1, T + 1], I32)
        p_small = ps("p_small", [P, 512])
        p_ends = ps("p_ends", [P, 512])
        p_carry = ps("p_carry", [P, 512])
        p_hist = ps("p_hist", [P, 512])
        p_cols = [ps(f"p_cols{j}", [P, T]) for j in range(2)]
        p_row = [ps(f"p_row{j}", [P, T]) for j in range(2)]
        (ld_edges, ld_lists, v, pe_s, st_lin, ld_lin, ld_hist, st_hist, digit_ready, digit_used, counted,
         turned, taken) = sems(
            nc, ctx, "index", "edges", "lists", "dve", "pe", "stored", "relisted", "hist_in", "hist_out",
            "digit_ready", "digit_used", "counted", "turned", "taken")
        lin = [nc.dram_tensor(f"lin{j}", [R], FP32).ap() for j in range(3)]
        hist_d = nc.dram_tensor("hist_d", [HI * LO], FP32).ap()

        def pmajor(a, off=0):
            return a[off:off + R].rearrange("(p t) -> p t", p=P)

        def blocks(a, off=0):
            return a[off:off + R].rearrange("(b t p) -> t b p", b=4, p=P)

        marks = {}
        with nc.Block() as block:
            @block.vector
            def _(dve):
                count = [0]

                def link(ins, name=None):
                    count[0] += 1
                    ins.then_inc(v, 1)
                    dve.wait_ge(v, count[0])
                    if name:
                        marks[name] = count[0]

                dve.memset(onesT[:, :], 1.0)
                dve.memset(urow[:, 0:1], 0.0)
                link(dve.memset(carry[:, :], 0.0))
                dve.wait_ge(ld_edges, 64)
                dve.tensor_copy(typf[:, :], typi[:, :])
                link(dve.tensor_copy(dstf[:, :, :], dsti[:, :, :]))
                for side in (0, 1):
                    last = dve.tensor_tensor(same[:, side, :], dstf[:, 1, :], dstf[:, 2 * side, :], ALU.is_equal)
                link(last)
                link(dve.tensor_scalar(first[:, :], same[:, 0, :], -1.0, 1.0, ALU.mult, ALU.add))
                dve.tensor_tensor(fdst[:, :], first[:, :], dstf[:, 1, :], ALU.mult)
                link(dve.tensor_tensor_scan(rank[:, :], onesT[:, :], first[:, :], 0.0, ALU.mult, ALU.add), "run")
                dve.wait_ge(pe_s, 1)
                link(dve.tensor_copy(before[:, :], p_small[:, 0:1]))
                link(dve.tensor_scalar(rank[:, :], rank[:, :], before[:, 0:1], -1.0, ALU.add, ALU.add), "rank")
                link(dve.tensor_scalar(digits_i[:, 0, :], dsti[:, 1, :], 7, None, ALU.arith_shift_right))
                dve.tensor_scalar(digits_i[:, 1, :], digits_i[:, 0, :], 4, None, ALU.arith_shift_right)
                link(dve.tensor_scalar(digits_i[:, 2, :], digits_i[:, 0, :], 15, None, ALU.bitwise_and))
                link(dve.tensor_copy(digits[:, :, :], digits_i[:, 1:3, :]))
                link(dve.scalar_tensor_tensor(digits[:, 0, :], digits[:, 0, :], 1.0, first[:, :], ALU.add, ALU.mult))
                link(dve.tensor_scalar(digits[:, 0, :], digits[:, 0, :], -1.0, None, ALU.add))

                def digit_turn(i, h):
                    if not isinstance(i, int):
                        dve.wait_ge(digit_used, i * 2 + h - 1)
                    for oh, d, n in ((one_hi, 0, HI), (one_lo, 1, LO)):
                        ins = dve.tensor_tensor(
                            oh[:, h, :, :],
                            c.ramp[:, None, 0:n].to_broadcast([P, UN, n]),
                            digits[:, d, bass.ds(i * 2 * UN + h * UN, UN)][:, :, None].to_broadcast([P, UN, n]),
                            ALU.is_equal)
                    ins.then_inc(digit_ready, 1)
                for h in (0, 1):
                    digit_turn(0, h)
                with dve.Fori(1, TURNS // 2) as i:
                    for h in (0, 1):
                        digit_turn(i, h)
                dve.wait_ge(digit_used, TURNS // 2 * 2 - 1)
                for oh, d, n in ((one_hi, 0, HI), (one_lo, 1, LO)):
                    ins = dve.tensor_tensor(
                        oh[:, 0, :, :], c.ramp[:, None, 0:n].to_broadcast([P, UN, n]),
                        digits[:, d, T - UN:T][:, :, None].to_broadcast([P, UN, n]), ALU.is_equal)
                ins.then_inc(digit_ready, 1)
                dve.wait_ge(counted, 1)
                link(dve.tensor_copy(hist[:, :], p_hist[0:HI, 0:LO]), "hist")
                for r in range(REL):
                    last = dve.tensor_scalar(masks[:, r, :], typf[:, :], float(r), None, ALU.is_equal)
                link(last)
                for side in (0, 1):
                    seg = same[:, side, :] if side == 0 else same[:, side, ::-1]
                    way = slice(None) if side == 0 else slice(None, None, -1)
                    end = slice(T - 1, T) if side == 0 else slice(0, 1)
                    for r in range(REL):
                        dve.tensor_tensor_scan(run[:, r, way], seg, masks[:, r, way], 0.0, ALU.mult, ALU.add)
                    link(dve.tensor_tensor_scan(through[:, way], seg, seg, 1.0, ALU.mult, ALU.mult))
                    dve.tensor_copy(ends[:, 0, :, None], run[:, :, end])
                    link(dve.tensor_copy(ends[:, 1, :, None], through[:, None, end].to_broadcast([P, REL, 1])),
                         f"ends{side}")
                    dve.wait_ge(pe_s, 2 + 2 * side)
                    link(dve.tensor_copy(endsT[:, :, :], p_ends[0:REL, 0:2 * P].rearrange("r (a p) -> r a p", a=2)))
                    if side == 0:
                        link(dve.tensor_tensor_scan(carry[:, 1:P + 1], endsT[:, 1, :], endsT[:, 0, :], 0.0,
                                                    ALU.mult, ALU.add), "carry0")
                    else:
                        link(dve.memset(carry[:, P:P + 1], 0.0))
                        link(dve.tensor_tensor_scan(carry[:, 0:P][:, ::-1], endsT[:, 1, ::-1], endsT[:, 0, ::-1],
                                                    0.0, ALU.mult, ALU.add), "carry1")
                    dve.wait_ge(pe_s, 3 + 2 * side)
                    link(dve.tensor_copy(carryC[:, :], p_carry[:, 0:REL]))
                    link(dve.tensor_tensor(tmp[:, :, :], through[:, None, :].to_broadcast([P, REL, T]),
                                           carryC[:, :, None].to_broadcast([P, REL, T]), ALU.mult))
                    link(dve.tensor_tensor(tmp[:, :, :], tmp[:, :, :], run[:, :, :], ALU.add))
                    link(dve.tensor_tensor(tmp[:, :, :], tmp[:, :, :], masks[:, :, :], ALU.mult))
                    link(dve.tensor_reduce(total[:, side, :], tmp[:, :, :].rearrange("p r t -> p t r"), AXX, ALU.add))
                link(dve.scalar_tensor_tensor(total[:, 0, :], total[:, 0, :], -1.0, total[:, 1, :], ALU.add, ALU.add))
                link(dve.reciprocal(total[:, 1, :], total[:, 0, :]), "inv")
                dve.wait_ge(ld_hist, 16)
                link(dve.tensor_tensor_scan(urow[:, 1:HI * LO + 1], onesT[0:1, 0:1].to_broadcast([1, HI * LO]),
                                            hrow[:, :], 0.0, ALU.mult, ALU.add))
                link(dve.tensor_copy(c.sum_start[:, :], urow[:, 0:T]))
                dve.wait_ge(ld_lists, 48)
                dve.tensor_copy(lists[:, 2, :, :], lists_i[:, 1, :, :])
                link(dve.tensor_copy(lists[:, 1, :, :], lists_i[:, 0, :, :]), "lists")
                dve.wait_ge(turned, 1)
                dve.tensor_copy(c.norm[:, :], p_cols[0][:, :]).then_inc(taken, 1)
                dve.wait_ge(turned, 2)
                dve.tensor_copy(c.src[:, :], p_cols[1][:, :]).then_inc(taken, 1)
                dve.wait_ge(turned, 3)
                for r in range(REL):
                    ins = dve.tensor_scalar(c.is_rel[:, :, r], p_cols[0][:, :], float(r), None, ALU.is_equal)
                ins.then_inc(taken, 1)
                dve.wait_ge(turned, 4)
                link(dve.tensor_copy(c.rank[:, :], p_cols[1][:, :]))
                dve.nop().then_inc(taken, 1)
                dve.wait_ge(turned, 5)
                dve.tensor_copy(c.inv[:, :], p_cols[0][:, :]).then_inc(taken, 1)
                dve.wait_ge(turned, 6)
                dve.tensor_copy(c.first_dst[:, :], p_cols[1][:, :]).then_inc(taken, 1)
                link(dve.tensor_copy(row_i[:, 0:T], c.rank[0:1, :]))
                link(dve.tensor_scalar(row_i[:, 0:T], row_i[:, 0:T], 7, 7, ALU.arith_shift_right,
                                       ALU.logical_shift_left))
                link(dve.tensor_copy(row[:, 0, :], row_i[:, 0:T]))
                dve.memset(row[:, 1, :], 1.0)
                link(dve.memset(row[:, 2, :], 0.0))
                link(dve.tensor_tensor(row[:, 1, 0:T - 1], row[:, 0, 1:T], row[:, 0, 0:T - 1], ALU.is_gt))
                link(dve.tensor_scalar(row[:, 2, :], row[:, 1, :], -1.0, 1.0, ALU.mult, ALU.add), "rows")
                link(dve.tensor_scalar(row[:, 3, :], c.tile_base[0:1, :], float(DUMP), None, ALU.add))
                link(dve.tensor_tensor(row[:, 4, :], row[:, 0, :], row[:, 3, :], ALU.subtract))
                link(dve.tensor_tensor(row[:, 4, :], row[:, 4, :], row[:, 1, :], ALU.mult))
                link(dve.tensor_tensor(row[:, 4, :], row[:, 4, :], row[:, 3, :], ALU.add))
                dve.tensor_copy(c.sum_row[:, 0:T], row[:, 4, :])
                dve.tensor_scalar(c.sum_row[:, T:T + 1], row[:, 0, T - 1:T], float(P), None, ALU.add)
                link(dve.tensor_scalar(c.sum_row[:, T + 1:T + 2], row[:, 0, T - 1:T], float(2 * P), None, ALU.add))
                dve.wait_ge(pe_s, 6)
                dve.tensor_tensor(c.rank[:, :], c.rank[:, :], p_row[0][:, :], ALU.subtract)
                link(dve.tensor_copy(c.goes_on[:, :], p_row[1][:, :]))
                dve.tensor_scalar(c.minus_rank[:, :], c.rank[:, :], -1.0, None, ALU.mult)
                link(dve.tensor_scalar(c.minus_inv[:, :], c.inv[:, :], -1.0, None, ALU.mult))

            @block.sync
            def _(sp):
                for j in range(3):
                    sp.dma_start(dsti[:, j, :], pmajor(A["dst"], j)).then_inc(ld_edges, 16)
                sp.dma_start(typi[:, :], pmajor(A["etype"])).then_inc(ld_edges, 16)
                sp.dma_start(lists[:, 0, :, :], blocks(A["norm"])).then_inc(ld_lists, 16)
                sp.dma_start(lists_i[:, 0, :, :], blocks(A["src"])).then_inc(ld_lists, 16)
                sp.dma_start(lists_i[:, 1, :, :], blocks(A["etype"])).then_inc(ld_lists, 16)
                sp.wait_ge(v, marks["rank"])
                sp.dma_start(pmajor(lin[0]), rank[:, :]).then_inc(st_lin, 16)
                sp.dma_start(pmajor(lin[2]), fdst[:, :]).then_inc(st_lin, 16)
                sp.wait_ge(ld_lists, 48)
                sp.wait_ge(st_lin, 32)
                unsorted = sp.value_load(c.falls[0:1, 0:1], min_val=0, max_val=P)
                with sp.If(unsorted > 0):
                    sp.sem_inc(c.raw64_ready, 16)
                with sp.Else():
                    sp.dma_start(A["raw64"], raw64_in).then_inc(c.raw64_ready, 16)
                sp.wait_ge(v, marks["hist"])
                sp.dma_start(hist_d.rearrange("(h l) -> h l", l=LO), hist[:, :]).then_inc(st_hist, 16)
                sp.wait_ge(st_hist, 16)
                sp.dma_start(hrow[:, :], hist_d.rearrange("(a h) -> a h", a=1)).then_inc(ld_hist, 16)
                sp.wait_ge(v, marks["inv"])
                sp.dma_start(pmajor(lin[1]), total[:, 1, :]).then_inc(st_lin, 16)
                sp.wait_ge(st_lin, 48)
                for j in range(3):
                    sp.dma_start(lists[:, 3 + j, :, :], blocks(lin[j])).then_inc(ld_lin, 16)
                sp.wait_ge(ld_lin, 48)

            @block.tensor
            def _(pe):
                pe.wait_ge(v, marks["run"])
                pe.matmul(p_small[:, 0:1], c.upper[:, :], rank[:, T - 1:T], start=True, stop=True).then_inc(pe_s, 1)

                def count_turn(i, h, start=False, stop=False):
                    pe.wait_ge(digit_ready, i * 2 + h + 1)
                    for u in range(UN):
                        ins = pe.matmul(p_hist[0:HI, 0:LO], one_hi[:, h, u, :], one_lo[:, h, u, :],
                                        start=start and u == 0, stop=stop and u == UN - 1)
                    ins.then_inc(digit_used, 1)
                count_turn(0, 0, start=True)
                count_turn(0, 1)
                with pe.Fori(1, TURNS // 2) as i:
                    for h in (0, 1):
                        count_turn(i, h)
                count_turn(TURNS // 2, 0, stop=True)
                pe.wait_ge(digit_used, TURNS)
                pe.nop().then_inc(counted, 1)
                for side in (0, 1):
                    pe.wait_ge(v, marks[f"ends{side}"])
                    for a in (0, 1):
                        ins = pe.transpose(p_ends[0:REL, a * P:a * P + P], ends[:, a, :], c.ident[:, :])
                    ins.then_inc(pe_s, 1)
                    pe.wait_ge(v, marks[f"carry{side}"])
                    pe.transpose(p_carry[:, 0:REL], carry[:, side:side + P], c.ident[0:REL, 0:REL]).then_inc(pe_s, 1)
                pe.wait_ge(v, marks["lists"])
                for j in range(6):
                    if j == 3:
                        pe.wait_ge(ld_lin, 48)
                    if j >= 2:
                        pe.wait_ge(taken, j - 1)
                    for b in range(4):
                        ins = pe.transpose(p_cols[j % 2][:, b * BLK:b * BLK + BLK], lists[:, j, b, :],
                                           c.ident[0:BLK, 0:BLK])
                    ins.then_inc(turned, 1)
                pe.wait_ge(v, marks["rows"])
                pe.matmul(p_row[0][:, :], c.ones[0:1, :], row[:, 0, :], start=True, stop=True)
                pe.matmul(p_row[1][:, :], c.ones[0:1, :], row[:, 2, :], start=True, stop=True).then_inc(pe_s, 1)



def edge_stage(nc, c, layer, A, rows_in, width, sums):
    L = f"edge{layer}"
    with ExitStack() as ctx:
        def sb(name, shape, dt=FP32):
            return ctx.enter_context(nc.sbuf_tensor(f"{L}_{name}", shape, dt))

        def ps(name, shape):
            return ctx.enter_context(nc.psum_tensor(f"{L}_{name}", shape, FP32))

        wide = AUG if layer in (0, 3) else D
        idx = sb("idx", [P, UN], I32)
        gathered = sb("gathered", [P, UN, width])
        one_hot = sb("one_hot", [P, DEEP, 2 * P])
        acc = sb("acc", [P, AUG])
        out = sb("out", [P, UN, AUG])
        xT = sb("xT", [P, DEEP, P])
        msg = sb("msg", [P, DEEP, AUG])
        n_sum = 2 if layer in (1, 3) else DEEP
        p_sum = [ps(f"p_sum{j}", [P, 2, 256])[:, :, 0:wide] for j in range(n_sum)]
        if layer in (0, 1, 3):
            p_T = [ps(f"p_T{j}", [P, 512])[:, 0:P] for j in range(2)]
        if layer in (0, 3):
            p_z = [ps(f"p_z{j}", [P, 512])[:, 0:P] for j in range(2)]
        if layer == 0:
            raw = sb("raw", [K9, 2, HALF * P])
        if layer == 1:
            p_z = [ps(f"p_z{j}", [P, REL, P]) for j in range(2)]
            pick = sb("pick", [P, 2, 2, P])
            away = sb("away", [P, 2, 2 * P])
        if layer == 3:
            raw = sb("raw", [ER, 2, HALF * P])
            weight = sb("weight", [P, 2, HALF * P])
            h1 = sb("h1", [P, 2, HALF * P])
            tw = sb("tw", [P, 2, HALF * P])
            ef = sb("ef", [P, 2, HALF * P])
            p_e = [ps(f"p_e{j}", [P, HALF * P]) for j in range(2)]
        (prepared, indexed, turned, copied, product, message, hot, summed, closed, added,
         v, ended, drained, passed, passed_act, gone, picked) = sems(
            nc, ctx, L, "prepared", "indexed", "turned", "copied", "product", "message", "hot", "summed",
            "closed", "added", "dve", "ended", "drained", "passed", "passed_act", "gone", "picked")
        got, stored = c.got, c.closed_out
        if layer in (0, 3):
            raw_in = Ring(nc, f"{L}_raw_in", 2)
        if layer == 3:
            e_h1, e_relu, e_tw, e_ef, e_done = sems(nc, ctx, L, "e_h1", "e_relu", "e_tw", "e_ef", "e_done")

        PREPARED = 3

        with nc.Block() as block:
            def copy_indices(e, copy, t):
                if not t.real:
                    return
                for j in range(t.slot, t.slot + HALF):
                    wait(e, got[j], got.base[j] + 16 * t.round)
                copy(idx[:, t.slot:t.slot + HALF], c.src[:, bass.ds(t.n, HALF)]).then_inc(indexed, 1)

            @block.gpsimd
            def _(pool):
                pool.wait_ge(prepared, PREPARED)

                if layer != 2:
                    copy_indices(pool, pool.tensor_copy, Tile(0, 0))

                def step(t):
                    if t.k % HALF == 0:
                        pool.wait_ge(indexed, t.group + 1)
                    read = {0: copied, 2: summed}.get(layer, turned)
                    wait(pool, read, t.n + 1 - UN)
                    pool.sem_inc(passed, 1)
                    pool.indirect_dma_start(gathered[:, t.slot, :], None, rows_in,
                                            bass.IndirectOffsetOnAxis(ap=idx[:, t.slot:t.slot + 1], axis=0))\
                        .then_inc(got[t.slot], 16)
                    if layer != 2 and t.k % HALF == HALF - 1:
                        copy_indices(pool, pool.tensor_copy, t.back(-1))
                walk(pool, step)

            @block.sync
            def _(sp):
                def load_raw(t):
                    h = t.slot // HALF
                    cols = bass.ds(t.n * P, HALF * P)
                    sp.dma_start(raw[:, h, :], A["raw7" if layer == 0 else "raw64"][:, cols]).then_inc(raw_in[h], 16)
                    if layer == 3:
                        sp.dma_start(weight[:, h, :], A["weight"][cols].partition_broadcast(P))\
                            .then_inc(raw_in[h], 16)

                if layer == 3:
                    sp.wait_ge(c.raw64_ready, 16)
                if layer in (0, 3):
                    load_raw(Tile(0, 0))
                    load_raw(Tile(0, HALF))
                if layer == 3:
                    sp.wait_ge(e_h1, 1)
                    sp.wait_ge(e_tw, 1)
                    load_raw(Tile(0, UN))

                def step(t):
                    if layer == 0 and t.k % HALF == 1:
                        nxt = Tile(t.i, t.k - 1 + 2 * HALF)
                        if nxt.real:
                            sp.wait_ge(product, t.n + 3)
                            load_raw(nxt)
                    if layer == 3 and t.k % HALF == 0:
                        nxt = Tile(t.i, t.k + 3 * HALF)
                        if nxt.real:
                            sp.wait_ge(e_h1, t.group + 2)
                            sp.wait_ge(e_tw, t.group + 2)
                            load_raw(nxt)
                    row = row_number(nc, sp, c.sum_row[0:1, t.col()], DUMP + R)
                    sp.wait_ge(closed, t.n + 1)
                    sp.dma_start(sums[bass.ds(row, P), 0:wide], out[:, t.slot, 0:wide])\
                        .then_inc(stored[t.slot], 16)
                walk(sp, step, last=2)
                sp.wait_ge(ended, 1)
                row = sp.value_load(c.sum_row[0:1, T:T + 1], min_val=0, max_val=DUMP)
                sp.dma_start(sums[bass.ds(row, P), 0:wide], acc[:, 0:wide]).then_inc(drained, 16)
                if layer == 0:
                    row = sp.value_load(c.sum_row[0:1, T + 1:T + 2], min_val=0, max_val=DUMP)
                    sp.dma_start(sums[bass.ds(row, P), :], c.zeros[:, :]).then_inc(drained, 16)
                sp.wait_ge(drained, 32 if layer == 0 else 16)
                for k in range(UN):
                    sp.wait_ge(stored[k], stored.base[k] + 16 * TURNS)

            @block.scalar
            def _(act):
                def copy_turned(t):
                    if not t.real:
                        return
                    act.wait_ge(turned, t.n + 1)
                    wait(act, product, (t.n + 1 - DEEP) * (2 if layer == 1 else 1))
                    if layer == 0:
                        wait(act, summed, t.n + 1 - DEEP)
                        act.copy(xT[:, t.j, :], p_T[t.b])
                        act.copy(msg[:, t.j, P:P + 1], c.first_dst[:, t.col()])
                        act.copy(c.src_scale[:, t.col()], gathered[:, t.slot, D:D + 1]).then_inc(copied, 1)
                    else:
                        act.copy(xT[:, t.j, :], p_T[t.b]).then_inc(copied, 1)

                def relu_message(t):
                    if not t.real:
                        return
                    act.wait_ge(product, t.n + 1)
                    wait(act, summed, t.n + 1 - DEEP)
                    act.activation(msg[:, t.j, 0:P], p_z[t.b], ACT.Relu).then_inc(message, 1)

                def edge_half(t):
                    if not t.real:
                        return
                    g, h = t.group, t.slot // HALF
                    act.wait_ge(e_h1, g + 1)
                    wait(act, e_done, g - 1)
                    wait(act, e_ef, g - 1)
                    act.activation(h1[:, h, :], p_e[0][:, :], ACT.Relu, bias=c.cols[:, 0:1]).then_inc(e_relu, 1)
                    act.activation(tw[:, h, :], weight[:, h, :], ACT.Sigmoid, scale=c.cols[:, 2:3],
                                   bias=c.cols[:, 3:4]).then_inc(e_tw, 1)

                def hot_scaled(t):
                    if not t.real:
                        return
                    wait(act, summed, t.n + 1 - DEEP)
                    act.sem_inc(passed_act, 1)
                    act.activation(away[:, t.b, :], c.ramp[:, :], ACT.Abs, bias=c.minus_rank[:, t.col()])\
                        .then_inc(gone, 1)
                    act.wait_ge(gone, t.n + 1)
                    act.sem_inc(passed_act, 1)
                    act.activation(one_hot[:, t.j, :], away[:, t.b, :], ACT.Relu,
                                   bias=c.inv[:, t.col()], scale=c.minus_inv[:, t.col()]).then_inc(hot, 1)

                def pick_first(t):
                    if not t.real:
                        return
                    act.wait_ge(product, 2 * t.n + 1)
                    wait(act, message, t.n - 1)
                    act.sem_inc(passed_act, 1)
                    for r in (0, 1):
                        ins = act.activation(pick[:, r, t.b, :], p_z[t.b][:, r, :], ACT.Copy,
                                             scale=c.is_rel[:, bass.ds(t.n, 1), r])
                    ins.then_inc(picked, 1)

                if layer == 0:
                    walk(act, copy_turned)
                if layer == 2:
                    def step(t):
                        if t.k % HALF == 0:
                            copy_indices(act, act.copy, t)
                    walk(act, step)
                if layer == 1:
                    def step(t):
                        copy_turned(t)
                        pick_first(t.back(2))
                        hot_scaled(t.back(2))
                    walk(act, step, 2)
                if layer == 3:
                    def step(t):
                        if t.k % HALF == 2:
                            edge_half(t.back(-2))
                        copy_turned(t)
                        relu_message(t.back(3))
                    edge_half(Tile(0, 0))
                    walk(act, step, 3)

            @block.tensor
            def _(pe):
                pe.wait_ge(prepared, PREPARED)

                def turn(t):
                    if not t.real:
                        return
                    pe.wait_ge(got[t.slot], got.base[t.slot] + 16 * t.round + 16)
                    wait(pe, copied, t.n - 1)
                    pe.transpose(p_T[t.b], gathered[:, t.slot, 0:D], c.ident[:, :]).then_inc(turned, 1)

                def multiply(t):
                    if not t.real:
                        return
                    x = xT[:, t.j, :]
                    if layer == 0:
                        pe.wait_ge(raw_in[t.slot // HALF], 16 * t.round + 16)
                    if layer == 3:
                        pe.wait_ge(e_ef, 2 * t.round + t.slot // HALF + 1)
                    pe.wait_ge(copied, t.n + 1)
                    if layer != 1:
                        wait(pe, message, t.n - 1)
                    if layer == 0:
                        pe.matmul(p_z[t.b], x, c.w0[:, :], start=True, stop=False)
                        pe.matmul(p_z[t.b], raw[:, t.slot // HALF, bass.ts(t.slot % HALF, P)], c.we9[:, :],
                                  start=False, stop=True).then_inc(product, 1)
                    if layer == 1:
                        for half in (0, 1):
                            wait(pe, v, (t.n - 2) * (REL - 2) + (2, REL - 2)[half])
                            rels = slice(half * REL // 2, (half + 1) * REL // 2)
                            ins = pe.matmul(p_z[t.b][:, rels, :], x, c.w1[:, rels, :], start=True, stop=True)
                            ins.then_inc(product, 1)
                    if layer == 3:
                        k = t.slot % HALF
                        pe.matmul(p_z[t.b], x, c.wn1a[:, :], start=True, stop=False)
                        pe.matmul(p_z[t.b], ef[:, t.slot // HALF, k * P:k * P + P], c.wn1b[:, :],
                                  start=False, stop=False)
                        pe.matmul(p_z[t.b], c.ones3[:, :], c.bias3[:, 2, :], start=False, stop=True)\
                            .then_inc(product, 1)

                def add_up(t):
                    if not t.real:
                        return
                    if layer == 2:
                        pe.wait_ge(got[t.slot], got.base[t.slot] + 16 * t.round + 16)
                        rows = gathered[:, t.slot, 0:D]
                    else:
                        pe.wait_ge(message, t.n + 1)
                        rows = msg[:, t.j, 0:wide]
                    pe.wait_ge(hot, t.n + 1)
                    wait(pe, added, t.n + 1 - n_sum)
                    for half in (0, 1):
                        ins = pe.matmul(p_sum[t.slot % n_sum][:, half, :], one_hot[:, t.j, half * P:half * P + P], rows,
                                        start=True, stop=True)
                    ins.then_inc(summed, 1)

                def features(t):
                    if not t.real:
                        return
                    g, h = t.group, t.slot // HALF
                    pe.wait_ge(raw_in[h], 32 * t.round + 32)
                    wait(pe, e_relu, g)
                    pe.matmul(p_e[0][:, :], c.we1[:, :], raw[:, h, :], start=True, stop=True).then_inc(e_h1, 1)

                def features2(t):
                    if not t.real:
                        return
                    g, h = t.group, t.slot // HALF
                    pe.wait_ge(e_relu, g + 1)
                    wait(pe, e_ef, g)
                    pe.matmul(p_e[1][:, :], c.we2[:, :], h1[:, h, :], start=True, stop=True).then_inc(e_done, 1)

                if layer == 2:
                    walk(pe, add_up)
                else:
                    def step(t):
                        turn(t)
                        if layer == 3 and t.k % HALF == 2:
                            features(t.back(-2))
                        if layer == 3 and t.k % HALF == 3:
                            features2(t.back(-1))
                        multiply(t.back(2))
                        add_up(t.back(4))
                    if layer == 3:
                        features(Tile(0, 0))
                        features2(Tile(0, 0))
                    walk(pe, step, 4)

            @block.vector
            def _(dve):
                dve.memset(acc[:, :], 0.0).then_inc(prepared, 1)
                dve.memset(msg[:, :, P:P + 1], 1.0).then_inc(prepared, 1)
                dve.memset(msg[:, :, P + 1:AUG], 0.0).then_inc(prepared, 1)
                dve.wait_ge(prepared, PREPARED)

                def make_hot(t):
                    if not t.real:
                        return
                    wait(dve, summed, t.n + 1 - DEEP)
                    j = t.j
                    rank = c.rank[:, t.col()]
                    if layer in (0, 3):
                        dve.tensor_scalar(one_hot[:, j, :], c.ramp[:, :], rank, None, ALU.is_equal).then_inc(hot, 1)
                    else:
                        dve.tensor_scalar(one_hot[:, j, :], c.ramp[:, :], rank, c.src_scale[:, t.col()],
                                          ALU.is_equal, ALU.mult).then_inc(hot, 1)

                def make_message(t):
                    if not t.real:
                        return
                    if layer == 0:
                        dve.wait_ge(product, t.n + 1)
                        wait(dve, summed, t.n + 1 - DEEP)
                        dve.tensor_scalar(msg[:, t.j, 0:P], p_z[t.b], 0.0, c.norm[:, t.col()],
                                          ALU.max, ALU.mult).then_inc(message, 1)
                    if layer == 1:
                        j = t.b
                        dve.wait_ge(picked, t.n + 1)
                        for r in range(2, REL):
                            if r == REL // 2:
                                dve.wait_ge(product, 2 * t.n + 2)
                            if r > 3:
                                dve.wait_ge(v, t.n * (REL - 2) + r - 3)
                            dve.scalar_tensor_tensor(pick[:, r % 2, j, :], p_z[j][:, r, :],
                                                     c.is_rel[:, bass.ds(t.n, 1), r], pick[:, r % 2, j, :],
                                                     ALU.mult, ALU.add).then_inc(v, 1)

                def join(t):
                    if not t.real:
                        return
                    j = t.b
                    dve.wait_ge(v, t.n * (REL - 2) + REL - 2)
                    wait(dve, summed, t.n + 1 - DEEP)
                    dve.tensor_tensor(msg[:, t.j, 0:P], pick[:, 0, j, :], pick[:, 1, j, :], ALU.add)\
                        .then_inc(message, 1)

                def close(t):
                    if not t.real:
                        return
                    j = t.j
                    dve.wait_ge(summed, t.n + 1)
                    wait(dve, stored[t.slot], stored.base[t.slot] + 16 * t.round)
                    wait(dve, added, t.n)
                    dve.tensor_tensor(out[:, t.slot, 0:wide], acc[:, 0:wide], p_sum[t.slot % n_sum][:, 0, :], ALU.add)\
                        .then_inc(closed, 1)

                def go_on(t):
                    if not t.real:
                        return
                    dve.wait_ge(closed, t.n + 1)
                    dve.scalar_tensor_tensor(acc[:, 0:wide], out[:, t.slot, 0:wide], c.goes_on[:, t.col()],
                                             p_sum[t.slot % n_sum][:, 1, :], ALU.mult, ALU.add).then_inc(added, 1)

                def weigh(t):
                    if not t.real:
                        return
                    g, h = t.group, t.slot // HALF
                    dve.wait_ge(e_tw, g + 1)
                    dve.wait_ge(e_done, g + 1)
                    wait(dve, product, t.n - HALF)
                    dve.scalar_tensor_tensor(ef[:, h, :], p_e[1][:, :], c.cols[:, 1:2], tw[:, h, :],
                                             ALU.add, ALU.mult).then_inc(e_ef, 1)

                def step(t):
                    if layer == 1:
                        make_message(t.back(3))
                        close(t.back(5))
                        join(t.back(3))
                        go_on(t.back(5))
                        return
                    lag = 2 if layer == 2 else 5
                    if layer == 0:
                        make_message(t.back(3))
                    close(t.back(lag))
                    make_hot(t.back(2) if layer != 2 else t)
                    if layer == 3 and t.k % HALF == 3:
                        weigh(t.back(-1))
                    go_on(t.back(lag))
                if layer == 3:
                    weigh(Tile(0, 0))
                walk(dve, step, 2 if layer == 2 else 5)
                dve.wait_ge(added, T)
                dve.nop().then_inc(ended, 1)



def node_stage(nc, c, layer, rows_in, rows_out, sums):
    L = f"node{layer}"
    with ExitStack() as ctx:
        def sb(name, shape, dt=FP32):
            return ctx.enter_context(nc.sbuf_tensor(f"{L}_{name}", shape, dt))

        def ps(name, shape):
            return ctx.enter_context(nc.psum_tensor(f"{L}_{name}", shape, FP32))

        wide = AUG if layer in (0, 3) else D
        x = sb("x", [P, WIDE, D])
        sumrows = sb("sumrows", [P, WIDE, AUG])
        place = sb("place", [P, DEEP, P])
        y = sb("y", [P, WIDE, D])
        out = sb("out", [P, WIDE, D])
        stats = sb("stats", [P, WIDE, 6])
        moments = sb("moments", [P, WIDE, 2])
        std = sb("std", [P, WIDE])
        rstd = sb("rstd", [P, WIDE])
        shift = sb("shift", [P, WIDE])
        p_y = [ps(f"p_y{j}", [P, 512])[:, 0:P] for j in range(DEEP)]
        if layer == 0:
            xT = sb("xT", [P, DEEP, P])
            own = sb("own", [P, DEEP, P])
            p_T = [ps(f"p_T{j}", [P, 512])[:, 0:P] for j in range(2)]
            p_h = [ps(f"p_h{j}", [P, 512])[:, 0:P] for j in range(2)]
        if layer == 3:
            sT = sb("sT", [P, DEEP, P])
            deg = sb("deg", [1, DEEP, P])
            p_s = [ps(f"p_s{j}", [P, 2, 256]) for j in range(2)]
        (placed, turned, copied, product, owned, summed, made, halves, measured, rooted, inverted,
         shifted, normed, marked, passed, passed_act, passed_pool, passed_dve) = sems(
            nc, ctx, L, "placed", "turned", "copied", "product", "owned", "summed", "made", "halves", "measured",
            "rooted", "inverted", "shifted", "normed", "marked", "passed", "passed_act", "passed_pool", "passed_dve")
        ROOT_LAG, INVERT_LAG, NORM_LAG, STORE_LAG = UN + 2, UN + 4, WIDE, 2 * WIDE
        act_stores = layer in (1, 2)
        x_in, sums_in, stored = c.x_in, c.sums_in, c.rows_out

        with nc.Block() as block:
            last_used = turned if layer == 3 else summed

            def load_sums(e, signal, t):
                row = row_number(nc, e, c.sum_start[0:1, t.col()], R)
                wait(e, last_used, t.n + 1 - WIDE)
                e.sem_inc(signal, 1)
                e.dma_start(sumrows[:, t.slot, 0:wide], sums[bass.ds(row, P), 0:wide])\
                    .then_inc(sums_in[t.slot], 16)

            def store(e, signal, t):
                if not t.real:
                    return
                e.wait_ge(normed, t.n + HALF)
                e.sem_inc(signal, 1)
                e.dma_start(rows_out[bass.ds(t.n * P, HALF * P), :].rearrange("(k p) d -> p k d", p=P),
                            out[:, t.slot:t.slot + HALF, :]).then_inc(stored[t.slot // HALF], 16)

            def all_stored(e):
                for h in range(WIDE // HALF):
                    e.wait_ge(stored[h], stored.base[h] + 16 * stored.uses[h])

            @block.sync
            def _(sp):
                def step(t):
                    if t.k % HALF == 0 and not act_stores:
                        store(sp, passed, t.back(STORE_LAG))
                    if not t.real:
                        return
                    if t.k % HALF == 0:
                        wait(sp, made, t.n + HALF - WIDE)
                        sp.sem_inc(passed, 1)
                        sp.dma_start(x[:, t.slot:t.slot + HALF, :],
                                     rows_in[bass.ds(t.n * P, HALF * P), 0:D].rearrange("(k p) d -> p k d", p=P))\
                            .then_inc(x_in[t.slot // HALF], 16)
                    if t.k % 2 == 0:
                        load_sums(sp, passed, t)
                walk(sp, step, STORE_LAG, WIDE)
                if not act_stores:
                    all_stored(sp)

            @block.gpsimd
            def _(pool):
                def step(t):
                    if t.k % 2 == 1:
                        load_sums(pool, passed_pool, t)
                walk(pool, step, unroll=WIDE)

            @block.scalar
            def _(act):
                def copy_turned(t):
                    if not t.real:
                        return
                    j = t.j
                    act.wait_ge(turned, t.n + 1)
                    wait(act, product if layer == 0 else summed, t.n + 1 - DEEP)
                    if layer == 0:
                        act.copy(xT[:, j, :], p_T[t.b]).then_inc(copied, 1)
                    else:
                        act.copy(deg[:, j, :], p_s[t.b][0:1, 1, 0:P])
                        act.copy(sT[:, j, :], p_s[t.b][:, 0, 0:P]).then_inc(copied, 1)

                def relu_own(t):
                    if not t.real:
                        return
                    j = t.j
                    act.wait_ge(product, t.n + 1)
                    wait(act, made, t.n + 1 - DEEP)
                    act.activation(own[:, j, :], p_h[t.b], ACT.Relu).then_inc(owned, 1)

                def root(t):
                    if not t.real:
                        return
                    act.wait_ge(measured, t.n + HALF)
                    g = slice(t.slot, t.slot + HALF)
                    act.activation(std[:, g, None], moments[:, g, 1:2], ACT.Sqrt, bias=c.eps[:, 0:1])\
                        .then_inc(rooted, 1)

                def norm(t):
                    if not t.real:
                        return
                    s = t.slot
                    if s % HALF == 0:
                        act.wait_ge(shifted, t.group + 1)
                        h = t.slot // HALF
                        wait(act, stored[h], stored.base[h] + 16 * t.round)
                    act.activation(out[:, t.slot, :], y[:, s, :], ACT.Identity, bias=shift[:, s:s + 1],
                                   scale=rstd[:, s:s + 1]).then_inc(normed, 1)

                def step(t):
                    if t.k % HALF == 2:
                        root(t.back(ROOT_LAG))
                    if layer in (0, 3):
                        copy_turned(t)
                    if layer == 0:
                        relu_own(t.back(2))
                    norm(t.back(NORM_LAG))
                    if act_stores and t.k % HALF == HALF - 1:
                        store(act, passed_act, t.back(NORM_LAG + HALF - 1))
                walk(act, step, NORM_LAG, WIDE)
                if act_stores:
                    all_stored(act)

            @block.tensor
            def _(pe):
                def turn(t):
                    if not t.real:
                        return
                    pe.wait_ge(x_in[t.slot // HALF], x_in.base[t.slot // HALF] + 16 * t.round + 16)
                    wait(pe, copied, t.n - 1)
                    pe.transpose(p_T[t.b], x[:, t.slot, :], c.ident[:, :]).then_inc(turned, 1)

                def own_product(t):
                    if not t.real:
                        return
                    j = t.j
                    pe.wait_ge(copied, t.n + 1)
                    wait(pe, owned, t.n - 1)
                    pe.matmul(p_h[t.b], xT[:, j, :], c.w0[:, :], start=True, stop=False)
                    pe.matmul(p_h[t.b], c.ones3[:, :], c.bias3[:, 0, :], start=False, stop=True)\
                        .then_inc(product, 1)

                def place_sums(t):
                    if not t.real:
                        return
                    j = t.j
                    pe.wait_ge(placed, t.n + 1)
                    wait(pe, made, t.n + 1 - DEEP)
                    if layer == 0:
                        pe.wait_ge(x_in[t.slot // HALF], x_in.base[t.slot // HALF] + 16 * t.round + 16)
                        pe.matmul(p_y[j], place[:, j, :], sumrows[:, t.slot, 0:D], start=True, stop=False)
                        pe.matmul(p_y[j], c.ident[:, :], x[:, t.slot, :], start=False, stop=True)\
                            .then_inc(summed, 1)
                    if layer == 1:
                        pe.matmul(p_y[j], place[:, j, :], sumrows[:, t.slot, 0:D], start=True, stop=False)
                        pe.matmul(p_y[j], c.ones3[:, :], c.bias3[:, 1, :], start=False, stop=True)\
                            .then_inc(summed, 1)
                    if layer == 2:
                        pe.matmul(p_y[j], place[:, j, :], sumrows[:, t.slot, 0:D], start=True, stop=True)\
                            .then_inc(summed, 1)

                def place_turned(t):
                    if not t.real:
                        return
                    j = t.j
                    pe.wait_ge(placed, t.n + 1)
                    wait(pe, copied, t.n - 1)
                    pe.matmul(p_s[t.b][0:1, 1, 0:P], sumrows[:, t.slot, D:D + 1], place[:, j, :], start=True, stop=True)
                    pe.matmul(p_s[t.b][:, 0, 0:P], sumrows[:, t.slot, 0:D], place[:, j, :], start=True, stop=True)\
                        .then_inc(turned, 1)

                def last_product(t):
                    if not t.real:
                        return
                    j = t.j
                    pe.wait_ge(copied, t.n + 1)
                    wait(pe, made, t.n + 1 - DEEP)
                    pe.matmul(p_y[j], sT[:, j, :], c.wn2[:, :], start=True, stop=False)
                    pe.matmul(p_y[j], deg[0:1, j, :], c.bn2[:, :], start=False, stop=True).then_inc(summed, 1)

                def step(t):
                    if layer == 0:
                        turn(t)
                        own_product(t.back(1))
                        place_sums(t.back(1))
                    elif layer == 3:
                        place_turned(t.back(1))
                        last_product(t.back(2))
                    else:
                        place_sums(t.back(1))
                walk(pe, step, 2, WIDE)

            @block.vector
            def _(dve):
                def number(t):
                    if not t.real:
                        return
                    dve.wait_ge(sums_in[t.slot], sums_in.base[t.slot] + 16 * t.round + 16)
                    if layer == 0:
                        dve.tensor_tensor(c.node_of[:, t.col()], sumrows[:, t.slot, D:D + 1],
                                          c.tile_base[:, t.col()], ALU.subtract).then_inc(marked, 1)

                def mark(t):
                    if not t.real:
                        return
                    j = t.j
                    wait(dve, turned if layer == 3 else summed, t.n + 1 - DEEP)
                    if layer == 0:
                        dve.wait_ge(marked, t.n + 1)
                    dve.tensor_scalar(place[:, j, :], c.ramp[:, 0:P], c.node_of[:, t.col()], None, ALU.is_equal)\
                        .then_inc(placed, 1)

                def make(t):
                    if not t.real:
                        return
                    j, s = t.j, t.slot
                    wait(dve, normed, t.n + 1 - WIDE)
                    dve.wait_ge(summed, t.n + 1)
                    if layer == 0:
                        dve.wait_ge(owned, t.n + 1)
                        ins = dve.scalar_tensor_tensor(y[:, t.slot, :], own[:, j, :], c.inv_deg[:, t.col()],
                                                       p_y[j], ALU.mult, ALU.add)
                    if layer != 0:
                        dve.wait_ge(x_in[s // HALF], x_in.base[s // HALF] + 16 * t.round + 16)
                    if layer == 1:
                        ins = dve.tensor_tensor(y[:, t.slot, :], p_y[j], x[:, s, :], ALU.add)
                    if layer == 2:
                        ins = dve.scalar_tensor_tensor(y[:, t.slot, :], p_y[j], c.scale2[:, t.col()],
                                                       x[:, s, :], ALU.mult, ALU.add)
                    if layer == 3:
                        ins = dve.scalar_tensor_tensor(y[:, t.slot, :], x[:, s, :], 2.0, p_y[j],
                                                       ALU.mult, ALU.add)
                    ins.then_inc(made, 1)

                def measure(t):
                    if not t.real:
                        return
                    dve.wait_ge(made, t.n + 1)
                    dve.bn_stats(stats[:, t.slot, :], y[:, t.slot, :]).then_inc(halves, 1)

                def spread_of(t):
                    if not t.real:
                        return
                    dve.wait_ge(halves, t.n + 1)
                    dve.sem_inc(passed_dve, 1)
                    dve.bn_aggr(moments[:, t.slot, :], stats[:, t.slot, :]).then_inc(measured, 1)

                def invert(t):
                    if not t.real:
                        return
                    g = slice(t.slot, t.slot + HALF)
                    dve.wait_ge(rooted, t.group + 1)
                    wait(dve, normed, t.n + HALF - WIDE)
                    dve.reciprocal(rstd[:, g], std[:, g]).then_inc(inverted, 1)

                def shift_of(t):
                    if not t.real:
                        return
                    g = slice(t.slot, t.slot + HALF)
                    dve.wait_ge(inverted, t.group + 1)
                    dve.scalar_tensor_tensor(shift[:, g, None], moments[:, g, 0:1], -1.0, rstd[:, g, None],
                                             ALU.mult, ALU.mult).then_inc(shifted, 1)

                def step(t):
                    number(t)
                    make(t.back(3))
                    mark(t)
                    measure(t.back(4))
                    spread_of(t.back(5))
                    if t.k % HALF == 0:
                        invert(t.back(INVERT_LAG))
                    if t.k % HALF == 1:
                        shift_of(t.back(INVERT_LAG + 1))
                walk(dve, step, INVERT_LAG + 2, WIDE)



INPUTS = ["x_aug", "ints", "floats", "raw64_rows", "src", "dst", "etype", "norm", "weight", "raw7", "raw64",
          "degree_cols", "scale2_cols",
          "L0_gnn_W", "L0_gnn_b", "L0_gnn_We", "L0_gnn_be", "L0_gnn_root_emb", "L1_gnn_weight", "L1_gnn_bias",
          "L3_gnn_We1", "L3_gnn_be1", "L3_gnn_We2", "L3_gnn_be2", "L3_gnn_Wt", "L3_gnn_bt", "L3_gnn_Wn1",
          "L3_gnn_bn1", "L3_gnn_Wn2", "L3_gnn_bn2"]


class Constants:

    def __init__(self, nc, ctx):
        def sb(name, shape, dt=FP32):
            return ctx.enter_context(nc.sbuf_tensor(name, shape, dt))

        self.ident = sb("ident", [P, P])
        self.upper = sb("upper", [P, P])
        self.ramp = sb("ramp", [P, 2 * P])
        self.tile_base = sb("tile_base", [P, T])
        self.ones = sb("ones", [P, P])
        self.zeros = sb("zeros", [P, AUG])
        self.eps = sb("eps", [P, 1])
        self.w0 = sb("w0", [D, D])
        self.we9 = sb("we9", [K9, D])
        self.ones3 = sb("ones3", [3, P], BF16)
        self.bias3 = sb("bias3", [3, 3, D], BF16)
        self.w1 = sb("w1", [D, REL, D])
        self.we1 = sb("we1", [ER, D])
        self.we2 = sb("we2", [D, D])
        self.wn1a = sb("wn1a", [D, D])
        self.wn1b = sb("wn1b", [D, D])
        self.wn2 = sb("wn2", [D, D])
        self.bn2 = sb("bn2", [1, D])
        self.cols = sb("cols", [P, 4])
        self.inv_deg = sb("inv_deg", [P, T])
        self.scale2 = sb("scale2", [P, T])
        self.src = sb("src_cols", [P, T], I32)
        self.norm = sb("norm_cols", [P, T])
        self.is_rel = sb("is_rel", [P, T, REL])
        self.rank = sb("rank_cols", [P, T])
        self.minus_rank = sb("minus_rank", [P, T])
        self.inv = sb("inv_cols", [P, T])
        self.minus_inv = sb("minus_inv", [P, T])
        self.first_dst = sb("first_dst", [P, T])
        self.src_scale = sb("src_scale", [P, T])
        self.goes_on = sb("goes_on", [P, T])
        self.node_of = sb("node_of", [P, T])
        self.got = Ring(nc, "got", UN, T)
        self.closed_out = Ring(nc, "closed_out", UN, T)
        self.x_in = Ring(nc, "x_in", WIDE // HALF, T // HALF)
        self.sums_in = Ring(nc, "sums_in", WIDE, T)
        self.rows_out = Ring(nc, "rows_out", WIDE // HALF, T // HALF)
        self.falls = sb("falls_found", [1, 1], I32)
        self.sum_row = sb("sum_row", [1, T + 2], I32)
        self.sum_start = sb("sum_start", [1, T], I32)


def program(nc, A, out):
    with ExitStack() as ctx:
        c = Constants(nc, ctx)
        sums = nc.dram_tensor("sums", [DUMP + R + P, AUG], FP32).ap()
        rows = [nc.dram_tensor(f"rows{j}", [R, D], FP32).ap() for j in range(3)]
        S = {name: nc.dram_tensor(f"by_dst_{name}", A[name].shape, A[name].dtype).ap()
             for name in LISTS + ("raw7", "raw64")}
        c.raw64_ready = nc.alloc_semaphore("raw64_ready")
        constants_stage(nc, c, A)
        order_stage(nc, c, A, S)
        index_stage(nc, c, S, A["raw64"])
        x = A["x_aug"]
        for layer in range(4):
            y = rows[layer] if layer < 3 else out
            edge_stage(nc, c, layer, S, x, AUG if layer == 0 else D, sums)
            node_stage(nc, c, layer, x, y, sums)
            for ring in (c.got, c.closed_out, c.x_in, c.sums_in, c.rows_out):
                ring.next_layer()
            x = y


def laid_out(inputs):
    import numpy as np

    def pad(a, rows, value=0):
        a = np.asarray(a)
        return np.concatenate([a, np.full((rows - a.shape[0],) + a.shape[1:], value, a.dtype)])

    def cols(a):
        return np.ascontiguousarray(a.reshape(T, P).T)

    A = {k: np.ascontiguousarray(inputs[k]) for k in INPUTS if k in inputs}
    nv = pad(np.asarray(inputs["node_vec1"]).reshape(-1), R, 1)
    x = pad(inputs["x"], R)
    A["x_aug"] = np.concatenate([x, nv[:, None], np.zeros((R, AUG - D - 1), x.dtype)], axis=1)
    A["src"] = pad(inputs["src"], R)
    dst = pad(inputs["dst"], R, R - 1)
    A["dst"] = np.concatenate([np.full(1, -1, dst.dtype), dst, np.full(1, R, dst.dtype)])
    A["etype"] = pad(inputs["edge_type_8"], R)
    A["norm"] = pad(np.asarray(inputs["edge_weight1"]).reshape(-1), R)
    A["weight"] = pad(inputs["edge_weight"], R)
    e7 = pad(inputs["edge_attr_7"], R)
    A["raw7"] = np.concatenate([e7.T, np.ones((2, R), e7.dtype)])
    A["raw64"] = np.ascontiguousarray(pad(inputs["edge_attr_64"], R).T)
    A["ints"] = np.stack([dst, A["src"], A["etype"]], axis=1)
    A["floats"] = np.concatenate([A["norm"][:, None], A["weight"][:, None], e7], axis=1)
    A["raw64_rows"] = pad(inputs["edge_attr_64"], R)
    A["degree_cols"] = cols(nv)
    A["scale2_cols"] = cols(pad(np.asarray(inputs["node_vec1_n2"]).reshape(-1), R, 1))
    return {k: A[k] for k in INPUTS}


def kernel(**inputs):
    import numpy as np
    import concourse.bacc as bacc
    from concourse.bass_utils import run_bass_kernel_spmd

    nc = bacc.Bacc("TRN2", target_bir_lowering=False, num_devices=1)
    arrays = {f"in_{k}": v for k, v in laid_out(inputs).items()}
    A = {k[3:]: nc.dram_tensor(k, v.shape, mybir.dt.from_np(v.dtype), kind="ExternalInput").ap()
         for k, v in arrays.items()}
    out = nc.dram_tensor("out_rows", (R, D), FP32, kind="ExternalOutput").ap()
    program(nc, A, out)
    r = run_bass_kernel_spmd(nc, [arrays], core_ids=[0])
    return r.results[0]["out_rows"][:N]
```
